# Optimizing a Trainium2 kernel written in Bass

```python
import numpy as np
import jax
import jax.numpy as jnp

def _softmax(x, axis=-1):
    return jax.nn.softmax(x, axis=axis)

def _gelu(x):
    return jax.nn.gelu(x, approximate=True)

def _silu(x):
    return jax.nn.silu(x)

def _sigmoid(x):
    return jax.nn.sigmoid(x)

def _layernorm(x, axis=-1, eps=1e-05):
    m = jnp.mean(x, axis=axis, keepdims=True)
    v = jnp.var(x, axis=axis, keepdims=True)
    return (x - m) / jnp.sqrt(v + eps)

def _scatter_add(tgt, idx, src, axis=0):
    return tgt.at[idx].add(src)

def _segment_sum(src, seg, n):
    return jax.ops.segment_sum(src, seg, n)
kernel_name = 'mk_flamingo_gated_d2_seqx_r8_5b5477'

def setup_inputs(seed: int=0):
    np.random.seed(seed)
    _w = jnp.asarray

    def _rec_inputs():
        import jax
        import jax.numpy as jnp
        _rk = jax.random.key(seed)
        x = 7.22e-05 + 1 * jax.random.normal(jax.random.fold_in(_rk, 1), (32, 128, 128), jnp.float32)
        _lenS = 128 - jax.random.randint(jax.random.fold_in(_rk, 7), (32,), 0, max(1, 128 // 4) + 1, jnp.int32)
        _lenS2 = 128 - jax.random.randint(jax.random.fold_in(_rk, 8), (32,), 0, max(1, 128 // 4) + 1, jnp.int32)
        _ctx_1024P = jax.random.normal(jax.random.fold_in(_rk, 11), (32, 16, 128), jnp.float32)
        _ctx_1024c = jax.random.dirichlet(jax.random.fold_in(_rk, 511), 0.3 * jnp.ones((16,), jnp.float32), (32, 128))
        _ctx_1024t = jnp.einsum('bsk,bkd->bsd', _ctx_1024c, _ctx_1024P)
        _ctx_1024t = _ctx_1024t * jax.lax.rsqrt(jnp.mean(jnp.square(_ctx_1024t)) + 1e-12) * 0.953939
        ctx_1024 = 4.13588e-05 + 0.999923 * (_ctx_1024t + 0.3 * jax.random.normal(jax.random.fold_in(_rk, 611), (32, 128, 128), jnp.float32))
        _validS = jnp.arange(128)[None, :] < _lenS[:, None]
        _validS2 = jnp.arange(128)[None, :] < _lenS2[:, None]
        _causal = jnp.tril(jnp.ones((128, 128), dtype=bool))
        mask_Bx1xSxS2_ik1 = jnp.where(jnp.broadcast_to(_validS2[:, None, None, :], (32, 1, 128, 128)), 1, 0).astype(jnp.int32)
        _g = jax.random.normal(jax.random.fold_in(_rk, 9001), (2, 2), jnp.float32)
        _g = jnp.sign(_g) * jnp.maximum(jnp.abs(_g), 1.0) + (_g == 0) * 1.0
        g_xattn = _g[0]
        g_ffn = _g[1]
        return (x, ctx_1024, mask_Bx1xSxS2_ik1, g_xattn, g_ffn)
    x, ctx_1024, mask_Bx1xSxS2_ik1, g_xattn, g_ffn = _rec_inputs()

    def _L0_xattn_setup():
        import jax, jax.numpy as jnp
        import numpy as np
        D_MODEL = 128
        N_HEADS = 16
        D_K = D_MODEL // N_HEADS
        NEG = -1000000000.0
        key = jax.random.key(seed)
        k1, k2, k3, k4 = jax.random.split(key, 4)
        B, S = (4, 256)
        query = jax.random.normal(k1, (B, S, D_MODEL), dtype=jnp.float32)
        key_t = jax.random.normal(k2, (B, S, D_MODEL), dtype=jnp.float32)
        value = jax.random.normal(k3, (B, S, D_MODEL), dtype=jnp.float32)
        mask = jax.random.randint(k4, (B, 1, S, S), 0, 2, dtype=jnp.int32)
        return {'query': query, 'key': key_t, 'value': value, 'mask': mask}
    _L0_xattn_all = _L0_xattn_setup()
    _L0_xattn_in = {k: v for k, v in _L0_xattn_all.items() if k in ()}
    del _L0_xattn_all

    def _L0_ffn_setup():
        import jax, jax.numpy as jnp
        import numpy as np
        D_MODEL, D_FF, N_EXPERTS, TOP_K = (128, 512, 8, 2)
        key = jax.random.key(seed)
        k0, k1, k2, k3 = jax.random.split(key, 4)
        x = jax.random.normal(k0, (2, 256, D_MODEL), dtype=jnp.float32)
        Wg = jax.random.normal(k1, (D_MODEL, N_EXPERTS), dtype=jnp.float32) * 0.02
        W1 = jax.random.normal(k2, (N_EXPERTS, D_MODEL, D_FF), dtype=jnp.float32) * 0.02
        b1 = jnp.zeros((N_EXPERTS, D_FF), dtype=jnp.float32)
        W2 = jax.random.normal(k3, (N_EXPERTS, D_FF, D_MODEL), dtype=jnp.float32) * 0.02
        b2 = jnp.zeros((N_EXPERTS, D_MODEL), dtype=jnp.float32)
        return {'x': x, 'Wg': Wg, 'W1': W1, 'b1': b1, 'W2': W2, 'b2': b2}
    _L0_ffn_all = _L0_ffn_setup()
    _L0_ffn_in = {k: v for k, v in _L0_ffn_all.items() if k in ('Wg', 'W1', 'b1', 'W2', 'b2')}
    del _L0_ffn_all

    def _L1_xattn_setup():
        import jax, jax.numpy as jnp
        import numpy as np
        B, S, D, NH = (2, 256, 128, 8)
        DH = D // NH
        EPS = 1e-06
        LN_EPS = 1e-05

        def _mlstm_cell(q, k, v, igate_w, igate_b, fgate_w, fgate_b, ln_scale):
            Slen = q.shape[0]
            ifg = jnp.concatenate([q, k, v], axis=-1)
            ig = (ifg @ igate_w.T + igate_b).T
            fg = (ifg @ fgate_w.T + fgate_b).T
            qh = q.reshape(Slen, NH, DH).transpose(1, 0, 2)
            kh = k.reshape(Slen, NH, DH).transpose(1, 0, 2)
            vh = v.reshape(Slen, NH, DH).transpose(1, 0, 2)
            log_f = jax.nn.log_sigmoid(fg)
            cs = jnp.cumsum(log_f, axis=1)
            fg_mat = cs[:, :, None] - cs[:, None, :]
            mask = jnp.tril(jnp.ones((Slen, Slen), dtype=bool))
            log_fg_mat = jnp.where(mask, fg_mat, -jnp.inf)
            log_D = log_fg_mat + ig[:, None, :]
            max_log_D = jnp.max(log_D, axis=-1, keepdims=True)
            D_mat = jnp.exp(log_D - max_log_D)
            qk = jnp.einsum('hsd,htd->hst', qh, kh) / np.sqrt(DH)
            C = qk * D_mat
            normalizer = jnp.maximum(jnp.abs(C.sum(axis=-1, keepdims=True)), jnp.exp(-max_log_D))
            h = jnp.einsum('hst,htd->hsd', C / (normalizer + EPS), vh)
            h = h.transpose(1, 0, 2).reshape(Slen, D)
            mu = h.mean(axis=-1, keepdims=True)
            var = h.var(axis=-1, keepdims=True)
            return (h - mu) / jnp.sqrt(var + LN_EPS) * ln_scale
        key = jax.random.key(seed)
        ks = jax.random.split(key, 8)
        rnd = lambda k, sh, s=1.0: jax.random.normal(k, sh, dtype=jnp.float32) * s
        return {'q': rnd(ks[0], (B, S, D)), 'k': rnd(ks[1], (B, S, D)), 'v': rnd(ks[2], (B, S, D)), 'igate_w': rnd(ks[3], (NH, 3 * D), 0.02), 'igate_b': jnp.linspace(3.0, 6.0, NH, dtype=jnp.float32), 'fgate_w': rnd(ks[4], (NH, 3 * D), 0.02), 'fgate_b': rnd(ks[5], (NH,), 0.3162278), 'ln_scale': jnp.ones((D,), dtype=jnp.float32)}
    _L1_xattn_all = _L1_xattn_setup()
    _L1_xattn_in = {k: v for k, v in _L1_xattn_all.items() if k in ('igate_w', 'igate_b', 'fgate_w', 'fgate_b', 'ln_scale')}
    del _L1_xattn_all

    def _L1_ffn_setup():
        import jax, jax.numpy as jnp
        import numpy as np
        D_MODEL = 128
        D_HIDDEN = 512
        NUM_EXPERT = 8
        TOP_K = 2
        B, N = (1, 1024)

        def _expert_mlp(x, W1, b1, W2, b2, W3, b3):
            h = jax.nn.gelu(jnp.einsum('bnd,dh->bnh', x, W1) + b1, approximate=False)
            h = jax.nn.gelu(jnp.einsum('bnh,hk->bnk', h, W2) + b2, approximate=False)
            return jnp.einsum('bnh,hd->bnd', h, W3) + b3
        key = jax.random.key(seed)
        ks = jax.random.split(key, 8)
        s1 = 1.0 / np.sqrt(D_MODEL)
        s2 = 1.0 / np.sqrt(D_HIDDEN)
        return {'x': jax.random.normal(ks[0], (B, N, D_MODEL), jnp.float32), 'expert_tokens': jax.random.normal(ks[1], (NUM_EXPERT, D_MODEL), jnp.float32), 'W1': jax.random.normal(ks[2], (NUM_EXPERT, D_MODEL, D_HIDDEN), jnp.float32) * s1, 'b1': jnp.zeros((NUM_EXPERT, D_HIDDEN), jnp.float32), 'W2': jax.random.normal(ks[3], (NUM_EXPERT, D_HIDDEN, D_HIDDEN), jnp.float32) * s2, 'b2': jnp.zeros((NUM_EXPERT, D_HIDDEN), jnp.float32), 'W3': jax.random.normal(ks[4], (NUM_EXPERT, D_HIDDEN, D_MODEL), jnp.float32) * s2, 'b3': jnp.zeros((NUM_EXPERT, D_MODEL), jnp.float32)}
    _L1_ffn_all = _L1_ffn_setup()
    _L1_ffn_in = {k: v for k, v in _L1_ffn_all.items() if k in ('expert_tokens', 'W1', 'b1', 'W2', 'b2', 'W3', 'b3')}
    del _L1_ffn_all
    return {'x': x, 'ctx_1024': ctx_1024, 'mask_Bx1xSxS2_ik1': mask_Bx1xSxS2_ik1, 'g_xattn': g_xattn, 'g_ffn': g_ffn, 'L0_ffn_Wg': _L0_ffn_in['Wg'], 'L0_ffn_W1': _L0_ffn_in['W1'], 'L0_ffn_b1': _L0_ffn_in['b1'], 'L0_ffn_W2': _L0_ffn_in['W2'], 'L0_ffn_b2': _L0_ffn_in['b2'], 'L1_xattn_igate_w': _L1_xattn_in['igate_w'], 'L1_xattn_igate_b': _L1_xattn_in['igate_b'], 'L1_xattn_fgate_w': _L1_xattn_in['fgate_w'], 'L1_xattn_fgate_b': _L1_xattn_in['fgate_b'], 'L1_xattn_ln_scale': _L1_xattn_in['ln_scale'], 'L1_ffn_expert_tokens': _L1_ffn_in['expert_tokens'], 'L1_ffn_W1': _L1_ffn_in['W1'], 'L1_ffn_b1': _L1_ffn_in['b1'], 'L1_ffn_W2': _L1_ffn_in['W2'], 'L1_ffn_b2': _L1_ffn_in['b2'], 'L1_ffn_W3': _L1_ffn_in['W3'], 'L1_ffn_b3': _L1_ffn_in['b3']}

def reference(x, ctx_1024, mask_Bx1xSxS2_ik1, g_xattn, g_ffn, L0_ffn_Wg, L0_ffn_W1, L0_ffn_b1, L0_ffn_W2, L0_ffn_b2, L1_xattn_igate_w, L1_xattn_igate_b, L1_xattn_fgate_w, L1_xattn_fgate_b, L1_xattn_ln_scale, L1_ffn_expert_tokens, L1_ffn_W1, L1_ffn_b1, L1_ffn_W2, L1_ffn_b2, L1_ffn_W3, L1_ffn_b3):
    import jax
    import jax.numpy as jnp

    def _L0_xattn_ref(query, key, value, mask):
        import jax, jax.numpy as jnp
        import numpy as np
        D_MODEL = 128
        N_HEADS = 16
        D_K = D_MODEL // N_HEADS
        NEG = -1000000000.0
        B, S, _ = query.shape
        q = query.reshape(B, S, N_HEADS, D_K).transpose(0, 2, 1, 3)
        k = key.reshape(B, S, N_HEADS, D_K).transpose(0, 2, 1, 3)
        v = value.reshape(B, S, N_HEADS, D_K).transpose(0, 2, 1, 3)
        scale = jnp.asarray(np.sqrt(D_K), dtype=q.dtype)
        scores = jnp.einsum('bhqd,bhkd->bhqk', q, k) / scale
        scores = jnp.where(mask == 0, jnp.asarray(NEG, scores.dtype), scores)
        attn = jax.nn.softmax(scores, axis=-1)
        out = jnp.einsum('bhqk,bhkd->bhqd', attn, v)
        return out.transpose(0, 2, 1, 3).reshape(B, S, D_MODEL)

    def _L0_ffn_ref(x, Wg, W1, b1, W2, b2):
        import jax, jax.numpy as jnp
        import numpy as np
        D_MODEL, D_FF, N_EXPERTS, TOP_K = (128, 512, 8, 2)
        B = x.shape[:-1]
        xs = x.reshape(-1, x.shape[-1])
        T = xs.shape[0]
        gate_logits = xs @ Wg
        weights, sel = jax.lax.top_k(gate_logits, TOP_K)
        weights = jax.nn.softmax(weights.astype(jnp.float32), axis=1).astype(x.dtype)
        h = jax.nn.relu(jnp.einsum('td,edf->etf', xs, W1) + b1[:, None, :])
        out_e = jnp.einsum('etf,efd->etd', h, W2) + b2[:, None, :]
        tok = jnp.arange(T)
        picked = out_e[sel, tok[:, None]]
        out = jnp.einsum('tk,tkd->td', weights, picked)
        return out.reshape(*B, x.shape[-1])

    def _L1_xattn_ref(q, k, v, igate_w, igate_b, fgate_w, fgate_b, ln_scale):
        import jax, jax.numpy as jnp
        import numpy as np
        B, S, D, NH = (2, 256, 128, 8)
        DH = D // NH
        EPS = 1e-06
        LN_EPS = 1e-05

        def _mlstm_cell(q, k, v, igate_w, igate_b, fgate_w, fgate_b, ln_scale):
            Slen = q.shape[0]
            ifg = jnp.concatenate([q, k, v], axis=-1)
            ig = (ifg @ igate_w.T + igate_b).T
            fg = (ifg @ fgate_w.T + fgate_b).T
            qh = q.reshape(Slen, NH, DH).transpose(1, 0, 2)
            kh = k.reshape(Slen, NH, DH).transpose(1, 0, 2)
            vh = v.reshape(Slen, NH, DH).transpose(1, 0, 2)
            log_f = jax.nn.log_sigmoid(fg)
            cs = jnp.cumsum(log_f, axis=1)
            fg_mat = cs[:, :, None] - cs[:, None, :]
            mask = jnp.tril(jnp.ones((Slen, Slen), dtype=bool))
            log_fg_mat = jnp.where(mask, fg_mat, -jnp.inf)
            log_D = log_fg_mat + ig[:, None, :]
            max_log_D = jnp.max(log_D, axis=-1, keepdims=True)
            D_mat = jnp.exp(log_D - max_log_D)
            qk = jnp.einsum('hsd,htd->hst', qh, kh) / np.sqrt(DH)
            C = qk * D_mat
            normalizer = jnp.maximum(jnp.abs(C.sum(axis=-1, keepdims=True)), jnp.exp(-max_log_D))
            h = jnp.einsum('hst,htd->hsd', C / (normalizer + EPS), vh)
            h = h.transpose(1, 0, 2).reshape(Slen, D)
            mu = h.mean(axis=-1, keepdims=True)
            var = h.var(axis=-1, keepdims=True)
            return (h - mu) / jnp.sqrt(var + LN_EPS) * ln_scale
        return jax.vmap(lambda qq, kk, vv: _mlstm_cell(qq, kk, vv, igate_w, igate_b, fgate_w, fgate_b, ln_scale))(q, k, v)

    def _L1_ffn_ref(x, expert_tokens, W1, b1, W2, b2, W3, b3):
        import jax, jax.numpy as jnp
        import numpy as np
        D_MODEL = 128
        D_HIDDEN = 512
        NUM_EXPERT = 8
        TOP_K = 2
        B, N = (1, 1024)

        def _expert_mlp(x, W1, b1, W2, b2, W3, b3):
            h = jax.nn.gelu(jnp.einsum('bnd,dh->bnh', x, W1) + b1, approximate=False)
            h = jax.nn.gelu(jnp.einsum('bnh,hk->bnk', h, W2) + b2, approximate=False)
            return jnp.einsum('bnh,hd->bnd', h, W3) + b3
        scores = jnp.einsum('bnd,ed->bne', x, expert_tokens)
        _, topk_idx = jax.lax.top_k(scores, TOP_K)
        outputs = jnp.zeros_like(x)
        num_expert = W1.shape[0]
        for i in range(num_expert):
            w = jnp.mean((topk_idx == i).astype(x.dtype), axis=-1, keepdims=True)
            y = _expert_mlp(x, W1[i], b1[i], W2[i], b2[i], W3[i], b3[i])
            outputs = outputs + y * w
        return outputs
    x = x + jnp.tanh(g_xattn[0]) * _L0_xattn_ref(_layernorm(x, axis=-1), ctx_1024, ctx_1024, mask_Bx1xSxS2_ik1)
    x = x + jnp.tanh(g_ffn[0]) * _L0_ffn_ref(_layernorm(x, axis=-1), L0_ffn_Wg, L0_ffn_W1, L0_ffn_b1, L0_ffn_W2, L0_ffn_b2)
    x = x + jnp.tanh(g_xattn[1]) * _L1_xattn_ref(_layernorm(x, axis=-1), ctx_1024, ctx_1024, L1_xattn_igate_w, L1_xattn_igate_b, L1_xattn_fgate_w, L1_xattn_fgate_b, L1_xattn_ln_scale)
    x = x + jnp.tanh(g_ffn[1]) * _L1_ffn_ref(_layernorm(x, axis=-1), L1_ffn_expert_tokens, L1_ffn_W1, L1_ffn_b1, L1_ffn_W2, L1_ffn_b2, L1_ffn_W3, L1_ffn_b3)
    return x

_drawn_inputs = setup_inputs


def setup_inputs(seed=0):
    import zlib

    import numpy as np

    out = dict(_drawn_inputs(seed))
    spreads = {'g_ffn': (-1.0, 0.6),
     'L0_ffn_b1': (0.0, 0.1),
     'L0_ffn_b2': (0.0, 0.1),
     'L1_xattn_ln_scale': (1.0, 0.2),
     'L1_ffn_b1': (0.0, 0.417),
     'L1_ffn_b2': (0.0, 0.288),
     'L1_ffn_b3': (0.0, 0.1)}
    factors = {}
    for name, (base, spread) in spreads.items():
        noise = np.random.default_rng([zlib.crc32(name.encode()), seed]).standard_normal(out[name].shape)
        drawn = base * np.exp(spread * noise) if base else spread * noise
        out[name] = jnp.asarray(drawn.astype(out[name].dtype))
    for name, factor in factors.items():
        out[name] = (out[name] * factor).astype(out[name].dtype)
    return out
```

```python
import concourse.bass as bass
from concourse import mybir
from contextlib import ExitStack

F32 = mybir.dt.float32
F32R = mybir.dt.float32r
BF16 = mybir.dt.bfloat16
I32 = mybir.dt.int32
U32 = mybir.dt.uint32
ALU = mybir.AluOpType
ACT = mybir.ActivationFunctionType
AX = mybir.AxisListType

P = 128
B = 32
E = 8
F = 512
FC = F // P
NH0, DH0 = 16, 8
NH1, DH1 = 8, 16
TOPK = 2
NT = TOPK * B + E
LN_EPS = 1e-5
NORM_EPS = 1e-6
BIG = 1e9

CF_ID, CF_UPI, CF_IOTA, CF_P, CF_SELM, CF_E, CF_THR, CF_J, CF_W = 0, 128, 256, 384, 385, 897, 1153, 1409, 1481
CB_ID, CB_UPS, CB_ONE, CB_TRI, CB_SEL, CB_T, CB_W = 0, 128, 256, 384, 512, 544, 608
BO = [0, E * F, E * F + E * P, 2 * E * F + E * P, 3 * E * F + E * P]
BN = 3 * E * F + 2 * E * P
BN1 = BN - BO[2]


def constants():
    import numpy as np
    p = np.arange(P)
    cf = np.zeros((P, CF_W), np.float32)
    cf[:, CF_ID:CF_ID + P] = np.eye(P)
    cf[:, CF_UPI:CF_UPI + P] = p[:, None] <= p[None, :]
    cf[:, CF_IOTA:CF_IOTA + P] = p
    cf[:, CF_P] = p
    for t in range(4):
        cf[(p % 32 == t) | (p % 32 == 4 + t), CF_SELM + t * P:CF_SELM + (t + 1) * P] = -1
    cf[:, CF_E:CF_E + E * B] = np.repeat(np.arange(E), B)
    cf[:, CF_THR:CF_THR + E * B] = np.tile(np.arange(B) * P, E)
    cf[:, CF_J:CF_J + NT] = np.arange(NT)
    cb = np.zeros((P, CB_W), np.float32)
    cb[:, CB_ID:CB_ID + P] = np.eye(P)
    cb[:, CB_UPS:CB_UPS + P] = p[:, None] < p[None, :]
    cb[:, CB_ONE:CB_ONE + P] = 1
    cb[:, CB_TRI:CB_TRI + P] = np.where(p[:, None] <= p[None, :], 0, -1e30)
    cb[:, CB_SEL:CB_SEL + 32] = (p[:, None] % 32 == np.arange(32)) & (p[:, None] < 96)
    cb[:, CB_T:CB_T + TOPK * B] = np.repeat(np.arange(B), TOPK)
    return cf, cb


def wait(eng, sem, value):
    if not isinstance(value, int) or value > 0:
        eng.wait_ge(sem, value)


def wait_apart(eng, sem, value, fence):
    if not isinstance(value, int) or value > 0:
        eng.wait_ge(sem, value)
        fence(eng)


class Chain:

    def __init__(self, eng, sem, i, per):
        self.eng, self.sem, self.base, self.per, self.n = eng, sem, i * (per or 0), per, 0

    def __call__(self, ins, fence=None):
        self.n += 1
        ins.then_inc(self.sem, 1)
        if fence is None:
            self.eng.wait_ge(self.sem, self.base + self.n)
        else:
            wait_apart(self.eng, self.sem, self.base + self.n, fence)

    def end(self):
        assert self.per in (None, self.n), (self.n, self.per)


def skewed(eng, n, stages, unroll=2):
    leads = [lead for lead, _ in stages]

    def step(j):
        for lead, stage in stages:
            if 0 <= j + lead < n:
                stage(j + lead, (j + lead) % 2, (j + lead) // 2)

    first = 2 + max(0, -min(leads))
    first += -first % unroll
    last = n - max(0, max(leads))
    last -= (last - first) % unroll
    for j in range(-max(leads), first):
        step(j)
    with eng.Fori(first // unroll, last // unroll) as jj:
        for k in range(unroll):
            for lead, stage in stages:
                at = k + lead
                stage(unroll * jj + at, at % 2, (unroll // 2) * jj + at // 2)
    for j in range(last, n - min(leads)):
        step(j)


def build(nc, cf_d, cb_d, x_d, ctx_d, mask_d, gx_d, gf_d, wg0_d, w01_d, b01_d, w02_d, b02_d, igw_d,
          igb_d, fgw_d, fgb_d, lns_d, tok_d, w11_d, b11_d, w12_d, b12_d, w13_d, b13_d, out_d):
    def dram(name, shape, dt=F32):
        return nc.dram_tensor(name, shape, dt).ap()

    bparts_d = dram("bias_parts", (3, BN), BF16)
    xn_d = [dram("normed0", (B * P, P)), dram("normed1", (B * P, P))]
    ys_d = [dram("sorted0", (NT * P, P)), dram("sorted1", (NT * P, P))]

    keep = ExitStack()

    def sb(stack, name, shape, dt=F32):
        return stack.enter_context(nc.sbuf_tensor(name, shape, dt))

    def ps(stack, name, shape=(P, 512), dt=F32):
        return stack.enter_context(nc.psum_tensor(name, list(shape), dt))

    def sem(stack, name):
        return stack.enter_context(nc.semaphore(name))

    cf = sb(keep, "cf", [P, CF_W])
    cb = sb(keep, "cb", [P, CB_W], BF16)
    xs = sb(keep, "xs", [P, B, P])
    cx = sb(keep, "cx", [P, B, P])
    wts = sb(keep, "wts", [P, 2 * E * F + E * FC * F])
    brow = sb(keep, "brow", [P, BN1], BF16)
    selm = sb(keep, "selm", [P, 4, P], F32R)
    gts = sb(keep, "gts", [P, 4])
    half = sb(keep, "half", [P, 1])
    wr = [sb(keep, "wr0", [P, E]), sb(keep, "wr1", [P, E])]
    wgate = sb(keep, "wgate", [P, 3, 2 * NH1])
    gbias = sb(keep, "gbias", [P, 2, NH1])
    lnsc = sb(keep, "lnsc", [P, P])
    topv = sb(keep, "topv", [P, B, 2])
    topi = sb(keep, "topi", [P, B, 2])
    wt = sb(keep, "wt", [P, B, 2])
    slot = sb(keep, "slot", [P, B, 2], I32)
    src = sb(keep, "src", [P, NT], I32)
    texp = sb(keep, "texp", [P, NT], I32)

    junk = [sb(keep, "junk_v", [P, 32]), sb(keep, "junk_g", [P, 32])]
    fences = [0, 0]

    def vfence(v):
        fences[0] = (fences[0] + 1) % 32
        v.memset(junk[0][:, fences[0]:fences[0] + 1], 0.0)

    def gfence(g):
        fences[1] = (fences[1] + 1) % 32
        g.tensor_tensor(junk[1][:, fences[1]:fences[1] + 1], half[:], half[:], ALU.mult)

    ident = cf[:, CF_ID:CF_ID + P]
    identb = cb[:, CB_ID:CB_ID + P]
    identb4 = identb.unsqueeze(1).broadcast_to([P, 4, P])
    w01 = wts[:, 0:E * F].rearrange("p (e f) -> p e f", e=E)
    w02 = wts[:, E * F:2 * E * F].rearrange("p (e c d) -> p e c d", e=E, c=FC)
    w12 = wts[:, 2 * E * F:].rearrange("p (e c f) -> p e c f", e=E, c=FC)

    biases = [(b01_d, 0), (b02_d, BO[1]), (b11_d, BO[2]), (b12_d, BO[3]), (b13_d, BO[4])]
    with ExitStack() as st:
        cbf = sb(st, "cbf", [P, CB_W])
        braw = sb(st, "braw", [P, BN // P])
        bmid = sb(st, "bmid", [P, BN // P])
        bpart = sb(st, "bpart", [P, 3, BN // P], BF16)
        s_c, s_small, s_b, s_bp, s_br = [sem(st, n) for n in ("const_in", "small_in", "bias_in", "bias_out", "bias_rows")]
        s_ch, s_z, s_p, s_t, s_w = [sem(st, n) for n in ("dve_step", "rows_zero", "parts_ready", "tanh_done", "weights_in")]
        with nc.Block() as block:
            @block.sync
            def _(sp):
                sp.dma_start(cf[:], cf_d).then_inc(s_c, 16)
                sp.dma_start(cbf[:], cb_d).then_inc(s_c, 16)
                for bd, at in biases:
                    n = bd.shape[0] * bd.shape[1] // P
                    sp.dma_start(braw[:, at // P:at // P + n],
                                 bd.rearrange("e f -> (e f)").rearrange("(p c) -> p c", p=P)).then_inc(s_b, 16)
                for to, row in ((gts[:, 0:2], gx_d), (gts[:, 2:4], gf_d), (gbias[:, 0, :], igb_d),
                                (gbias[:, 1, :], fgb_d), (lnsc[:], lns_d)):
                    sp.dma_start(to, row.rearrange("(a n) -> a n", a=1).broadcast_to([P, row.shape[0]])).then_inc(s_small, 16)
                sp.dma_start(wr[0][:], wg0_d).then_inc(s_small, 16)
                sp.dma_start(w01, w01_d.rearrange("e d f -> d e f")).then_inc(s_w, 16)
                for e in range(E):
                    sp.dma_start(w02[:, e], w02_d[e].rearrange("(c p) d -> p c d", p=P)).then_inc(s_w, 16)
                    sp.dma_start(w12[:, e], w12_d[e].rearrange("(c p) f -> p c f", p=P)).then_inc(s_w, 16)
                sp.wait_ge(s_p, 1)
                for bd, at in biases:
                    n = bd.shape[0] * bd.shape[1]
                    sp.dma_start(bparts_d[:, at:at + n].rearrange("t (p c) -> p t c", p=P),
                                 bpart[:, :, at // P:(at + n) // P]).then_inc(s_bp, 16)
                sp.wait_ge(s_bp, 16 * len(biases))
                sp.wait_ge(s_z, 1)
                sp.dma_start(brow[0:3, 0:BO[2]], bparts_d[:, 0:BO[2]]).then_inc(s_br, 16)
                sp.wait_ge(s_br, 16)
                sp.wait_ge(s_w, 16 * (1 + 2 * E))

            @block.scalar
            def _(act):
                with nc.allow_non_contiguous_dma(reason="small weights, transposed on the way in"):
                    act.dma_start(wr[1][:], tok_d.rearrange("e d -> d e")).then_inc(s_small, 16)
                    for r in range(3):
                        act.dma_start(wgate[:, r, 0:NH1], igw_d[:, r * P:(r + 1) * P].rearrange("h d -> d h")).then_inc(s_small, 16)
                        act.dma_start(wgate[:, r, NH1:], fgw_d[:, r * P:(r + 1) * P].rearrange("h d -> d h")).then_inc(s_small, 16)
                act.wait_ge(s_small, 13 * 16)
                nc.scalar.activation(gts[:], gts[:], ACT.Tanh).then_inc(s_t, 1)

            @block.gpsimd
            def _(g):
                g.memset(half[:], -0.5)
                g.memset(brow[:], 0.0).then_inc(s_z, 1)

            @block.vector
            def _(v):
                v.wait_ge(s_c, 32)
                v.tensor_copy(cb[:], cbf[:])
                v.tensor_copy(selm[:].rearrange("p a b -> p (a b)"), cf[:, CF_SELM:CF_SELM + 4 * P])
                v.wait_ge(s_b, 16 * len(biases))
                ch = Chain(v, s_ch, 0, 3)
                ch(v.tensor_copy(bpart[:, 0, :], braw[:]))
                ch(v.tensor_sub(bmid[:], braw[:], bpart[:, 0, :]))
                ch(v.tensor_copy(bpart[:, 1, :], bmid[:]))
                ch.end()
                v.tensor_sub(bpart[:, 2, :], bmid[:], bpart[:, 1, :]).then_inc(s_p, 1)
                v.wait_ge(s_t, 1)
                v.tensor_scalar(lnsc[:], lnsc[:], gts[:, 1:2], None, ALU.mult)

    def router_pe_dve(st, l):
        o = {}
        o["xn"] = sb(st, f"xn{l}", [P, 2, P])
        o["xnT"] = sb(st, f"xnT{l}", [P, 2, P])
        o["sc"] = sb(st, f"sc{l}", [P, E])
        o["mx8"] = sb(st, f"mx8{l}", [P, 8])
        o["ix8"] = sb(st, f"ix8{l}", [P, 8], U32)
        o["ps"] = ps(st, f"psR{l}")
        for n in ("xn_ready", "xn_t", "xnT_ready", "score_mm", "score_read", "rt_step"):
            o[n] = sem(st, n + str(l))
        o["stored"] = [sem(st, f"xn_stored{l}{k}") for k in range(2)]
        return o

    def pe_xnT(pe, o):
        def stage(i, k, h):
            pe.wait_ge(o["xn_ready"], i + 1)
            wait(pe, o["score_read"], i)
            nc.tensor.transpose(o["ps"][:, 0:P], o["xn"][:, k, :], ident).then_inc(o["xn_t"], 1)
        return stage

    def pe_score(pe, o, l):
        def stage(i, k, h):
            pe.wait_ge(o["xnT_ready"], i + 1)
            nc.tensor.matmul(o["ps"][:, P:P + E], o["xnT"][:, k, :], wr[l][:], start=True, stop=True).then_inc(o["score_mm"], 1)
        return stage

    def dve_xnT(v, o):
        def stage(i, k, h):
            v.wait_ge(o["xn_t"], i + 1)
            nc.vector.tensor_copy(o["xnT"][:, k, :], o["ps"][:, 0:P]).then_inc(o["xnT_ready"], 1)
        return stage

    def dve_top(v, o):
        def stage(i, k, h):
            v.wait_ge(o["score_mm"], i + 1)
            v.tensor_copy(o["sc"][:], o["ps"][:, P:P + E]).then_inc(o["score_read"], 1)
            wait_apart(v, o["score_read"], i + 1, vfence)
            ch = Chain(v, o["rt_step"], i, 4)
            ch(v.max(o["mx8"][:], o["sc"][:]), vfence)
            ch(v.max_index(o["ix8"][:], o["mx8"][:], o["sc"][:]))
            ch(v.tensor_copy(topv[:, bass.ds(i, 1), :].rearrange("p a c -> p (a c)"), o["mx8"][:, 0:2]))
            ch(v.tensor_copy(topi[:, bass.ds(i, 1), :].rearrange("p a c -> p (a c)"), o["ix8"][:, 0:2]))
            ch.end()
        return stage

    def sp_xn(sp, o, l):
        def stage(i, k, h):
            sp.wait_ge(o["xn_ready"], i + 1)
            sp.dma_start(xn_d[l][bass.ts(i, P), :], o["xn"][:, k, :]).then_inc(o["stored"][k], 16)
        return stage

    with ExitStack() as st:
        mk = sb(st, "mk", [P, 2, P], I32)
        nz = sb(st, "nz", [P, 2, P])
        anyk = sb(st, "anyk", [P, 2, 2])
        mb = sb(st, "mb", [P, 2, P], BF16)
        st6 = sb(st, "st6", [P, 6])
        mv = sb(st, "mv", [P, 2, 2])
        rs = sb(st, "rs", [P, 2, 1])
        qn = sb(st, "qn", [P, P])
        qx = sb(st, "qx", [P, 2, NH0, 32])
        kx = sb(st, "kx", [P, 2, NH0, 32])
        vx = sb(st, "vx", [P, 2, NH0, DH0 + 1])
        qT = sb(st, "qT", [P, 2, 4, P], F32R)
        kT = sb(st, "kT", [P, 2, 4, P], F32R)
        pr = sb(st, "pr", [P, 2, 4, 4 * P])
        mx = sb(st, "mx", [P, 4, 4])
        m2 = sb(st, "m2", [P, 4, 32])
        mT = sb(st, "mT", [P, 2, P], F32R)
        rd = sb(st, "rd", [P, NH0])
        at = sb(st, "at", [P, NH0, DH0])
        st6b = sb(st, "st6b", [P, 6])
        mvb = sb(st, "mvb", [P, 2, 2])
        rsb = sb(st, "rsb", [P, 2, 1])
        p1 = [ps(st, f"p1{k}") for k in range(2)]
        p2 = [ps(st, f"p2{k}") for k in range(2)]
        pqk, po, pm = ps(st, "pqk"), ps(st, "po"), ps(st, "pm")
        o = router_pe_dve(st, 0)
        names = ("mask_bits", "mask_ready", "row_any", "bias_step", "kx_ready", "vx_ready", "var1", "rstd1", "q_step", "qx_ready",
                 "qk_t", "qk_ready", "s1_done", "max_done", "m_step", "m_ready", "m_t", "mT_ready", "s2_done", "exp_done",
                 "av_done", "o_read", "o_step", "var2", "rstd2", "pool_step", "init_done", "x_step")
        s = {n: sem(st, n + "A") for n in names}
        s_in = [sem(st, f"tile_in{k}") for k in range(2)]

        with nc.Block() as block:
            @block.sync
            def _(sp):
                def load(i, k, h):
                    wait(sp, s["mask_bits"], i - 1)
                    sp.dma_start(xs[:, bass.ds(i, 1), :], x_d[bass.ds(i, 1), :, :].rearrange("a s d -> s a d")).then_inc(s_in[k], 16)
                    sp.dma_start(cx[:, bass.ds(i, 1), :], ctx_d[bass.ds(i, 1), :, :].rearrange("a s d -> s a d")).then_inc(s_in[k], 16)
                    sp.dma_start(mk[:, k, :], mask_d[bass.ds(i, 1), :, :, :].rearrange("a b q k -> (a b q) k")).then_inc(s_in[k], 16)
                skewed(sp, B, [(4, load), (-2, sp_xn(sp, o, 0))])
                for k in range(2):
                    sp.wait_ge(o["stored"][k], 16 * B // 2)

            @block.gpsimd
            def _(g):
                g.memset(qx[:], 0.0)
                g.memset(kx[:], 0.0)
                g.memset(m2[:], 0.0)
                g.memset(vx[:], 1.0).then_inc(s["init_done"], 1)
                g.wait_ge(s["init_done"], 1)

                def keys(i, k, h):
                    wait(g, s["qk_t"], 2 * i - 2)
                    wait_apart(g, s_in[k], 48 * (h + 1), gfence)
                    c = cx[:, bass.ds(i, 1), :].rearrange("p a (h d) -> p (a h) d", d=DH0)
                    ch = Chain(g, s["pool_step"], i, 1)
                    ch(g.tensor_copy(kx[:, k, :, 0:8].bitcast(F32R), c), gfence)
                    ch.end()
                    g.tensor_copy(kx[:, k, :, 8:16].bitcast(F32R), c)
                    g.tensor_tensor(kx[:, k, :, 16:24], c, kx[:, k, :, 0:8], ALU.subtract).then_inc(s["kx_ready"], 1)

                def values(i, k, h):
                    wait_apart(g, s["av_done"], i - 1, gfence)
                    g.tensor_copy(vx[:, k, :, 0:DH0],
                                  cx[:, bass.ds(i, 1), :].rearrange("p a (h d) -> p (a h) d", d=DH0)).then_inc(s["vx_ready"], 1)

                def root1(i, k, h):
                    g.wait_ge(s["var1"], i + 1)
                    g.tensor_tensor(rs[:, k, :], mv[:, k, 1:2], half[:], ALU.pow).then_inc(s["rstd1"], 1)

                def root2(i, k, h):
                    g.wait_ge(s["var2"], i + 1)
                    g.tensor_tensor(rsb[:, k, :], mvb[:, k, 1:2], half[:], ALU.pow).then_inc(s["rstd2"], 1)
                skewed(g, B, [(2, keys), (0, values), (-1, root2), (3, root1)])

            @block.vector
            def _(v):
                v.wait_ge(s["init_done"], 1)

                def norm1(i, k, h):
                    wait(v, s["rstd1"], i - 1)
                    wait_apart(v, s_in[k], 48 * (h + 1), vfence)
                    ch = Chain(v, s["x_step"], i, 2)
                    ch(v.bn_stats(st6[:], xs[:, bass.ds(i, 1), :].rearrange("p a d -> p (a d)")), vfence)
                    ch(v.bn_aggr(mv[:, k, :], st6[:]))
                    ch.end()
                    v.tensor_scalar(mv[:, k, 1:2], mv[:, k, 1:2], LN_EPS, None, ALU.add).then_inc(s["var1"], 1)
                    wait(v, s["mask_ready"], i - 1)
                    v.tensor_scalar(nz[:, k, :], mk[:, k, :], 0.0, None, ALU.not_equal).then_inc(s["mask_bits"], 1)
                    v.wait_ge(s["mask_bits"], i + 1)
                    v.reduce_max(anyk[:, k, 0:1], nz[:, k, :], AX.X).then_inc(s["row_any"], 1)
                    v.wait_ge(s["row_any"], i + 1)
                    ch = Chain(v, s["bias_step"], i, 1)
                    ch(v.tensor_scalar(anyk[:, k, 1:2], anyk[:, k, 0:1], BIG, None, ALU.mult))
                    ch.end()

                def query(i, k, h):
                    v.wait_ge(s["rstd1"], i + 1)
                    wait(v, s["qk_t"], 2 * i - 2)
                    wait(v, s["s2_done"], 4 * i - 4)
                    v.tensor_scalar(mb[:, k, :], nz[:, k, :], 1.0, anyk[:, k, 1:2], ALU.subtract, ALU.mult).then_inc(s["mask_ready"], 1)
                    ch = Chain(v, s["q_step"], i, 3)
                    ch(v.tensor_tensor(rs[:, k, :], rs[:, k, :], anyk[:, k, 0:1], ALU.mult))
                    ch(v.tensor_scalar(qn[:], xs[:, bass.ds(i, 1), :].rearrange("p a d -> p (a d)"), mv[:, k, 0:1], rs[:, k, :],
                                       ALU.subtract, ALU.mult))
                    q = qn[:].rearrange("p (h d) -> p h d", d=DH0)
                    ch(v.tensor_copy(qx[:, k, :, 0:8].bitcast(F32R), q))
                    ch.end()
                    v.tensor_copy(qx[:, k, :, 16:24].bitcast(F32R), q)
                    v.tensor_tensor(qx[:, k, :, 8:16], q, qx[:, k, :, 0:8], ALU.subtract).then_inc(s["qx_ready"], 1)

                def maxima(i, k, h):
                    for g in range(4):
                        v.wait_ge(s["s1_done"], 4 * i + g + 1)
                        if g == 0:
                            wait(v, s["m_ready"], i)
                        v.reduce_max(mx[:, g, :], p1[g % 2][:].rearrange("p (t k) -> p t k", t=4), AX.X).then_inc(s["max_done"], 1)
                    v.wait_ge(s["max_done"], 4 * i + 4)
                    wait(v, s["m_t"], i)
                    ch = Chain(v, s["m_step"], i, 1)
                    ch(v.tensor_copy(m2[:, :, 0:4].bitcast(F32R), mx[:]))
                    ch.end()
                    v.tensor_tensor(m2[:, :, 4:8], mx[:], m2[:, :, 0:4], ALU.subtract).then_inc(s["m_ready"], 1)

                def max_rows(i, k, h):
                    v.wait_ge(s["m_t"], i + 1)
                    wait(v, s["s2_done"], 4 * i - 4)
                    v.tensor_copy(mT[:, k, :], pm[:, 0:P]).then_inc(s["mT_ready"], 1)

                def attended(i, k, h):
                    v.wait_ge(s["av_done"], i + 1)
                    ov = po[:, 0:NH0 * (DH0 + 1)].rearrange("p (h d) -> p h d", d=DH0 + 1)
                    ch = Chain(v, s["o_step"], i, 4)
                    ch(v.reciprocal(rd[:], ov[:, :, DH0]))
                    v.tensor_tensor(at[:], ov[:, :, 0:DH0], rd[:].unsqueeze(2).broadcast_to([P, NH0, DH0]), ALU.mult).then_inc(s["o_read"], 1)
                    wait(v, s["rstd2"], i - 1)
                    v.wait_ge(s["o_read"], i + 1)
                    xv = xs[:, bass.ds(i, 1), :].rearrange("p a d -> p (a d)")
                    ch(v.scalar_tensor_tensor(xv, at[:].rearrange("p h d -> p (h d)"), gts[:, 0:1], xv, ALU.mult, ALU.add), vfence)
                    ch(v.bn_stats(st6b[:], xv), vfence)
                    ch(v.bn_aggr(mvb[:, k, :], st6b[:]))
                    ch.end()
                    v.tensor_scalar(mvb[:, k, 1:2], mvb[:, k, 1:2], LN_EPS, None, ALU.add).then_inc(s["var2"], 1)

                def norm2(i, k, h):
                    v.wait_ge(s["rstd2"], i + 1)
                    wait(v, o["stored"][k], 16 * h)
                    wait(v, o["xn_t"], i - 1)
                    v.tensor_scalar(o["xn"][:, k, :], xs[:, bass.ds(i, 1), :].rearrange("p a d -> p (a d)"), mvb[:, k, 0:1],
                                    rsb[:, k, :], ALU.subtract, ALU.mult).then_inc(o["xn_ready"], 1)
                skewed(v, B, [(0, maxima), (-4, dve_top(v, o)), (0, max_rows), (3, norm1), (2, query),
                              (-1, attended), (-2, norm2), (-3, dve_xnT(v, o))])

            @block.scalar
            def _(act):
                def operands(i, k, h):
                    for n, to in enumerate((qT, kT)):
                        act.wait_ge(s["qk_t"], 2 * i + n + 1)
                        wait(act, s["s2_done"], 4 * i - 4)
                        nc.scalar.activation(to[:, k].rearrange("p a b -> p (a b)"), pqk[:], ACT.Copy).then_inc(s["qk_ready"], 1)

                def exps(i, k, h):
                    for g in range(4):
                        act.wait_ge(s["s2_done"], 4 * i + g + 1)
                        if g == 0:
                            wait(act, s["av_done"], i - 1)
                        nc.scalar.activation(pr[:, k, g, :], p2[g % 2][:], ACT.Exp, scale=float(DH0) ** -0.5).then_inc(s["exp_done"], 1)
                skewed(act, B, [(1, operands), (0, exps)])

            @block.tensor
            def _(pe):
                mm = nc.tensor.matmul

                def first(i, k, h):
                    pe.wait_ge(s["qk_ready"], 2 * i + 2)
                    pe.wait_ge(s["mask_ready"], i + 1)
                    for g in range(4):
                        wait(pe, s["max_done"], 4 * i + g - 1)
                        mm(p1[g % 2][:].rearrange("p (t k) -> p t k", t=4), identb,
                           mb[:, k, :].unsqueeze(1).broadcast_to([P, 4, P]), start=True, stop=True)
                        for t in range(4):
                            last = mm(p1[g % 2][:, t * P:(t + 1) * P], qT[32 * g:32 * g + 32, k, t, :],
                                      kT[32 * g:32 * g + 32, k, t, :], start=False, stop=True, skip_group_check=True)
                        last.then_inc(s["s1_done"], 1)

                def turn(n, i, k):
                    pe.wait_ge(s["qx_ready" if n == 0 else "kx_ready"], i + 1)
                    wait(pe, s["qk_ready"], 2 * i + n)
                    x = (qx, kx)[n]
                    for t in range(4):
                        last = nc.tensor.transpose(pqk[:, t * P:(t + 1) * P], x[:, k, 4 * t:4 * t + 4, :].rearrange("p h d -> p (h d)"), ident)
                    last.then_inc(s["qk_t"], 1)

                def turn_m(i, k, h):
                    pe.wait_ge(s["m_ready"], i + 1)
                    wait(pe, s["mT_ready"], i)
                    nc.tensor.transpose(pm[:, 0:P], m2[:].rearrange("p g t -> p (g t)"), ident).then_inc(s["m_t"], 1)

                def second(i, k, h):
                    pe.wait_ge(s["mT_ready"], i + 1)
                    for g in range(4):
                        wait(pe, s["exp_done"], 4 * i + g - 1)
                        mm(p2[g % 2][:].rearrange("p (t k) -> p t k", t=4), mb[:, k, :], identb4, start=True, stop=True)
                        rows = slice(32 * g, 32 * g + 32)
                        for t in range(4):
                            to = p2[g % 2][:, t * P:(t + 1) * P]
                            mm(to, kT[rows, k, t, :], qT[rows, k, t, :], start=False, stop=False, skip_group_check=True)
                            last = mm(to, selm[rows, t, :], mT[rows, k, :], start=False, stop=True, skip_group_check=True)
                        last.then_inc(s["s2_done"], 1)

                def weigh(i, k, h):
                    pe.wait_ge(s["exp_done"], 4 * i + 4)
                    pe.wait_ge(s["vx_ready"], i + 1)
                    wait(pe, s["o_read"], i)
                    for t in range(4):
                        for g in range(4):
                            hd = 4 * t + g
                            last = mm(po[:, hd * 9:hd * 9 + 9], pr[:, k, g, t * P:(t + 1) * P], vx[:, k, hd, :], start=True, stop=True)
                    last.then_inc(s["av_done"], 1)
                skewed(pe, B, [(0, first), (1, lambda i, k, h: turn(0, i, k)), (-4, pe_score(pe, o, 0)), (-1, weigh),
                               (1, lambda i, k, h: turn(1, i, k)), (-3, pe_xnT(pe, o)), (0, turn_m), (0, second)])


    def route(l):
        with ExitStack() as st:
            def t(name, shape, dt=F32):
                return sb(st, f"{name}_r{l}", shape, dt)
            one = t("one", [P, E * B])
            oh = [t("oh0", [P, E, B]), t("oh1", [P, E, B])]
            sel = t("sel", [P, E, B], BF16)
            pre = t("pre", [P, E, B])
            tot = t("tot", [P, E, B])
            run = t("run", [P, E, B])
            exc = t("exc", [P, E, B])
            cmp = t("cmp", [P, E, B])
            cnt, nte, end, off = [t(n, [P, E]) for n in ("cnt", "nte", "end", "off")]
            slf = t("slf", [P, B, 2])
            hi = t("hi", [P, B, 2], I32)
            lo = t("lo", [P, B, 2], I32)
            hif, lof = t("hif", [P, B, 2]), t("lof", [P, B, 2])
            cmpj = t("cmpj", [P, NT, E])
            tef = t("tef", [P, NT])
            H = B
            ohlo = t("ohlo", [P, H, P], BF16)
            ohhi = t("ohhi", [P, H, NT], BF16)
            rhs = t("rhs", [P, H, 2, NT], BF16)
            srcf = t("srcf", [P, NT])
            wx = t("wx", [P, B])
            pp, pt, pi = [ps(st, f"{n}_r{l}") for n in ("pp", "pt", "pi")]
            s_st, s_sel, s_pre, s_rhs, s_inv, s_wx, s_we = [sem(st, f"{n}_r{l}") for n in
                ("route_step", "sel_ready", "prefix_done", "lists_ready", "inverse_done", "gap_ready", "gap_exp")]
            with nc.Block() as block:
                @block.tensor
                def _(pe):
                    pe.wait_ge(s_sel, 1)
                    se = sel[:].rearrange("p e t -> p (e t)")
                    nc.tensor.matmul(pp[:, 0:E * B], cb[:, CB_UPS:CB_UPS + P], se, start=True, stop=True)
                    nc.tensor.matmul(pt[:, 0:E * B], cb[:, CB_ONE:CB_ONE + P], se, start=True, stop=True).then_inc(s_pre, 1)
                    for part in range(TOPK * B // H):
                        pe.wait_ge(s_rhs, part + 1)
                        for m in range(H):
                            last = nc.tensor.matmul(pi[:, 0:2 * NT], ohlo[:, m, :], rhs[:, m].rearrange("p a j -> p (a j)"),
                                                    start=(part == 0 and m == 0), stop=(part == TOPK * B // H - 1 and m == H - 1))
                        last.then_inc(s_inv, 1)

                @block.scalar
                def _(act):
                    if l == 0:
                        act.wait_ge(s_wx, 1)
                        nc.scalar.activation(wx[:], wx[:], ACT.Exp).then_inc(s_we, 1)

                @block.vector
                def _(v):
                    ch = Chain(v, s_st, 0, None)
                    tt, ts = v.tensor_tensor, v.tensor_scalar
                    eb = cf[:, CF_E:CF_E + E * B].rearrange("p (e t) -> p e t", e=E)
                    for k in range(2):
                        ch(tt(oh[k][:], topi[:, :, k].unsqueeze(1).broadcast_to([P, E, B]), eb, ALU.is_equal))
                    tt(sel[:], oh[0][:], oh[1][:], ALU.add).then_inc(s_sel, 1)
                    if l == 0:
                        tt(wx[:], topv[:, :, 1], topv[:, :, 0], ALU.subtract).then_inc(s_wx, 1)
                        v.wait_ge(s_we, 1)
                        ch(ts(wt[:, :, 1], wx[:], 1.0, None, ALU.add))
                        ch(v.reciprocal(wt[:, :, 0], wt[:, :, 1]))
                        ch(tt(wt[:, :, 1], wx[:], wt[:, :, 0], ALU.mult))
                        ch(ts(wt[:].rearrange("p t k -> p (t k)"), wt[:].rearrange("p t k -> p (t k)"), gts[:, 2:3], None, ALU.mult))
                    else:
                        ch(v.memset(wt[:], 1.0 / TOPK))
                        ch(ts(wt[:].rearrange("p t k -> p (t k)"), wt[:].rearrange("p t k -> p (t k)"), gts[:, 3:4], None, ALU.mult))
                    ch(v.memset(one[:], 1.0))
                    v.wait_ge(s_pre, 1)
                    ch(v.tensor_copy(pre[:].rearrange("p e t -> p (e t)"), pp[:, 0:E * B]))
                    ch(v.tensor_copy(tot[:].rearrange("p e t -> p (e t)"), pt[:, 0:E * B]))
                    ch(v.tensor_tensor_scan(run[:].rearrange("p e t -> p (e t)"), one[:], tot[:].rearrange("p e t -> p (e t)"),
                                            0.0, ALU.mult, ALU.add))
                    ch(tt(exc[:], run[:], tot[:], ALU.subtract))
                    ch(tt(cnt[:], run[:, :, B - 1], exc[:, :, 0], ALU.subtract))
                    ch(tt(cmp[:], cnt[:].unsqueeze(2).broadcast_to([P, E, B]),
                          cf[:, CF_THR:CF_THR + E * B].rearrange("p (e t) -> p e t", e=E), ALU.is_gt))
                    ch(v.tensor_reduce(nte[:], cmp[:], AX.X, ALU.add))
                    ch(v.tensor_tensor_scan(end[:], one[:, 0:E], nte[:], 0.0, ALU.mult, ALU.add))
                    ch(tt(off[:], end[:], nte[:], ALU.subtract))
                    ch(v.scalar_tensor_tensor(off[:], off[:], float(P), exc[:, :, 0], ALU.mult, ALU.subtract))
                    ch(tt(pre[:], pre[:], exc[:], ALU.add))
                    ch(tt(pre[:], pre[:], off[:].unsqueeze(2).broadcast_to([P, E, B]), ALU.add))
                    for k in range(2):
                        ch(tt(oh[k][:], oh[k][:], pre[:], ALU.mult))
                        ch(v.tensor_reduce(slf[:, :, k], oh[k][:].rearrange("p e t -> p t e"), AX.X, ALU.add))
                    ch(v.tensor_copy(slot[:], slf[:]))
                    ch(ts(hi[:], slot[:], 7, None, ALU.arith_shift_right))
                    ch(ts(lo[:], slot[:], P - 1, None, ALU.bitwise_and))
                    ch(v.tensor_copy(hif[:], hi[:]))
                    ch(v.tensor_copy(lof[:], lo[:]))
                    jb = cf[:, CF_J:CF_J + NT]
                    ch(tt(cmpj[:], end[:].unsqueeze(1).broadcast_to([P, NT, E]), jb.unsqueeze(2).broadcast_to([P, NT, E]), ALU.is_le))
                    ch(v.tensor_reduce(tef[:], cmpj[:], AX.X, ALU.add))
                    ch(ts(tef[:], tef[:], float(E - 1), None, ALU.min))
                    ch(v.tensor_copy(texp[:], tef[:]))
                    lf = lof[:].rearrange("p t k -> p (t k)")
                    hf = hif[:].rearrange("p t k -> p (t k)")
                    for part in range(TOPK * B // H):
                        ms = slice(part * H, (part + 1) * H)
                        wait(v, s_inv, part)
                        ch(tt(ohlo[:], lf[:, ms].unsqueeze(2).broadcast_to([P, H, P]),
                              cf[:, CF_IOTA:CF_IOTA + P].unsqueeze(1).broadcast_to([P, H, P]), ALU.is_equal))
                        ch(tt(ohhi[:], hf[:, ms].unsqueeze(2).broadcast_to([P, H, NT]), jb.unsqueeze(1).broadcast_to([P, H, NT]), ALU.is_equal))
                        ch(tt(rhs[:, :, 0, :], ohhi[:], cb[:, CB_T + part * H:CB_T + (part + 1) * H].unsqueeze(2).broadcast_to([P, H, NT]), ALU.mult))
                        ts(rhs[:, :, 1, :], ohhi[:], cf[:, CF_P:CF_P + 1], None, ALU.mult).then_inc(s_rhs, 1)
                        v.wait_ge(s_rhs, part + 1)
                    v.wait_ge(s_inv, TOPK * B // H)
                    ch(ts(srcf[:], pi[:, 0:NT], float(P), None, ALU.mult))
                    ch(tt(srcf[:], srcf[:], pi[:, NT:2 * NT], ALU.add))
                    ch(v.tensor_copy(src[:], srcf[:]))
                    ch.end()

    route(0)

    def experts(l, layers, bofs):
        L = len(layers)
        with ExitStack() as st:
            ix = sb(st, f"ix_f{l}", [P, 2], I32)
            xg = sb(st, f"xg_f{l}", [P, 2, P])
            act_in = [sb(st, f"in{n}_f{l}", [P, 2, c * P]) for n, (_, c, _, _) in enumerate(layers)]
            hid = [None] + [sb(st, f"h{n}_f{l}", [P, 2, F]) for n in range(1, L)]
            y = sb(st, f"y_f{l}", [P, 2, P])
            ptr = [ps(st, f"pt{n}_f{l}") for n in range(L)]
            pmm = [ps(st, f"pm{n}_f{l}") for n in range(L)]
            s_g = [sem(st, f"gathered{k}_f{l}") for k in range(2)]
            s_o = [sem(st, f"stored{k}_f{l}") for k in range(2)]
            s_ix = sem(st, f"index_ready_f{l}")
            s_t = [sem(st, f"turned{n}_f{l}") for n in range(L)]
            s_in = [sem(st, f"input_ready{n}_f{l}") for n in range(L)]
            s_m = [sem(st, f"product{n}_f{l}") for n in range(L)]
            s_h = [sem(st, f"hidden{n}_f{l}") for n in range(L)]
            tl = [2 * (L - 1 - n) + 1 for n in range(L)]
            ml = [2 * (L - 1 - n) for n in range(L)]
            with nc.Block() as block:
                @block.gpsimd
                def _(g):
                    def gather(i, k, h):
                        wait_apart(g, s_t[0], i - 1, gfence)
                        g.tensor_copy(ix[:, k:k + 1], src[:, bass.ds(i, 1)]).then_inc(s_ix, 1)
                        wait_apart(g, s_ix, i + 1, gfence)
                        g.indirect_dma_start(xg[:, k, :], None, xn_d[l], bass.IndirectOffsetOnAxis(ix[:, k:k + 1], axis=0)).then_inc(s_g[k], 16)
                    skewed(g, NT, [(tl[0] + 1, gather)])

                @block.tensor
                def _(pe):
                    def turn(n):
                        def stage(i, k, h):
                            if n == 0:
                                pe.wait_ge(s_g[k], 16 * (h + 1))
                            else:
                                pe.wait_ge(s_h[n - 1], i + 1)
                            wait(pe, s_in[n], i)
                            a = xg[:, k, :] if n == 0 else hid[n][:, k, :]
                            for c in range(layers[n][1]):
                                last = nc.tensor.transpose(ptr[n][:, c * P:(c + 1) * P], a[:, c * P:(c + 1) * P], ident)
                            last.then_inc(s_t[n], 1)
                        return stage

                    def product(n):
                        w, chunks, cols, _ = layers[n]

                        def stage(i, k, h):
                            pe.wait_ge(s_in[n], i + 1)
                            wait(pe, s_h[n], i)
                            e = pe.value_load(texp[0:1, bass.ds(i, 1)], min_val=0, max_val=E - 1)
                            nc.tensor.matmul(pmm[n][:, 0:cols], cb[:, CB_ONE:CB_ONE + P], brow[:, bass.ds(e * cols + bofs[n], cols)],
                                             start=True, stop=False)
                            for c in range(chunks):
                                last = nc.tensor.matmul(pmm[n][:, 0:cols], act_in[n][:, k, c * P:(c + 1) * P], w(e, c),
                                                        start=False, stop=c == chunks - 1)
                            last.then_inc(s_m[n], 1)
                        return stage
                    stages = [(ml[n], product(n)) for n in range(L)] + [(tl[n], turn(n)) for n in range(L)]
                    skewed(pe, NT, stages)

                @block.scalar
                def _(act):
                    def hidden(n):
                        def stage(i, k, h):
                            act.wait_ge(s_m[n], i + 1)
                            wait(act, s_t[n + 1], i - 1)
                            nc.scalar.activation(hid[n + 1][:, k, :], pmm[n][:], layers[n][3]).then_inc(s_h[n], 1)
                        return stage
                    skewed(act, NT, [(ml[n], hidden(n)) for n in range(L - 1)])

                @block.vector
                def _(v):
                    def inputs(n):
                        def stage(i, k, h):
                            v.wait_ge(s_t[n], i + 1)
                            wait(v, s_m[n], i - 1)
                            nc.vector.tensor_copy(act_in[n][:, k, :], ptr[n][:, 0:layers[n][1] * P]).then_inc(s_in[n], 1)
                        return stage

                    def result(i, k, h):
                        v.wait_ge(s_m[L - 1], i + 1)
                        wait(v, s_o[k], 16 * h)
                        nc.vector.tensor_copy(y[:, k, :], pmm[L - 1][:, 0:P]).then_inc(s_h[L - 1], 1)
                    skewed(v, NT, [(0, result)] + [(tl[n], inputs(n)) for n in range(L)])

                @block.sync
                def _(sp):
                    def store(i, k, h):
                        sp.wait_ge(s_h[L - 1], i + 1)
                        sp.dma_start(ys_d[l][bass.ts(i, P), :], y[:, k, :]).then_inc(s_o[k], 16)
                    skewed(sp, NT, [(0, store)])
                    for k in range(2):
                        sp.wait_ge(s_o[k], 16 * NT // 2)

    def expert(w):
        if len(w.shape) == 3:
            return lambda e, c: w[:, bass.ds(e, 1), :].rearrange("p a f -> p (a f)")
        return lambda e, c: w[:, bass.ds(e, 1), c, :].rearrange("p a f -> p (a f)")

    experts(0, [(expert(w01), 1, F, ACT.Relu), (expert(w02), FC, P, None)], BO[:2])

    w11 = wts[:, 0:E * F].rearrange("p (e f) -> p e f", e=E)
    w13 = wts[:, E * F:2 * E * F].rearrange("p (e c d) -> p e c d", e=E, c=FC)

    def gather_pair(g, l, ix, yg, s_ix, s_g, free, free_of):
        def stage(i, k, h):
            wait_apart(g, free, free_of(i), gfence)
            for n in range(TOPK):
                g.tensor_copy(ix[n][:, k:k + 1], slot[:, bass.ds(i, 1), n]).then_inc(s_ix, 1)
            wait_apart(g, s_ix, 2 * i + 2, gfence)
            for n in range(TOPK):
                g.indirect_dma_start(yg[n][:, k, :], None, ys_d[l], bass.IndirectOffsetOnAxis(ix[n][:, k:k + 1], axis=0)).then_inc(s_g[k], 16)
        return stage

    stB = ExitStack()
    gall = sb(stB, "gall", [P, 2, B, NH1])
    mvx = sb(stB, "mvx", [P, B, 2])
    enm = sb(stB, "enm", [P, B, NH1])
    aT3 = sb(stB, "aT3", [96, B // 4, P], BF16)
    nT3 = sb(stB, "nT3", [96, B // 4, P], BF16)
    with ExitStack() as st:
        ix = [sb(st, f"ix{n}_b", [P, 2], I32) for n in range(TOPK)]
        yg = [sb(st, f"yg{n}_b", [P, 2, P]) for n in range(TOPK)]
        tmp = sb(st, "tmp_b", [P, P])
        st6 = sb(st, "st6_b", [P, 6])
        mv = sb(st, "mv_b", [P, 2, 2])
        rs = sb(st, "rs_b", [P, 2, 1])
        xn = sb(st, "xn_b", [P, 2, P])
        xT = sb(st, "xT_b", [P, 2, 2, P])
        cT_in = sb(st, "cT_in", [P, 2, P])
        s_ctx = sem(st, "ctx_copied_b")
        pT, pG = ps(st, "pT_b"), ps(st, "pG_b")
        names = ("ix_ready", "x_added", "norm_step", "var_ready", "rstd_ready", "xn_ready", "turned", "xT_ready", "gates_mm", "gates_read", "w_in")
        s = {n: sem(st, n + "_b") for n in names}
        s_g = [sem(st, f"y_in{k}_b") for k in range(2)]
        with nc.Block() as block:
            @block.sync
            def _(sp):
                sp.dma_start(w11, w11_d.rearrange("e d f -> d e f")).then_inc(s["w_in"], 16)
                for e in range(E):
                    sp.dma_start(w13[:, e], w13_d[e].rearrange("(c p) d -> p c d", p=P)).then_inc(s["w_in"], 16)
                sp.dma_start(brow[0:3, 0:BN1], bparts_d[:, BO[2]:BN]).then_inc(s["w_in"], 16)
                sp.wait_ge(s["w_in"], 16 * (E + 2))

            @block.gpsimd
            def _(g):
                def root(i, k, h):
                    g.wait_ge(s["var_ready"], i + 1)
                    g.tensor_tensor(rs[:, k, :], mv[:, k, 1:2], half[:], ALU.pow).then_inc(s["rstd_ready"], 1)
                skewed(g, B, [(2, gather_pair(g, 0, ix, yg, s["ix_ready"], s_g, s["x_added"], lambda i: i - 1)), (0, root)])

            @block.vector
            def _(v):
                def combine(i, k, h):
                    v.wait_ge(s_g[k], 32 * (h + 1))
                    xv = xs[:, bass.ds(i, 1), :].rearrange("p a d -> p (a d)")
                    wv = wt[:, bass.ds(i, 1), :].rearrange("p a n -> p (a n)")
                    ch = Chain(v, s["norm_step"], i, 3)
                    ch(v.scalar_tensor_tensor(tmp[:], yg[0][:, k, :], wv[:, 0:1], xv, ALU.mult, ALU.add))
                    v.scalar_tensor_tensor(xv, yg[1][:, k, :], wv[:, 1:2], tmp[:], ALU.mult, ALU.add).then_inc(s["x_added"], 1)
                    wait_apart(v, s["x_added"], i + 1, vfence)
                    ch(v.bn_stats(st6[:], xv), vfence)
                    wait_apart(v, s["xn_ready"], i - 1, vfence)
                    ch(v.bn_aggr(mv[:, k, :], st6[:]))
                    ch.end()
                    v.tensor_scalar(mv[:, k, 1:2], mv[:, k, 1:2], LN_EPS, None, ALU.add).then_inc(s["var_ready"], 1)

                def normed(i, k, h):
                    v.wait_ge(s["rstd_ready"], i + 1)
                    wait(v, s["turned"], i - 1)
                    mo = mvx[:, bass.ds(i, 1), :].rearrange("p a n -> p (a n)")
                    v.tensor_copy(mo[:, 0:1], mv[:, k, 0:1])
                    v.tensor_copy(mo[:, 1:2], rs[:, k, :])
                    v.tensor_scalar(xn[:, k, :], xs[:, bass.ds(i, 1), :].rearrange("p a d -> p (a d)"), mv[:, k, 0:1], rs[:, k, :],
                                    ALU.subtract, ALU.mult).then_inc(s["xn_ready"], 1)

                def turned(i, k, h):
                    v.wait_ge(s["turned"], i + 1)
                    wait(v, s["gates_mm"], i - 1)
                    v.tensor_copy(xT[:, k].rearrange("p a s -> p (a s)"), pT[:, 0:2 * P]).then_inc(s["xT_ready"], 1)

                def gates(i, k, h):
                    v.wait_ge(s["gates_mm"], i + 1)
                    v.tensor_copy(gall[:, :, bass.ds(i, 1), :].rearrange("p n a h -> p n (a h)"),
                                  pG[:, 0:2 * NH1].rearrange("p (n h) -> p n h", n=2)).then_inc(s["gates_read"], 1)
                skewed(v, B, [(0, combine), (-1, normed), (-2, turned), (-3, gates)])

            @block.tensor
            def _(pe):
                def turn(i, k, h):
                    pe.wait_ge(s["xn_ready"], i + 1)
                    pe.wait_ge(s_ctx, i + 1)
                    wait(pe, s["xT_ready"], i)
                    nc.tensor.transpose(pT[:, 0:P], xn[:, k, :], ident)
                    nc.tensor.transpose(pT[:, P:2 * P], cT_in[:, k, :], ident).then_inc(s["turned"], 1)

                def gate(i, k, h):
                    pe.wait_ge(s["xT_ready"], i + 1)
                    wait(pe, s["gates_read"], i)
                    for r in range(3):
                        last = nc.tensor.matmul(pG[:, 0:2 * NH1], xT[:, k, min(r, 1), :], wgate[:, r, :], start=r == 0, stop=r == 2)
                    last.then_inc(s["gates_mm"], 1)
                skewed(pe, B, [(-1, turn), (-2, gate)])

            @block.scalar
            def _(act):
                def context(i, k, h):
                    wait(act, s["turned"], i - 1)
                    nc.scalar.activation(cT_in[:, k, :], cx[:, bass.ds(i, 1), :].rearrange("p a d -> p (a d)"), ACT.Copy).then_inc(s_ctx, 1)
                skewed(act, B, [(0, context)])

    with ExitStack() as st:
        def t(name, shape=(P, B * NH1), dt=F32):
            return sb(st, name + "_g", list(shape), dt)
        ig, fg, ab, l1, mn, lf, cs, a, ac, nac, mm_ = [t(n) for n in ("ig", "fg", "ab", "l1", "mn", "lf", "cs", "a", "ac", "nac", "mm")]
        AT = t("AT", (P, 2, P))
        one = t("one", (P, P))
        res = t("res")
        parts = t("parts", (P, B // 4, 3, 4 * NH1), BF16)
        nparts = t("nparts", (P, B // 4, 3, 4 * NH1), BF16)
        pcs, paT, pAc = ps(st, "pcs"), ps(st, "paT"), ps(st, "pAc")
        p3 = [ps(st, f"p3{n}", (P, 1024), BF16) for n in range(2)]
        names = ("step", "abs_ready", "exp_done", "ln_done", "lf_ready", "cs_done", "a_ready", "aT_done", "AT_ready", "Ac_done",
                 "m_ready", "enm_done", "parts_ready", "parts_t")
        s = {n: sem(st, n + "_g") for n in names}
        with nc.Block() as block:
            @block.scalar
            def _(act):
                act.wait_ge(s["abs_ready"], 1)
                nc.scalar.activation(l1[:], ab[:], ACT.Exp, scale=-1.0).then_inc(s["exp_done"], 1)
                act.wait_ge(s["exp_done"], 1)
                nc.scalar.activation(l1[:], l1[:], ACT.Ln, bias=1.0).then_inc(s["ln_done"], 1)
                act.wait_ge(s["m_ready"], 1)
                nc.scalar.activation(enm[:].rearrange("p b h -> p (b h)"), mm_[:], ACT.Exp, scale=-1.0).then_inc(s["enm_done"], 1)

            @block.vector
            def _(v):
                ch = Chain(v, s["step"], 0, None)
                tt = v.tensor_tensor
                bh = lambda x: x[:].rearrange("p (b h) -> p b h", b=B)
                bb = lambda n: gbias[:, n, :].unsqueeze(1).broadcast_to([P, B, NH1])
                ch(tt(bh(fg), gall[:, 1], bb(1), ALU.add))
                v.scalar_tensor_tensor(ab[:], fg[:], -1.0, fg[:], ALU.mult, ALU.max).then_inc(s["abs_ready"], 1)
                ch(tt(bh(ig), gall[:, 0], bb(0), ALU.add))
                ch(v.tensor_scalar(mn[:], fg[:], 0.0, None, ALU.min))
                ch(v.memset(one[:], 1.0))
                v.wait_ge(s["ln_done"], 1)
                tt(lf[:], mn[:], l1[:], ALU.subtract).then_inc(s["lf_ready"], 1)
                v.wait_ge(s["cs_done"], 1)
                ch(v.tensor_copy(cs[:], pcs[:, 0:B * NH1]))
                tt(a[:], ig[:], cs[:], ALU.subtract).then_inc(s["a_ready"], 1)
                v.wait_ge(s["aT_done"], 1)
                for n in range(2):
                    v.tensor_tensor_scan(AT[:, n, :], one[:], paT[:, n * P:(n + 1) * P], -3e38, ALU.mult, ALU.max).then_inc(s["AT_ready"], 1)
                v.wait_ge(s["Ac_done"], 1)
                ch(v.tensor_copy(ac[:], pAc[:, 0:B * NH1]))
                tt(mm_[:], cs[:], ac[:], ALU.add).then_inc(s["m_ready"], 1)
                ch(v.tensor_scalar(nac[:], ac[:], -1.0, None, ALU.mult))
                for x, to in ((a, parts), (nac, nparts)):
                    g4 = lambda y: y[:].rearrange("p (g c) -> p g c", c=4 * NH1)
                    ch(v.tensor_copy(to[:, :, 0, :], g4(x)))
                    ch(tt(g4(res), g4(x), to[:, :, 0, :], ALU.subtract))
                    ch(v.tensor_copy(to[:, :, 1, :], g4(res)))
                    ch(tt(g4(res), g4(res), to[:, :, 1, :], ALU.subtract))
                    v.tensor_copy(to[:, :, 2, :], g4(res)).then_inc(s["parts_ready"], 1)
                    v.wait_ge(s["parts_ready"], 1 if to is parts else 2)
                for n, to in enumerate((aT3, nT3)):
                    v.wait_ge(s["parts_t"], n + 1)
                    ch(v.tensor_copy(to[:].rearrange("p g s -> p (g s)"), p3[n][0:96, :]))

            @block.tensor
            def _(pe):
                pe.wait_ge(s["lf_ready"], 1)
                nc.tensor.matmul(pcs[:, 0:B * NH1], cf[:, CF_UPI:CF_UPI + P], lf[:], start=True, stop=True).then_inc(s["cs_done"], 1)
                pe.wait_ge(s["a_ready"], 1)
                nc.tensor.transpose(paT[:, 0:P], a[:, 0:P], ident)
                nc.tensor.transpose(paT[:, P:2 * P], a[:, P:2 * P], ident).then_inc(s["aT_done"], 1)
                pe.wait_ge(s["AT_ready"], 2)
                nc.tensor.transpose(pAc[:, 0:P], AT[:, 0, :], ident)
                nc.tensor.transpose(pAc[:, P:2 * P], AT[:, 1, :], ident).then_inc(s["Ac_done"], 1)
                pe.wait_ge(s["parts_ready"], 2)
                for n, x in enumerate((parts, nparts)):
                    for g in range(B // 4):
                        last = nc.tensor.transpose(p3[n][0:96, g * P:(g + 1) * P], x[:, g].rearrange("p t c -> p (t c)"), identb)
                    last.then_inc(s["parts_t"], 1)

    with ExitStack() as st:
        qn = sb(st, "qn_c", [P, P])
        qx = sb(st, "qx_c", [P, 2, NH1, 64])
        kx = sb(st, "kx_c", [P, 2, NH1, 64])
        vx = sb(st, "vx_c", [P, 2, NH1, DH1 + 1])
        qT = sb(st, "qT_c", [P, 2, 4, P], F32R)
        kT = sb(st, "kT_c", [P, 2, 4, P], F32R)
        D = sb(st, "D_c", [P, 2, 2, 4 * P])
        C = sb(st, "C_c", [P, 2, 2, 4 * P])
        den = sb(st, "den_c", [P, NH1])
        hh = sb(st, "hh_c", [P, 2, NH1, DH1])
        hn = sb(st, "hn_c", [P, P])
        st6, st6b = sb(st, "st6_c", [P, 6]), sb(st, "st6b_c", [P, 6])
        mv, mvb = sb(st, "mv_c", [P, 2, 2]), sb(st, "mvb_c", [P, 2, 2])
        rs, rsb = sb(st, "rs_c", [P, 2, 1]), sb(st, "rsb_c", [P, 2, 1])
        pd = [ps(st, f"pd{r}") for r in range(2)]
        pq = [ps(st, f"pq{r}") for r in range(2)]
        pqk, ph = ps(st, "pqk_c"), ps(st, "ph_c")
        o = router_pe_dve(st, 1)
        names = ("init", "kx_ready", "vx_ready", "qx_ready", "qk_t", "qk_ready", "d_done", "D_ready", "s_done", "C_ready",
                 "h_done", "h_read", "pool_step", "q_step", "h_step", "var1", "rstd1", "var2", "rstd2", "x_step")
        s = {n: sem(st, n + "_c") for n in names}
        sel32 = cb[0:96, CB_SEL:CB_SEL + 4 * NH1]
        with nc.Block() as block:
            @block.sync
            def _(sp):
                skewed(sp, B, [(-3, sp_xn(sp, o, 1))])
                for k in range(2):
                    sp.wait_ge(o["stored"][k], 16 * B // 2)

            @block.gpsimd
            def _(g):
                g.memset(qx[:], 0.0)
                g.memset(kx[:], 0.0)
                g.memset(vx[:], 1.0).then_inc(s["init"], 1)
                g.wait_ge(s["init"], 1)
                c = lambda i: cx[:, bass.ds(i, 1), :].rearrange("p a (h d) -> p (a h) d", d=DH1)

                def keys(i, k, h):
                    wait_apart(g, s["qk_t"], 2 * i - 2, gfence)
                    ch = Chain(g, s["pool_step"], i, 1)
                    ch(g.tensor_copy(kx[:, k, :, 0:16].bitcast(F32R), c(i)), gfence)
                    ch.end()
                    g.tensor_copy(kx[:, k, :, 16:32].bitcast(F32R), c(i))
                    g.tensor_tensor(kx[:, k, :, 32:48], c(i), kx[:, k, :, 0:16], ALU.subtract).then_inc(s["kx_ready"], 1)

                def values(i, k, h):
                    wait_apart(g, s["h_done"], i - 1, gfence)
                    g.tensor_copy(vx[:, k, :, 0:DH1], c(i)).then_inc(s["vx_ready"], 1)

                def root1(i, k, h):
                    g.wait_ge(s["var1"], i + 1)
                    g.tensor_tensor(rs[:, k, :], mv[:, k, 1:2], half[:], ALU.pow).then_inc(s["rstd1"], 1)

                def root2(i, k, h):
                    g.wait_ge(s["var2"], i + 1)
                    g.tensor_tensor(rsb[:, k, :], mvb[:, k, 1:2], half[:], ALU.pow).then_inc(s["rstd2"], 1)
                skewed(g, B, [(2, keys), (0, values), (-1, root1), (-2, root2)])

            @block.vector
            def _(v):
                v.wait_ge(s["init"], 1)

                def query(i, k, h):
                    wait(v, s["qk_t"], 2 * i - 2)
                    wait(v, s["qx_ready"], i)
                    mo = mvx[:, bass.ds(i, 1), :].rearrange("p a n -> p (a n)")
                    ch = Chain(v, s["q_step"], i, 3)
                    ch(v.tensor_scalar(qn[:], xs[:, bass.ds(i, 1), :].rearrange("p a d -> p (a d)"), mo[:, 0:1], mo[:, 1:2],
                                       ALU.subtract, ALU.mult))
                    ch(v.tensor_scalar(qn[:], qn[:], float(DH1) ** -0.5, None, ALU.mult))
                    q = qn[:].rearrange("p (h d) -> p h d", d=DH1)
                    ch(v.tensor_copy(qx[:, k, :, 0:16].bitcast(F32R), q))
                    ch.end()
                    v.tensor_copy(qx[:, k, :, 32:48].bitcast(F32R), q)
                    v.tensor_tensor(qx[:, k, :, 16:32], q, qx[:, k, :, 0:16], ALU.subtract).then_inc(s["qx_ready"], 1)

                def products(i, k, h):
                    for r in range(2):
                        v.wait_ge(s["s_done"], 2 * i + r + 1)
                        v.wait_ge(s["D_ready"], 2 * i + r + 1)
                        if r == 0:
                            wait(v, s["h_done"], i - 1)
                        v.tensor_tensor(C[:, k, r, :], pq[r][:], D[:, k, r, :], ALU.mult).then_inc(s["C_ready"], 1)

                def divide(i, k, h):
                    v.wait_ge(s["h_done"], i + 1)
                    hv = ph[:, 0:NH1 * (DH1 + 1)].rearrange("p (h d) -> p h d", d=DH1 + 1)
                    ch = Chain(v, s["h_step"], i, 6)
                    ch(v.scalar_tensor_tensor(den[:], hv[:, :, DH1], -1.0, enm[:, bass.ds(i, 1), :].rearrange("p a h -> p (a h)"), ALU.mult, ALU.max))
                    ch(v.tensor_tensor(den[:], hv[:, :, DH1], den[:], ALU.max))
                    ch(v.tensor_scalar(den[:], den[:], NORM_EPS, None, ALU.add))
                    ch(v.reciprocal(den[:], den[:]))
                    v.tensor_tensor(hh[:, k], hv[:, :, 0:DH1], den[:].unsqueeze(2).broadcast_to([P, NH1, DH1]), ALU.mult).then_inc(s["h_read"], 1)
                    wait_apart(v, s["h_read"], i + 1, vfence)
                    ch(v.bn_stats(st6[:], hh[:, k].rearrange("p h d -> p (h d)")), vfence)
                    ch(v.bn_aggr(mv[:, k, :], st6[:]))
                    ch.end()
                    v.tensor_scalar(mv[:, k, 1:2], mv[:, k, 1:2], LN_EPS, None, ALU.add).then_inc(s["var1"], 1)

                def add(i, k, h):
                    v.wait_ge(s["rstd1"], i + 1)
                    xv = xs[:, bass.ds(i, 1), :].rearrange("p a d -> p (a d)")
                    ch = Chain(v, s["x_step"], i, 5)
                    ch(v.tensor_scalar(hn[:], hh[:, k].rearrange("p h d -> p (h d)"), mv[:, k, 0:1], rs[:, k, :], ALU.subtract, ALU.mult))
                    ch(v.tensor_tensor(hn[:], hn[:], lnsc[:], ALU.mult))
                    ch(v.tensor_tensor(xv, xv, hn[:], ALU.add), vfence)
                    ch(v.bn_stats(st6b[:], xv), vfence)
                    ch(v.bn_aggr(mvb[:, k, :], st6b[:]))
                    ch.end()
                    v.tensor_scalar(mvb[:, k, 1:2], mvb[:, k, 1:2], LN_EPS, None, ALU.add).then_inc(s["var2"], 1)

                def norm2(i, k, h):
                    v.wait_ge(s["rstd2"], i + 1)
                    wait(v, o["stored"][k], 16 * h)
                    wait(v, o["xn_t"], i - 1)
                    v.tensor_scalar(o["xn"][:, k, :], xs[:, bass.ds(i, 1), :].rearrange("p a d -> p (a d)"), mvb[:, k, 0:1],
                                    rsb[:, k, :], ALU.subtract, ALU.mult).then_inc(o["xn_ready"], 1)
                skewed(v, B, [(0, products), (-5, dve_top(v, o)), (2, query), (-1, divide), (-2, add), (-3, norm2), (-4, dve_xnT(v, o))])

            @block.scalar
            def _(act):
                def operands(i, k, h):
                    for n, to in enumerate((qT, kT)):
                        act.wait_ge(s["qk_t"], 2 * i + n + 1)
                        wait(act, s["s_done"], 2 * i - 2)
                        nc.scalar.activation(to[:, k].rearrange("p a b -> p (a b)"), pqk[:], ACT.Copy).then_inc(s["qk_ready"], 1)

                def decays(i, k, h):
                    for r in range(2):
                        act.wait_ge(s["d_done"], 2 * i + r + 1)
                        if r == 0:
                            wait(act, s["C_ready"], 2 * i - 2)
                        nc.scalar.activation(D[:, k, r, :], pd[r][:], ACT.Exp).then_inc(s["D_ready"], 1)
                skewed(act, B, [(0, decays), (1, operands)])

            @block.tensor
            def _(pe):
                mm = nc.tensor.matmul
                h4 = lambda x: x.rearrange("p (t k) -> p t k", t=4)

                def exponents(i, k, h):
                    for r in range(2):
                        wait(pe, s["D_ready"], 2 * i + r - 1)
                        c0 = (i % 4) * NH1 + r
                        grp = i // 4
                        mm(h4(pd[r][:]), identb, cb[:, CB_TRI:CB_TRI + P].unsqueeze(1).broadcast_to([P, 4, P]), start=True, stop=True)
                        mm(h4(pd[r][:]), aT3[:, bass.ds(grp, 1), :].rearrange("p g s -> p (g s)"),
                           cb[0:96, bass.ds(CB_SEL + c0, 4, 2)].unsqueeze(2).broadcast_to([96, 4, P]), start=False, stop=True, skip_group_check=True)
                        for t in range(4):
                            last = mm(pd[r][:, t * P:(t + 1) * P], cb[0:96, bass.ds(CB_SEL + c0 + 2 * t, 1)].broadcast_to([96, P]),
                                      nT3[:, bass.ds(grp, 1), :].rearrange("p g s -> p (g s)"), start=False, stop=True, skip_group_check=True)
                        last.then_inc(s["d_done"], 1)

                def turn(n, i, k):
                    pe.wait_ge(s["qx_ready" if n == 0 else "kx_ready"], i + 1)
                    wait(pe, s["qk_ready"], 2 * i + n)
                    x = (qx, kx)[n]
                    for t in range(4):
                        last = nc.tensor.transpose(pqk[:, t * P:(t + 1) * P], x[:, k, 2 * t:2 * t + 2, :].rearrange("p h d -> p (h d)"), ident)
                    last.then_inc(s["qk_t"], 1)

                def scores(i, k, h):
                    pe.wait_ge(s["qk_ready"], 2 * i + 2)
                    for r in range(2):
                        wait(pe, s["C_ready"], 2 * i + r - 1)
                        rows = slice(64 * r, 64 * r + 64)
                        for t in range(4):
                            last = mm(pq[r][:, t * P:(t + 1) * P], kT[rows, k, t, :], qT[rows, k, t, :], start=True, stop=True)
                        last.then_inc(s["s_done"], 1)

                def weigh(i, k, h):
                    pe.wait_ge(s["C_ready"], 2 * i + 2)
                    pe.wait_ge(s["vx_ready"], i + 1)
                    wait(pe, s["h_read"], i)
                    for t in range(4):
                        for r in range(2):
                            hd = 2 * t + r
                            last = mm(ph[:, hd * (DH1 + 1):(hd + 1) * (DH1 + 1)], C[:, k, r, t * P:(t + 1) * P], vx[:, k, hd, :], start=True, stop=True)
                    last.then_inc(s["h_done"], 1)
                skewed(pe, B, [(0, exponents), (1, lambda i, k, h: turn(0, i, k)), (-5, pe_score(pe, o, 1)), (0, scores),
                               (1, lambda i, k, h: turn(1, i, k)), (-4, pe_xnT(pe, o)), (-1, weigh)], unroll=4)
    stB.close()

    route(1)
    experts(1, [(expert(w11), 1, F, ACT.Gelu), (expert(w12), FC, F, ACT.Gelu), (expert(w13), FC, P, None)],
            [b - BO[2] for b in BO[2:]])

    with ExitStack() as st:
        ix = [sb(st, f"ix{n}_e", [P, 2], I32) for n in range(TOPK)]
        yg = [sb(st, f"yg{n}_e", [P, 2, P]) for n in range(TOPK)]
        tmp = sb(st, "tmp_e", [P, P])
        xo = sb(st, "xo_e", [P, 2, P])
        s_ix, s_x, s_st = sem(st, "ix_ready_e"), sem(st, "x_added_e"), sem(st, "step_e")
        s_g = [sem(st, f"y_in{k}_e") for k in range(2)]
        s_o = [sem(st, f"out_stored{k}") for k in range(2)]
        with nc.Block() as block:
            @block.gpsimd
            def _(g):
                skewed(g, B, [(2, gather_pair(g, 1, ix, yg, s_ix, s_g, s_x, lambda i: i - 1))])

            @block.vector
            def _(v):
                def combine(i, k, h):
                    v.wait_ge(s_g[k], 32 * (h + 1))
                    xv = xs[:, bass.ds(i, 1), :].rearrange("p a d -> p (a d)")
                    wv = wt[:, bass.ds(i, 1), :].rearrange("p a n -> p (a n)")
                    wait(v, s_x, i)
                    ch = Chain(v, s_st, i, 1)
                    ch(v.scalar_tensor_tensor(tmp[:], yg[0][:, k, :], wv[:, 0:1], xv, ALU.mult, ALU.add))
                    ch.end()
                    wait(v, s_o[k], 16 * h)
                    v.scalar_tensor_tensor(xo[:, k, :], yg[1][:, k, :], wv[:, 1:2], tmp[:], ALU.mult, ALU.add).then_inc(s_x, 1)
                skewed(v, B, [(0, combine)])

            @block.sync
            def _(sp):
                def store(i, k, h):
                    sp.wait_ge(s_x, i + 1)
                    sp.dma_start(out_d[bass.ds(i, 1), :, :].rearrange("a s d -> (a s) d"), xo[:, k, :]).then_inc(s_o[k], 16)
                skewed(sp, B, [(0, store)])
                for k in range(2):
                    sp.wait_ge(s_o[k], 16 * B // 2)
    return keep


INS = ['x', 'ctx_1024', 'mask_Bx1xSxS2_ik1', 'g_xattn', 'g_ffn', 'L0_ffn_Wg', 'L0_ffn_W1', 'L0_ffn_b1', 'L0_ffn_W2', 'L0_ffn_b2',
       'L1_xattn_igate_w', 'L1_xattn_igate_b', 'L1_xattn_fgate_w', 'L1_xattn_fgate_b', 'L1_xattn_ln_scale',
       'L1_ffn_expert_tokens', 'L1_ffn_W1', 'L1_ffn_b1', 'L1_ffn_W2', 'L1_ffn_b2', 'L1_ffn_W3', 'L1_ffn_b3']


def kernel(**inputs):
    import numpy as np
    import concourse.bacc as bacc
    from concourse.bass_utils import run_bass_kernel_spmd

    nc = bacc.Bacc("TRN2", target_bir_lowering=False, num_devices=1)
    arrays, args = {}, []
    cf, cb = constants()
    for name, a in [("const_f32", cf), ("const_small", cb)] + [(n, np.ascontiguousarray(inputs[n])) for n in INS]:
        arrays[f"in_{name}"] = a
        args.append(nc.dram_tensor(f"in_{name}", a.shape, mybir.dt.from_np(a.dtype), kind="ExternalInput").ap())
    args.append(nc.dram_tensor("out_0", (B, P, P), F32, kind="ExternalOutput").ap())
    build(nc, *args)
    r = run_bass_kernel_spmd(nc, [arrays], core_ids=[0])
    return r.results[0]["out_0"]
```

```python
import concourse.bass as bass
from concourse import mybir
from contextlib import ExitStack

F32 = mybir.dt.float32
F32R = mybir.dt.float32r
BF16 = mybir.dt.bfloat16
I32 = mybir.dt.int32
U32 = mybir.dt.uint32
ALU = mybir.AluOpType
ACT = mybir.ActivationFunctionType
AX = mybir.AxisListType

P = 128
B = 32
E = 8
F = 512
FC = F // P
NH0, DH0 = 16, 8
NH1, DH1 = 8, 16
TOPK = 2
NT = TOPK * B + E
LN_EPS = 1e-5
NORM_EPS = 1e-6
BIG = 1e9

CF_ID, CF_UPI, CF_IOTA, CF_P, CF_E, CF_THR, CF_J, CF_W = 0, 128, 256, 384, 385, 641, 897, 969
CB_ID, CB_UPS, CB_ONE, CB_TRI, CB_SEL, CB_T, CB_SELM, CB_W = 0, 128, 256, 384, 512, 544, 608, 616
BO = [0, E * F, E * F + E * P, 2 * E * F + E * P, 3 * E * F + E * P]
BN = 3 * E * F + 2 * E * P
BN1 = BN - BO[2]


def constants():
    import numpy as np
    p = np.arange(P)
    cf = np.zeros((P, CF_W), np.float32)
    cf[:, CF_ID:CF_ID + P] = np.eye(P)
    cf[:, CF_UPI:CF_UPI + P] = p[:, None] <= p[None, :]
    cf[:, CF_IOTA:CF_IOTA + P] = p
    cf[:, CF_P] = p
    cf[:, CF_E:CF_E + E * B] = np.repeat(np.arange(E), B)
    cf[:, CF_THR:CF_THR + E * B] = np.tile(np.arange(B) * P, E)
    cf[:, CF_J:CF_J + NT] = np.arange(NT)
    cb = np.zeros((P, CB_W), np.float32)
    cb[:, CB_ID:CB_ID + P] = np.eye(P)
    cb[:, CB_UPS:CB_UPS + P] = p[:, None] < p[None, :]
    cb[:, CB_ONE:CB_ONE + P] = 1
    cb[:, CB_TRI:CB_TRI + P] = np.where(p[:, None] <= p[None, :], 0, -1e30)
    cb[:, CB_SEL:CB_SEL + 32] = (p[:, None] % 32 == np.arange(32)) & (p[:, None] < 96)
    cb[:, CB_T:CB_T + TOPK * B] = np.repeat(np.arange(B), TOPK)
    cb[:, CB_SELM:CB_SELM + 8] = -((p[:, None] % 8 == np.arange(8)) & (p[:, None] % 64 < 24)).astype(np.float32)
    return cf, cb


def wait(eng, sem, value):
    if not isinstance(value, int) or value > 0:
        eng.wait_ge(sem, value)


def wait_apart(eng, sem, value, fence):
    if not isinstance(value, int) or value > 0:
        eng.wait_ge(sem, value)
        fence(eng)


class Chain:

    def __init__(self, eng, sem, i, per):
        self.eng, self.sem, self.base, self.per, self.n = eng, sem, i * (per or 0), per, 0

    def __call__(self, ins, fence=None):
        self.n += 1
        ins.then_inc(self.sem, 1)
        if fence is None:
            self.eng.wait_ge(self.sem, self.base + self.n)
        else:
            wait_apart(self.eng, self.sem, self.base + self.n, fence)

    def step(self, ins, fence=None):
        self.n += 1
        ins.then_inc(self.sem, 1)
        yield
        if fence is None:
            self.eng.wait_ge(self.sem, self.base + self.n)
        else:
            wait_apart(self.eng, self.sem, self.base + self.n, fence)

    def end(self):
        assert self.per in (None, self.n), (self.n, self.per)


def woven(stages):
    while stages:
        stages = [st for st in stages if next(st, stages) is not stages]


def skewed(eng, n, stages, unroll=2):
    groups = [st if isinstance(st, list) else [st] for st in stages]
    leads = [lead for group in groups for lead, _ in group]

    def issue(group, tile):
        issued = [stage(*tile(lead)) for lead, stage in group if tile(lead)]
        woven([st for st in issued if st is not None])

    def step(j):
        for group in groups:
            issue(group, lambda lead: (j + lead, (j + lead) % 2, (j + lead) // 2) if 0 <= j + lead < n else None)

    first = 2 + max(0, -min(leads))
    first += -first % unroll
    last = n - max(0, max(leads))
    last -= (last - first) % unroll
    for j in range(-max(leads), first):
        step(j)
    with eng.Fori(first // unroll, last // unroll) as jj:
        for k in range(unroll):
            for group in groups:
                issue(group, lambda lead: (unroll * jj + k + lead, (k + lead) % 2, (unroll // 2) * jj + (k + lead) // 2))
    for j in range(last, n - min(leads)):
        step(j)


def build(nc, cf_d, cb_d, x_d, ctx_d, mask_d, gx_d, gf_d, wg0_d, w01_d, b01_d, w02_d, b02_d, igw_d,
          igb_d, fgw_d, fgb_d, lns_d, tok_d, w11_d, b11_d, w12_d, b12_d, w13_d, b13_d, out_d):
    def dram(name, shape, dt=F32):
        return nc.dram_tensor(name, shape, dt).ap()

    bparts_d = dram("bias_parts", (3, BN), BF16)
    xn_d = [dram("normed0", (B * P, P)), dram("normed1", (B * P, P))]
    ys_d = [dram("sorted0", (NT * P, P)), dram("sorted1", (NT * P, P))]

    keep = ExitStack()

    def sb(stack, name, shape, dt=F32):
        return stack.enter_context(nc.sbuf_tensor(name, shape, dt))

    def ps(stack, name, shape=(P, 512), dt=F32):
        return stack.enter_context(nc.psum_tensor(name, list(shape), dt))

    def sem(stack, name):
        return stack.enter_context(nc.semaphore(name))

    cf = sb(keep, "cf", [P, CF_W])
    cb = sb(keep, "cb", [P, CB_W], BF16)
    xs = sb(keep, "xs", [P, B, P])
    cx = sb(keep, "cx", [P, B, P])
    wts = sb(keep, "wts", [P, 2 * E * F + E * FC * F])
    brow = sb(keep, "brow", [P, BN1], BF16)
    gts = sb(keep, "gts", [P, 4])
    half = sb(keep, "half", [P, 1])
    wr = [sb(keep, "wr0", [P, E]), sb(keep, "wr1", [P, E])]
    wgate = sb(keep, "wgate", [P, 3, 2 * NH1])
    gbias = sb(keep, "gbias", [P, 2, NH1])
    lnsc = sb(keep, "lnsc", [P, P])
    topv = sb(keep, "topv", [P, B, 2])
    topi = sb(keep, "topi", [P, B, 2])
    wt = sb(keep, "wt", [P, B, 2])
    slot = sb(keep, "slot", [P, B, 2], I32)
    src = sb(keep, "src", [P, NT], I32)
    texp = sb(keep, "texp", [P, NT], I32)

    junk = [sb(keep, "junk_v", [P, 32]), sb(keep, "junk_g", [P, 32])]
    fences = [0, 0]

    def vfence(v):
        fences[0] = (fences[0] + 1) % 32
        v.memset(junk[0][:, fences[0]:fences[0] + 1], 0.0)

    def gfence(g):
        fences[1] = (fences[1] + 1) % 32
        g.tensor_tensor(junk[1][:, fences[1]:fences[1] + 1], half[:], half[:], ALU.mult)

    ident = cf[:, CF_ID:CF_ID + P]
    identb = cb[:, CB_ID:CB_ID + P]
    identb4 = identb.unsqueeze(1).broadcast_to([P, 4, P])
    w01 = wts[:, 0:E * F].rearrange("p (e f) -> p e f", e=E)
    w02 = wts[:, E * F:2 * E * F].rearrange("p (e c d) -> p e c d", e=E, c=FC)
    w12 = wts[:, 2 * E * F:].rearrange("p (e c f) -> p e c f", e=E, c=FC)

    s_w = sem(keep, "weights_in")
    biases = [(b01_d, 0), (b02_d, BO[1]), (b11_d, BO[2]), (b12_d, BO[3]), (b13_d, BO[4])]
    with ExitStack() as st:
        cbf = sb(st, "cbf", [P, CB_W])
        braw = sb(st, "braw", [P, BN // P])
        bmid = sb(st, "bmid", [P, BN // P])
        bpart = sb(st, "bpart", [P, 3, BN // P], BF16)
        s_c, s_small, s_b, s_bp, s_br = [sem(st, n) for n in ("const_in", "small_in", "bias_in", "bias_out", "bias_rows")]
        s_ch, s_z, s_p, s_t = [sem(st, n) for n in ("dve_step", "rows_zero", "parts_ready", "tanh_done")]
        with nc.Block() as block:
            @block.sync
            def _(sp):
                sp.dma_start(cf[:], cf_d).then_inc(s_c, 16)
                sp.dma_start(cbf[:], cb_d).then_inc(s_c, 16)
                for bd, at in biases:
                    n = bd.shape[0] * bd.shape[1] // P
                    sp.dma_start(braw[:, at // P:at // P + n],
                                 bd.rearrange("e f -> (e f)").rearrange("(p c) -> p c", p=P)).then_inc(s_b, 16)
                for to, row in ((gts[:, 0:2], gx_d), (gts[:, 2:4], gf_d), (gbias[:, 0, :], igb_d),
                                (gbias[:, 1, :], fgb_d), (lnsc[:], lns_d)):
                    sp.dma_start(to, row.rearrange("(a n) -> a n", a=1).broadcast_to([P, row.shape[0]])).then_inc(s_small, 16)
                sp.dma_start(wr[0][:], wg0_d).then_inc(s_small, 16)
                sp.dma_start(w01, w01_d.rearrange("e d f -> d e f")).then_inc(s_w, 16)
                for e in range(E):
                    sp.dma_start(w02[:, e], w02_d[e].rearrange("(c p) d -> p c d", p=P)).then_inc(s_w, 16)
                sp.wait_ge(s_p, 1)
                for bd, at in biases:
                    n = bd.shape[0] * bd.shape[1]
                    sp.dma_start(bparts_d[:, at:at + n].rearrange("t (p c) -> p t c", p=P),
                                 bpart[:, :, at // P:(at + n) // P]).then_inc(s_bp, 16)
                sp.wait_ge(s_bp, 16 * len(biases))
                sp.wait_ge(s_z, 1)
                sp.dma_start(brow[0:3, 0:BO[2]], bparts_d[:, 0:BO[2]]).then_inc(s_br, 16)
                sp.wait_ge(s_br, 16)

            @block.scalar
            def _(act):
                with nc.allow_non_contiguous_dma(reason="small weights, transposed on the way in"):
                    act.dma_start(wr[1][:], tok_d.rearrange("e d -> d e")).then_inc(s_small, 16)
                    for r in range(3):
                        act.dma_start(wgate[:, r, 0:NH1], igw_d[:, r * P:(r + 1) * P].rearrange("h d -> d h")).then_inc(s_small, 16)
                        act.dma_start(wgate[:, r, NH1:], fgw_d[:, r * P:(r + 1) * P].rearrange("h d -> d h")).then_inc(s_small, 16)
                act.wait_ge(s_small, 13 * 16)
                nc.scalar.activation(gts[:], gts[:], ACT.Tanh).then_inc(s_t, 1)

            @block.gpsimd
            def _(g):
                g.memset(half[:], -0.5)
                g.memset(brow[:], 0.0).then_inc(s_z, 1)

            @block.vector
            def _(v):
                v.wait_ge(s_c, 32)
                v.tensor_copy(cb[:], cbf[:])
                v.wait_ge(s_b, 16 * len(biases))
                ch = Chain(v, s_ch, 0, 3)
                ch(v.tensor_copy(bpart[:, 0, :], braw[:]))
                ch(v.tensor_sub(bmid[:], braw[:], bpart[:, 0, :]))
                ch(v.tensor_copy(bpart[:, 1, :], bmid[:]))
                ch.end()
                v.tensor_sub(bpart[:, 2, :], bmid[:], bpart[:, 1, :]).then_inc(s_p, 1)
                v.wait_ge(s_t, 1)
                v.tensor_scalar(lnsc[:], lnsc[:], gts[:, 1:2], None, ALU.mult)

    def router_pe_dve(st, l):
        o = {}
        o["xn"] = sb(st, f"xn{l}", [P, 2, P])
        o["xnT"] = sb(st, f"xnT{l}", [P, 2, P])
        o["sc"] = sb(st, f"sc{l}", [P, E])
        o["mx8"] = sb(st, f"mx8{l}", [P, 8])
        o["ix8"] = sb(st, f"ix8{l}", [P, 8], U32)
        o["ps"] = ps(st, f"psR{l}")
        for n in ("xn_ready", "xn_t", "xnT_ready", "score_mm", "score_read", "rt_step"):
            o[n] = sem(st, n + str(l))
        o["stored"] = [sem(st, f"xn_stored{l}{k}") for k in range(2)]
        return o

    def pe_xnT(pe, o):
        def stage(i, k, h):
            pe.wait_ge(o["xn_ready"], i + 1)
            wait(pe, o["score_read"], i)
            nc.tensor.transpose(o["ps"][:, 0:P], o["xn"][:, k, :], ident).then_inc(o["xn_t"], 1)
        return stage

    def pe_score(pe, o, l):
        def stage(i, k, h):
            pe.wait_ge(o["xnT_ready"], i + 1)
            nc.tensor.matmul(o["ps"][:, P:P + E], o["xnT"][:, k, :], wr[l][:], start=True, stop=True).then_inc(o["score_mm"], 1)
        return stage

    def act_xnT(act, o):
        def stage(i, k, h):
            act.wait_ge(o["xn_t"], i + 1)
            nc.scalar.activation(o["xnT"][:, k, :], o["ps"][:, 0:P], ACT.Copy).then_inc(o["xnT_ready"], 1)
        return stage

    def dve_top(v, o):
        def stage(i, k, h):
            v.wait_ge(o["score_mm"], i + 1)
            v.tensor_copy(o["sc"][:], o["ps"][:, P:P + E]).then_inc(o["score_read"], 1)
            yield
            wait_apart(v, o["score_read"], i + 1, vfence)
            ch = Chain(v, o["rt_step"], i, 4)
            yield from ch.step(v.max(o["mx8"][:], o["sc"][:]), vfence)
            yield from ch.step(v.max_index(o["ix8"][:], o["mx8"][:], o["sc"][:]))
            yield from ch.step(v.tensor_copy(topv[:, bass.ds(i, 1), :].rearrange("p a c -> p (a c)"), o["mx8"][:, 0:2]))
            yield from ch.step(v.tensor_copy(topi[:, bass.ds(i, 1), :].rearrange("p a c -> p (a c)"), o["ix8"][:, 0:2]))
            ch.end()
        return stage

    def sp_xn(sp, o, l):
        def stage(i, k, h):
            sp.wait_ge(o["xn_ready"], i + 1)
            sp.dma_start(xn_d[l][bass.ts(i, P), :], o["xn"][:, k, :]).then_inc(o["stored"][k], 16)
        return stage

    HR = 64

    def head_of(g, t):
        return 2 * (4 * (g // 2) + t) + g % 2

    with ExitStack() as st:
        free_at = [2 * E * F]

        def scratch(words):
            free_at[0] += words
            return wts[:, free_at[0] - words:free_at[0]]
        mk = sb(st, "mk", [P, 2, P], I32)
        nz = sb(st, "nz", [P, 2, P])
        anyk = sb(st, "anyk", [P, 2, 2])
        mb = scratch(B * P // 2).bitcast(BF16).rearrange("p (b k) -> p b k", b=B)
        st6 = sb(st, "st6", [P, 6])
        mv = sb(st, "mv", [P, 2, 2])
        rs = sb(st, "rs", [P, 2, 1])
        qn = sb(st, "qn", [P, P])
        qr = sb(st, "qr", [P, P])
        kr = sb(st, "kr", [P, P])
        qx = sb(st, "qx", [P, 2, NH0, HR], BF16)
        kx = sb(st, "kx", [P, 2, NH0, HR], BF16)
        vx = scratch(2 * NH0 * 32).rearrange("p (k h d) -> p k h d", k=2, h=NH0)
        qT = sb(st, "qT", [P, 2, 8, P], BF16)
        kT = sb(st, "kT", [P, 2, 8, P], BF16)
        pr = scratch(2 * 4 * 4 * P).rearrange("p (k g n) -> p k g n", k=2, g=4)
        mx = sb(st, "mx", [P, 2, 8])
        mr = sb(st, "mr", [P, 2, 8])
        m3 = sb(st, "m3", [P, 2, HR], BF16)
        mT = sb(st, "mT", [P, 2, P], BF16)
        ao = scratch(2 * 4 * P).rearrange("p (k n) -> p k n", k=2)
        rd = sb(st, "rd", [P, NH0])
        at = sb(st, "at", [P, NH0, DH0])
        st6b = sb(st, "st6b", [P, 6])
        mvb = sb(st, "mvb", [P, 2, 2])
        rsb = sb(st, "rsb", [P, 2, 1])
        p1 = [ps(st, f"p1{k}") for k in range(2)]
        p2 = [ps(st, f"p2{k}") for k in range(2)]
        pqk, po, pv = ps(st, "pqk", (P, 8 * P), BF16), ps(st, "po"), ps(st, "pv")
        o = router_pe_dve(st, 0)
        names = ("mask_bits", "mask_ready", "row_any", "bias_step", "kx_ready", "vx_ready", "var1", "rstd1", "q_step", "qx_ready",
                 "qk_t", "qk_ready", "s1_done", "max_done", "m_step", "m_ready", "m_t", "mT_ready", "s2_done", "exp_done",
                 "av_done", "ao_ready", "out_t", "o_read", "o_step", "var2", "rstd2", "pool_step", "init_done", "x_step")
        s = {n: sem(st, n + "A") for n in names}
        s_in = [sem(st, f"tile_in{k}") for k in range(2)]

        with nc.Block() as block:
            @block.sync
            def _(sp):
                def load(i, k, h):
                    wait(sp, s["mask_bits"], i - 1)
                    sp.dma_start(xs[:, bass.ds(i, 1), :], x_d[bass.ds(i, 1), :, :].rearrange("a s d -> s a d")).then_inc(s_in[k], 16)
                    sp.dma_start(cx[:, bass.ds(i, 1), :], ctx_d[bass.ds(i, 1), :, :].rearrange("a s d -> s a d")).then_inc(s_in[k], 16)
                    sp.dma_start(mk[:, k, :], mask_d[bass.ds(i, 1), :, :, :].rearrange("a b q k -> (a b q) k")).then_inc(s_in[k], 16)
                skewed(sp, B, [(5, load), (-4, sp_xn(sp, o, 0))])
                for k in range(2):
                    sp.wait_ge(o["stored"][k], 16 * B // 2)
                sp.wait_ge(s_w, 16 * (1 + E))

            @block.gpsimd
            def _(g):
                g.memset(kx[:], 0.0)
                g.memset(qx[:], 0.0)
                g.memset(m3[:], 0.0)
                g.memset(vx[:, :, :, DH0 + 1:], 0.0)
                g.memset(vx[:, :, :, DH0:DH0 + 1], 1.0).then_inc(s["init_done"], 1)
                g.wait_ge(s["init_done"], 1)

                def keys(i, k, h):
                    wait(g, s["qk_t"], 2 * i - 2)
                    wait_apart(g, s_in[k], 48 * (h + 1), gfence)
                    c = cx[:, bass.ds(i, 1), :].rearrange("p a (h d) -> p (a h) d", d=DH0)
                    r = kr[:].rearrange("p (h d) -> p h d", d=DH0)
                    ch = Chain(g, s["pool_step"], i, 4)
                    ch(g.tensor_copy(kx[:, k, :, 0:8], c), gfence)
                    ch(g.tensor_tensor(r, c, kx[:, k, :, 0:8], ALU.subtract), gfence)
                    ch(g.tensor_copy(kx[:, k, :, 8:16], r))
                    ch(g.tensor_tensor(kx[:, k, :, 16:24], r, kx[:, k, :, 8:16], ALU.subtract), gfence)
                    ch.end()
                    g.tensor_copy(kx[:, k, :, 24:40], kx[:, k, :, 0:16])
                    g.tensor_copy(kx[:, k, :, 40:48], kx[:, k, :, 0:8]).then_inc(s["kx_ready"], 1)

                def values(i, k, h):
                    wait_apart(g, s["av_done"], i - 1, gfence)
                    g.tensor_copy(vx[:, k, :, 0:DH0],
                                  cx[:, bass.ds(i, 1), :].rearrange("p a (h d) -> p (a h) d", d=DH0)).then_inc(s["vx_ready"], 1)

                def root1(i, k, h):
                    g.wait_ge(s["var1"], i + 1)
                    g.tensor_tensor(rs[:, k, :], mv[:, k, 1:2], half[:], ALU.pow).then_inc(s["rstd1"], 1)

                def root2(i, k, h):
                    g.wait_ge(s["var2"], i + 1)
                    g.tensor_tensor(rsb[:, k, :], mvb[:, k, 1:2], half[:], ALU.pow).then_inc(s["rstd2"], 1)
                skewed(g, B, [(2, keys), (-1, values), (-4, root2), (3, root1)])

            @block.vector
            def _(v):
                v.wait_ge(s["init_done"], 1)

                def norm1(i, k, h):
                    wait(v, s["rstd1"], i - 1)
                    wait_apart(v, s_in[k], 48 * (h + 1), vfence)
                    ch = Chain(v, s["x_step"], i, 2)
                    yield from ch.step(v.bn_stats(st6[:], xs[:, bass.ds(i, 1), :].rearrange("p a d -> p (a d)")), vfence)
                    yield from ch.step(v.bn_aggr(mv[:, k, :], st6[:]))
                    ch.end()
                    v.tensor_scalar(mv[:, k, 1:2], mv[:, k, 1:2], LN_EPS, None, ALU.add).then_inc(s["var1"], 1)
                    wait(v, s["mask_ready"], i - 1)
                    v.tensor_scalar(nz[:, k, :], mk[:, k, :], 0.0, None, ALU.not_equal).then_inc(s["mask_bits"], 1)
                    yield
                    v.wait_ge(s["mask_bits"], i + 1)
                    v.reduce_max(anyk[:, k, 0:1], nz[:, k, :], AX.X).then_inc(s["row_any"], 1)
                    yield
                    v.wait_ge(s["row_any"], i + 1)
                    ch = Chain(v, s["bias_step"], i, 1)
                    yield from ch.step(v.tensor_scalar(anyk[:, k, 1:2], anyk[:, k, 0:1], BIG, None, ALU.mult))
                    ch.end()

                def query(i, k, h):
                    v.wait_ge(s["rstd1"], i + 1)
                    wait(v, s["qk_t"], 2 * i - 2)
                    v.tensor_scalar(mb[:, bass.ds(i, 1), :].rearrange("p a k -> p (a k)"), nz[:, k, :], 1.0, anyk[:, k, 1:2],
                                    ALU.subtract, ALU.mult).then_inc(s["mask_ready"], 1)
                    ch = Chain(v, s["q_step"], i, 5)
                    yield from ch.step(v.tensor_tensor(rs[:, k, :], rs[:, k, :], anyk[:, k, 0:1], ALU.mult))
                    yield from ch.step(v.tensor_scalar(qn[:], xs[:, bass.ds(i, 1), :].rearrange("p a d -> p (a d)"), mv[:, k, 0:1], rs[:, k, :],
                                       ALU.subtract, ALU.mult))
                    q = qn[:].rearrange("p (h d) -> p h d", d=DH0)
                    r = qr[:].rearrange("p (h d) -> p h d", d=DH0)
                    yield from ch.step(v.tensor_copy(qx[:, k, :, 0:24].rearrange("p h (n d) -> p h n d", n=3), q.unsqueeze(2).broadcast_to([P, NH0, 3, DH0])))
                    yield from ch.step(v.tensor_tensor(r, q, qx[:, k, :, 0:8], ALU.subtract))
                    yield from ch.step(v.tensor_copy(qx[:, k, :, 24:40].rearrange("p h (n d) -> p h n d", n=2), r.unsqueeze(2).broadcast_to([P, NH0, 2, DH0])))
                    ch.end()
                    v.tensor_tensor(qx[:, k, :, 40:48], r, qx[:, k, :, 24:32], ALU.subtract).then_inc(s["qx_ready"], 1)

                def maxima(i, k, h):
                    for g in range(4):
                        v.wait_ge(s["s1_done"], 4 * i + g + 1)
                        if g == 0:
                            wait(v, s["m_ready"], i)
                        v.reduce_max(mx[:, g % 2, 4 * (g // 2):4 * (g // 2) + 4], p1[g % 2][:].rearrange("p (t k) -> p t k", t=4), AX.X).then_inc(s["max_done"], 1)
                    yield
                    v.wait_ge(s["max_done"], 4 * i + 4)
                    wait(v, s["m_t"], i)
                    ch = Chain(v, s["m_step"], i, 3)
                    yield from ch.step(v.tensor_copy(m3[:, :, 0:8], mx[:]))
                    yield from ch.step(v.tensor_tensor(mr[:], mx[:], m3[:, :, 0:8], ALU.subtract))
                    yield from ch.step(v.tensor_copy(m3[:, :, 8:16], mr[:]))
                    ch.end()
                    v.tensor_tensor(m3[:, :, 16:24], mr[:], m3[:, :, 8:16], ALU.subtract).then_inc(s["m_ready"], 1)

                def attended(i, k, h):
                    v.wait_ge(s["out_t"], i + 1)
                    ov = pv[:].rearrange("p (n d) -> p n d", d=32)
                    ch = Chain(v, s["o_step"], i, 4)
                    yield from ch.step(v.reciprocal(rd[:], ov[:, :, DH0]))
                    for a in range(2):
                        last = v.tensor_tensor(at[:].rearrange("p (a t b) d -> p a b t d", a=2, b=2)[:, a],
                                               ov[:, 8 * a:8 * a + 8, 0:DH0].rearrange("p (b t) d -> p b t d", b=2),
                                               rd[:, 8 * a:8 * a + 8].rearrange("p (b t) -> p b t", b=2).unsqueeze(3).broadcast_to([P, 2, 4, DH0]), ALU.mult)
                    last.then_inc(s["o_read"], 1)
                    yield
                    wait(v, s["rstd2"], i - 1)
                    v.wait_ge(s["o_read"], i + 1)
                    xv = xs[:, bass.ds(i, 1), :].rearrange("p a d -> p (a d)")
                    yield from ch.step(v.scalar_tensor_tensor(xv, at[:].rearrange("p h d -> p (h d)"), gts[:, 0:1], xv, ALU.mult, ALU.add), vfence)
                    yield from ch.step(v.bn_stats(st6b[:], xv), vfence)
                    yield from ch.step(v.bn_aggr(mvb[:, k, :], st6b[:]))
                    ch.end()
                    v.tensor_scalar(mvb[:, k, 1:2], mvb[:, k, 1:2], LN_EPS, None, ALU.add).then_inc(s["var2"], 1)

                def norm2(i, k, h):
                    v.wait_ge(s["rstd2"], i + 1)
                    wait(v, o["stored"][k], 16 * h)
                    wait(v, o["xn_t"], i - 1)
                    v.tensor_scalar(o["xn"][:, k, :], xs[:, bass.ds(i, 1), :].rearrange("p a d -> p (a d)"), mvb[:, k, 0:1],
                                    rsb[:, k, :], ALU.subtract, ALU.mult).then_inc(o["xn_ready"], 1)
                skewed(v, B, [[(0, maxima), (2, query), (-6, dve_top(v, o)), (3, norm1), (-3, attended)], (-4, norm2)])

            @block.scalar
            def _(act):
                def operand(n, i, k):
                    act.wait_ge(s["qk_t"], 2 * i + n + 1)
                    wait(act, s["s2_done"], 4 * i - 4)
                    nc.scalar.activation((qT, kT)[n][:, k].rearrange("p a b -> p (a b)"), pqk[:], ACT.Copy).then_inc(s["qk_ready"], 1)

                def max_rows(i, k, h):
                    act.wait_ge(s["m_t"], i + 1)
                    wait(act, s["s2_done"], 4 * i - 4)
                    nc.scalar.activation(mT[:, k, :], pqk[:, 0:P], ACT.Copy).then_inc(s["mT_ready"], 1)

                def exps(i, k, h):
                    for g in range(4):
                        act.wait_ge(s["s2_done"], 4 * i + g + 1)
                        if g == 0:
                            wait(act, s["av_done"], i - 1)
                        nc.scalar.activation(pr[:, k, g, :], p2[g % 2][:], ACT.Exp, scale=float(DH0) ** -0.5).then_inc(s["exp_done"], 1)

                def weighted(i, k, h):
                    act.wait_ge(s["av_done"], i + 1)
                    wait(act, s["out_t"], i - 1)
                    nc.scalar.activation(ao[:, k, :], po[:], ACT.Copy).then_inc(s["ao_ready"], 1)
                skewed(act, B, [(-1, max_rows), (-1, exps), (1, lambda i, k, h: operand(0, i, k)), (-5, act_xnT(act, o)),
                                (-2, weighted), (1, lambda i, k, h: operand(1, i, k))])

            @block.tensor
            def _(pe):
                mm = nc.tensor.matmul

                def first(i, k, h):
                    pe.wait_ge(s["qk_ready"], 2 * i + 2)
                    pe.wait_ge(s["mask_ready"], i + 1)
                    for g in range(4):
                        wait(pe, s["max_done"], 4 * i + g - 1)
                        mm(p1[g % 2][:].rearrange("p (t k) -> p t k", t=4), identb,
                           mb[:, bass.ds(i, 1), :].broadcast_to([P, 4, P]), start=True, stop=True)
                        rows = slice(HR * (g % 2), HR * (g % 2) + HR)
                        for t in range(4):
                            last = mm(p1[g % 2][:, t * P:(t + 1) * P], qT[rows, k, 4 * (g // 2) + t, :],
                                      kT[rows, k, 4 * (g // 2) + t, :], start=False, stop=True, skip_group_check=True)
                        last.then_inc(s["s1_done"], 1)

                def turn(n, i, k):
                    pe.wait_ge(s["qx_ready" if n == 0 else "kx_ready"], i + 1)
                    wait(pe, s["qk_ready"], 2 * i + n)
                    if n == 0:
                        wait(pe, s["mT_ready"], i - 1)
                    x = (qx, kx)[n]
                    for t in range(8):
                        last = nc.tensor.transpose(pqk[:, t * P:(t + 1) * P], x[:, k, 2 * t:2 * t + 2, :].rearrange("p h d -> p (h d)"), identb)
                    last.then_inc(s["qk_t"], 1)

                def turn_m(i, k, h):
                    pe.wait_ge(s["m_ready"], i + 1)
                    pe.wait_ge(s["qk_ready"], min(2 * i + 4, 2 * B) if isinstance(i, int) else 2 * i + 4)
                    nc.tensor.transpose(pqk[:, 0:P], m3[:].rearrange("p g t -> p (g t)"), identb).then_inc(s["m_t"], 1)

                def second(i, k, h):
                    pe.wait_ge(s["mT_ready"], i + 1)
                    for g in range(4):
                        wait(pe, s["exp_done"], 4 * i + g - 1)
                        mm(p2[g % 2][:].rearrange("p (t k) -> p t k", t=4), mb[:, bass.ds(i, 1), :].rearrange("p a k -> p (a k)"),
                           identb4, start=True, stop=True)
                        rows = slice(HR * (g % 2), HR * (g % 2) + HR)
                        for t in range(4):
                            to = p2[g % 2][:, t * P:(t + 1) * P]
                            j = 4 * (g // 2) + t
                            mm(to, kT[rows, k, j, :], qT[rows, k, j, :], start=False, stop=False, skip_group_check=True)
                            last = mm(to, cb[rows, CB_SELM + j:CB_SELM + j + 1].broadcast_to([HR, P]), mT[rows, k, :],
                                      start=False, stop=True, skip_group_check=True)
                        last.then_inc(s["s2_done"], 1)

                def weigh(i, k, h):
                    pe.wait_ge(s["exp_done"], 4 * i + 4)
                    pe.wait_ge(s["vx_ready"], i + 1)
                    wait(pe, s["ao_ready"], i)
                    for g in range(4):
                        for t in range(4):
                            last = mm(po[32 * t:32 * t + 32, g * P:(g + 1) * P], vx[:, k, head_of(g, t), :],
                                      pr[:, k, g, t * P:(t + 1) * P], start=True, stop=True)
                    last.then_inc(s["av_done"], 1)

                def turn_out(i, k, h):
                    pe.wait_ge(s["ao_ready"], i + 1)
                    wait(pe, s["o_read"], i)
                    for g in range(4):
                        last = nc.tensor.transpose(pv[:, g * P:(g + 1) * P], ao[:, k, g * P:(g + 1) * P], ident)
                    last.then_inc(s["out_t"], 1)
                skewed(pe, B, [(-6, pe_score(pe, o, 0)), (-3, turn_out), (-1, turn_m), (0, first), (-1, second),
                               (1, lambda i, k, h: turn(0, i, k)), (-5, pe_xnT(pe, o)), (-2, weigh),
                               (1, lambda i, k, h: turn(1, i, k))])


    def route(l):
        with ExitStack() as st:
            def t(name, shape, dt=F32):
                return sb(st, f"{name}_r{l}", shape, dt)
            one = t("one", [P, E * B])
            oh = [t("oh0", [P, E, B]), t("oh1", [P, E, B])]
            sel = t("sel", [P, E, B], BF16)
            pre = t("pre", [P, E, B])
            tot = t("tot", [P, E, B])
            run = t("run", [P, E, B])
            exc = t("exc", [P, E, B])
            cmp = t("cmp", [P, E, B])
            cnt, nte, end, off = [t(n, [P, E]) for n in ("cnt", "nte", "end", "off")]
            slf = t("slf", [P, B, 2])
            hi = t("hi", [P, B, 2], I32)
            lo = t("lo", [P, B, 2], I32)
            hif, lof = t("hif", [P, B, 2]), t("lof", [P, B, 2])
            cmpj = t("cmpj", [P, NT, E])
            tef = t("tef", [P, NT])
            H = B
            ohlo = t("ohlo", [P, H, P], BF16)
            ohhi = t("ohhi", [P, H, NT], BF16)
            rhs = t("rhs", [P, H, 2, NT], BF16)
            srcf = t("srcf", [P, NT])
            wx = t("wx", [P, B])
            pp, pt, pi = [ps(st, f"{n}_r{l}") for n in ("pp", "pt", "pi")]
            s_st, s_sel, s_pre, s_rhs, s_inv = [sem(st, f"{n}_r{l}") for n in
                ("route_step", "sel_ready", "prefix_done", "lists_ready", "inverse_done")]
            if l == 0:
                s_wx, s_we = sem(st, "gap_ready"), sem(st, "gap_exp")
            with nc.Block() as block:
                @block.tensor
                def _(pe):
                    pe.wait_ge(s_sel, 1)
                    se = sel[:].rearrange("p e t -> p (e t)")
                    nc.tensor.matmul(pp[:, 0:E * B], cb[:, CB_UPS:CB_UPS + P], se, start=True, stop=True)
                    nc.tensor.matmul(pt[:, 0:E * B], cb[:, CB_ONE:CB_ONE + P], se, start=True, stop=True).then_inc(s_pre, 1)
                    for part in range(TOPK * B // H):
                        pe.wait_ge(s_rhs, part + 1)
                        for m in range(H):
                            last = nc.tensor.matmul(pi[:, 0:2 * NT], ohlo[:, m, :], rhs[:, m].rearrange("p a j -> p (a j)"),
                                                    start=(part == 0 and m == 0), stop=(part == TOPK * B // H - 1 and m == H - 1))
                        last.then_inc(s_inv, 1)

                @block.scalar
                def _(act):
                    if l == 0:
                        act.wait_ge(s_wx, 1)
                        nc.scalar.activation(wx[:], wx[:], ACT.Exp).then_inc(s_we, 1)

                @block.vector
                def _(v):
                    ch = Chain(v, s_st, 0, None)
                    tt, ts = v.tensor_tensor, v.tensor_scalar
                    eb = cf[:, CF_E:CF_E + E * B].rearrange("p (e t) -> p e t", e=E)
                    for k in range(2):
                        ch(tt(oh[k][:], topi[:, :, k].unsqueeze(1).broadcast_to([P, E, B]), eb, ALU.is_equal))
                    tt(sel[:], oh[0][:], oh[1][:], ALU.add).then_inc(s_sel, 1)
                    if l == 0:
                        tt(wx[:], topv[:, :, 1], topv[:, :, 0], ALU.subtract).then_inc(s_wx, 1)
                        v.wait_ge(s_we, 1)
                        ch(ts(wt[:, :, 1], wx[:], 1.0, None, ALU.add))
                        ch(v.reciprocal(wt[:, :, 0], wt[:, :, 1]))
                        ch(tt(wt[:, :, 1], wx[:], wt[:, :, 0], ALU.mult))
                        ch(ts(wt[:].rearrange("p t k -> p (t k)"), wt[:].rearrange("p t k -> p (t k)"), gts[:, 2:3], None, ALU.mult))
                    else:
                        ch(v.memset(wt[:], 1.0 / TOPK))
                        ch(ts(wt[:].rearrange("p t k -> p (t k)"), wt[:].rearrange("p t k -> p (t k)"), gts[:, 3:4], None, ALU.mult))
                    ch(v.memset(one[:], 1.0))
                    v.wait_ge(s_pre, 1)
                    ch(v.tensor_copy(pre[:].rearrange("p e t -> p (e t)"), pp[:, 0:E * B]))
                    ch(v.tensor_copy(tot[:].rearrange("p e t -> p (e t)"), pt[:, 0:E * B]))
                    ch(v.tensor_tensor_scan(run[:].rearrange("p e t -> p (e t)"), one[:], tot[:].rearrange("p e t -> p (e t)"),
                                            0.0, ALU.mult, ALU.add))
                    ch(tt(exc[:], run[:], tot[:], ALU.subtract))
                    ch(tt(cnt[:], run[:, :, B - 1], exc[:, :, 0], ALU.subtract))
                    ch(tt(cmp[:], cnt[:].unsqueeze(2).broadcast_to([P, E, B]),
                          cf[:, CF_THR:CF_THR + E * B].rearrange("p (e t) -> p e t", e=E), ALU.is_gt))
                    ch(v.tensor_reduce(nte[:], cmp[:], AX.X, ALU.add))
                    ch(v.tensor_tensor_scan(end[:], one[:, 0:E], nte[:], 0.0, ALU.mult, ALU.add))
                    ch(tt(off[:], end[:], nte[:], ALU.subtract))
                    ch(v.scalar_tensor_tensor(off[:], off[:], float(P), exc[:, :, 0], ALU.mult, ALU.subtract))
                    ch(tt(pre[:], pre[:], exc[:], ALU.add))
                    ch(tt(pre[:], pre[:], off[:].unsqueeze(2).broadcast_to([P, E, B]), ALU.add))
                    for k in range(2):
                        ch(tt(oh[k][:], oh[k][:], pre[:], ALU.mult))
                        ch(v.tensor_reduce(slf[:, :, k], oh[k][:].rearrange("p e t -> p t e"), AX.X, ALU.add))
                    ch(v.tensor_copy(slot[:], slf[:]))
                    ch(ts(hi[:], slot[:], 7, None, ALU.arith_shift_right))
                    ch(ts(lo[:], slot[:], P - 1, None, ALU.bitwise_and))
                    ch(v.tensor_copy(hif[:], hi[:]))
                    ch(v.tensor_copy(lof[:], lo[:]))
                    jb = cf[:, CF_J:CF_J + NT]
                    ch(tt(cmpj[:], end[:].unsqueeze(1).broadcast_to([P, NT, E]), jb.unsqueeze(2).broadcast_to([P, NT, E]), ALU.is_le))
                    ch(v.tensor_reduce(tef[:], cmpj[:], AX.X, ALU.add))
                    ch(ts(tef[:], tef[:], float(E - 1), None, ALU.min))
                    ch(v.tensor_copy(texp[:], tef[:]))
                    lf = lof[:].rearrange("p t k -> p (t k)")
                    hf = hif[:].rearrange("p t k -> p (t k)")
                    for part in range(TOPK * B // H):
                        ms = slice(part * H, (part + 1) * H)
                        wait(v, s_inv, part)
                        ch(tt(ohlo[:], lf[:, ms].unsqueeze(2).broadcast_to([P, H, P]),
                              cf[:, CF_IOTA:CF_IOTA + P].unsqueeze(1).broadcast_to([P, H, P]), ALU.is_equal))
                        ch(tt(ohhi[:], hf[:, ms].unsqueeze(2).broadcast_to([P, H, NT]), jb.unsqueeze(1).broadcast_to([P, H, NT]), ALU.is_equal))
                        ch(tt(rhs[:, :, 0, :], ohhi[:], cb[:, CB_T + part * H:CB_T + (part + 1) * H].unsqueeze(2).broadcast_to([P, H, NT]), ALU.mult))
                        ts(rhs[:, :, 1, :], ohhi[:], cf[:, CF_P:CF_P + 1], None, ALU.mult).then_inc(s_rhs, 1)
                        v.wait_ge(s_rhs, part + 1)
                    v.wait_ge(s_inv, TOPK * B // H)
                    ch(ts(srcf[:], pi[:, 0:NT], float(P), None, ALU.mult))
                    ch(tt(srcf[:], srcf[:], pi[:, NT:2 * NT], ALU.add))
                    ch(v.tensor_copy(src[:], srcf[:]))
                    ch.end()

    route(0)

    def experts(l, hidden, w_out, fn, bofs, loads=()):
        L = len(hidden)
        with ExitStack() as st:
            ix = sb(st, f"ix_f{l}", [P, 2], I32)
            xg = sb(st, f"xg_f{l}", [P, 2, P])
            act_in = [sb(st, f"in{n}_f{l}", [P, 2, (F if n else P)]) for n in range(L + 1)]
            mats = hidden + [(w_out, FC)]
            cols = [F] * L + [P]
            wb = [sb(st, f"w{n}_f{l}", [P, 2, c * cols[n]]) for n, (_, c) in enumerate(mats)]
            bb = [sb(st, f"b{n}_f{l}", [P, 2, cols[n]], BF16) for n in range(L + 1)]
            y = sb(st, f"y_f{l}", [P, 2, P])
            ptr = ps(st, f"pt_f{l}")
            pmm = [ps(st, f"pm{n}_f{l}") for n in range(L + 1)]
            s_g = [sem(st, f"gathered{k}_f{l}") for k in range(2)]
            s_o = [sem(st, f"stored{k}_f{l}") for k in range(2)]
            s_ix, s_t = sem(st, f"index_ready_f{l}"), sem(st, f"turned_f{l}")
            s_ld = sem(st, f"loaded_f{l}") if loads else None
            s_in = [sem(st, f"input_ready{n}_f{l}") for n in range(L + 1)]
            s_w = [sem(st, f"weights_ready{n}_f{l}") for n in range(L + 1)]
            s_m = [sem(st, f"product{n}_f{l}") for n in range(L + 1)]
            s_y = sem(st, f"result_ready_f{l}")
            with nc.Block() as block:
                @block.gpsimd
                def _(g):
                    def gather(i, k, h):
                        wait_apart(g, s_t, i - 1, gfence)
                        g.tensor_copy(ix[:, k:k + 1], src[:, bass.ds(i, 1)]).then_inc(s_ix, 1)
                        wait_apart(g, s_ix, i + 1, gfence)
                        g.indirect_dma_start(xg[:, k, :], None, xn_d[l], bass.IndirectOffsetOnAxis(ix[:, k:k + 1], axis=0)).then_inc(s_g[k], 16)
                    skewed(g, NT, [(L + 2, gather)])

                @block.tensor
                def _(pe):
                    mm = nc.tensor.matmul

                    def turn(i, k, h):
                        pe.wait_ge(s_g[k], 16 * (h + 1))
                        wait(pe, s_in[0], i)
                        nc.tensor.transpose(ptr[:, 0:P], xg[:, k, :], ident).then_inc(s_t, 1)

                    def layer(n):
                        chunks = hidden[n][1]

                        def stage(i, k, h):
                            pe.wait_ge(s_in[n], i + 1)
                            pe.wait_ge(s_w[n], i + 1)
                            wait(pe, s_in[n + 1], i)
                            for f in range(FC):
                                to = pmm[n][:, f * P:(f + 1) * P]
                                mm(to, bb[n][:, k, f * P:(f + 1) * P], cb[:, CB_ONE:CB_ONE + P], start=True, stop=False)
                                for c in range(chunks):
                                    last = mm(to, wb[n][:, k, c * F + f * P:c * F + (f + 1) * P], act_in[n][:, k, c * P:(c + 1) * P],
                                              start=False, stop=c == chunks - 1)
                            last.then_inc(s_m[n], 1)
                        return stage

                    def output(i, k, h):
                        pe.wait_ge(s_in[L], i + 1)
                        pe.wait_ge(s_w[L], i + 1)
                        wait(pe, s_y, i)
                        mm(pmm[L][:, 0:P], cb[:, CB_ONE:CB_ONE + P], bb[L][:, k, :], start=True, stop=False)
                        for c in range(FC):
                            last = mm(pmm[L][:, 0:P], act_in[L][:, k, c * P:(c + 1) * P],
                                      wb[L][:, k, c * P:(c + 1) * P], start=False, stop=c == FC - 1)
                        last.then_inc(s_m[L], 1)
                    skewed(pe, NT, [(L + 1, turn)] + [(L - n, layer(n)) for n in range(L)] + [(0, output)], unroll=4)

                @block.scalar
                def _(act):
                    def activate(n):
                        def stage(i, k, h):
                            act.wait_ge(s_m[n], i + 1)
                            wait(act, s_m[n + 1], i - 1)
                            nc.scalar.activation(act_in[n + 1][:, k, :], pmm[n][:], fn).then_inc(s_in[n + 1], 1)
                        return stage
                    skewed(act, NT, [(L - n, activate(n)) for n in range(L)])

                @block.vector
                def _(v):
                    def inputs(i, k, h):
                        v.wait_ge(s_t, i + 1)
                        wait(v, s_m[0], i - 1)
                        nc.vector.tensor_copy(act_in[0][:, k, :], ptr[:, 0:P]).then_inc(s_in[0], 1)

                    def weights(n):
                        w, chunks = mats[n]

                        def stage(i, k, h):
                            e = v.value_load(texp[0:1, bass.ds(i, 1)], min_val=0, max_val=E - 1)
                            wait(v, s_m[n], i - 1)
                            frm = w[:, bass.ds(e, 1)].rearrange("p a c f -> p (a c f)" if chunks > 1 else "p a f -> p (a f)")
                            v.tensor_copy(wb[n][:, k, :], frm)
                            v.tensor_copy(bb[n][:, k, :], brow[:, bass.ds(e * cols[n] + bofs[n], cols[n])]).then_inc(s_w[n], 1)
                        return stage

                    def result(i, k, h):
                        v.wait_ge(s_m[L], i + 1)
                        wait(v, s_o[k], 16 * h)
                        nc.vector.tensor_copy(y[:, k, :], pmm[L][:, 0:P]).then_inc(s_y, 1)
                    skewed(v, NT, [(L + 1, inputs)] + [(L - n + 1, weights(n)) for n in range(L + 1)] + [(0, result)], unroll=4)

                @block.sync
                def _(sp):
                    for to, frm in loads:
                        sp.dma_start(to, frm).then_inc(s_ld, 16)

                    def store(i, k, h):
                        sp.wait_ge(s_y, i + 1)
                        sp.dma_start(ys_d[l][bass.ts(i, P), :], y[:, k, :]).then_inc(s_o[k], 16)
                    skewed(sp, NT, [(0, store)])
                    for k in range(2):
                        sp.wait_ge(s_o[k], 16 * NT // 2)
                    if loads:
                        sp.wait_ge(s_ld, 16 * len(loads))

    experts(0, [(w01, 1)], w02, ACT.Relu, BO[:2], [(w12[:, e], w12_d[e].rearrange("(c p) f -> p c f", p=P)) for e in range(E)])

    w11 = wts[:, 0:E * F].rearrange("p (e f) -> p e f", e=E)
    w13 = wts[:, E * F:2 * E * F].rearrange("p (e c d) -> p e c d", e=E, c=FC)

    def gather_pair(g, l, ix, yg, s_ix, s_g, free, free_of):
        def stage(i, k, h):
            wait_apart(g, free, free_of(i), gfence)
            for n in range(TOPK):
                g.tensor_copy(ix[n][:, k:k + 1], slot[:, bass.ds(i, 1), n]).then_inc(s_ix, 1)
            wait_apart(g, s_ix, 2 * i + 2, gfence)
            for n in range(TOPK):
                g.indirect_dma_start(yg[n][:, k, :], None, ys_d[l], bass.IndirectOffsetOnAxis(ix[n][:, k:k + 1], axis=0)).then_inc(s_g[k], 16)
        return stage

    stB = ExitStack()
    gall = sb(stB, "gall", [P, 2, B, NH1])
    mvx = sb(stB, "mvx", [P, B, 2])
    enm = sb(stB, "enm", [P, B, NH1])
    aT3 = sb(stB, "aT3", [96, B // 4, P], BF16)
    nT3 = sb(stB, "nT3", [96, B // 4, P], BF16)
    with ExitStack() as st:
        ix = [sb(st, f"ix{n}_b", [P, 2], I32) for n in range(TOPK)]
        yg = [sb(st, f"yg{n}_b", [P, 2, P]) for n in range(TOPK)]
        tmp = sb(st, "tmp_b", [P, P])
        st6 = sb(st, "st6_b", [P, 6])
        mv = sb(st, "mv_b", [P, 2, 2])
        rs = sb(st, "rs_b", [P, 2, 1])
        xn = sb(st, "xn_b", [P, 2, P])
        xT = sb(st, "xT_b", [P, 2, 2, P])
        cT_in = sb(st, "cT_in", [P, 2, P])
        s_ctx = sem(st, "ctx_copied_b")
        pT, pG = ps(st, "pT_b"), ps(st, "pG_b")
        names = ("ix_ready", "x_added", "norm_step", "var_ready", "rstd_ready", "xn_ready", "turned", "xT_ready", "gates_mm", "gates_read", "w_in")
        s = {n: sem(st, n + "_b") for n in names}
        s_g = [sem(st, f"y_in{k}_b") for k in range(2)]
        with nc.Block() as block:
            @block.sync
            def _(sp):
                sp.dma_start(w11, w11_d.rearrange("e d f -> d e f")).then_inc(s["w_in"], 16)
                for e in range(E):
                    sp.dma_start(w13[:, e], w13_d[e].rearrange("(c p) d -> p c d", p=P)).then_inc(s["w_in"], 16)
                sp.dma_start(brow[0:3, 0:BN1], bparts_d[:, BO[2]:BN]).then_inc(s["w_in"], 16)
                sp.wait_ge(s["w_in"], 16 * (E + 2))

            @block.gpsimd
            def _(g):
                def root(i, k, h):
                    g.wait_ge(s["var_ready"], i + 1)
                    g.tensor_tensor(rs[:, k, :], mv[:, k, 1:2], half[:], ALU.pow).then_inc(s["rstd_ready"], 1)
                skewed(g, B, [(2, gather_pair(g, 0, ix, yg, s["ix_ready"], s_g, s["x_added"], lambda i: i - 1)), (0, root)])

            @block.vector
            def _(v):
                def combine(i, k, h):
                    v.wait_ge(s_g[k], 32 * (h + 1))
                    xv = xs[:, bass.ds(i, 1), :].rearrange("p a d -> p (a d)")
                    wv = wt[:, bass.ds(i, 1), :].rearrange("p a n -> p (a n)")
                    ch = Chain(v, s["norm_step"], i, 3)
                    ch(v.scalar_tensor_tensor(tmp[:], yg[0][:, k, :], wv[:, 0:1], xv, ALU.mult, ALU.add))
                    v.scalar_tensor_tensor(xv, yg[1][:, k, :], wv[:, 1:2], tmp[:], ALU.mult, ALU.add).then_inc(s["x_added"], 1)
                    wait_apart(v, s["x_added"], i + 1, vfence)
                    ch(v.bn_stats(st6[:], xv), vfence)
                    wait_apart(v, s["xn_ready"], i - 1, vfence)
                    ch(v.bn_aggr(mv[:, k, :], st6[:]))
                    ch.end()
                    v.tensor_scalar(mv[:, k, 1:2], mv[:, k, 1:2], LN_EPS, None, ALU.add).then_inc(s["var_ready"], 1)

                def normed(i, k, h):
                    v.wait_ge(s["rstd_ready"], i + 1)
                    wait(v, s["turned"], i - 1)
                    mo = mvx[:, bass.ds(i, 1), :].rearrange("p a n -> p (a n)")
                    v.tensor_copy(mo[:, 0:1], mv[:, k, 0:1])
                    v.tensor_copy(mo[:, 1:2], rs[:, k, :])
                    v.tensor_scalar(xn[:, k, :], xs[:, bass.ds(i, 1), :].rearrange("p a d -> p (a d)"), mv[:, k, 0:1], rs[:, k, :],
                                    ALU.subtract, ALU.mult).then_inc(s["xn_ready"], 1)

                def turned(i, k, h):
                    v.wait_ge(s["turned"], i + 1)
                    wait(v, s["gates_mm"], i - 1)
                    v.tensor_copy(xT[:, k].rearrange("p a s -> p (a s)"), pT[:, 0:2 * P]).then_inc(s["xT_ready"], 1)

                def gates(i, k, h):
                    v.wait_ge(s["gates_mm"], i + 1)
                    v.tensor_copy(gall[:, :, bass.ds(i, 1), :].rearrange("p n a h -> p n (a h)"),
                                  pG[:, 0:2 * NH1].rearrange("p (n h) -> p n h", n=2)).then_inc(s["gates_read"], 1)
                skewed(v, B, [(0, combine), (-1, normed), (-2, turned), (-3, gates)])

            @block.tensor
            def _(pe):
                def turn(i, k, h):
                    pe.wait_ge(s["xn_ready"], i + 1)
                    pe.wait_ge(s_ctx, i + 1)
                    wait(pe, s["xT_ready"], i)
                    nc.tensor.transpose(pT[:, 0:P], xn[:, k, :], ident)
                    nc.tensor.transpose(pT[:, P:2 * P], cT_in[:, k, :], ident).then_inc(s["turned"], 1)

                def gate(i, k, h):
                    pe.wait_ge(s["xT_ready"], i + 1)
                    wait(pe, s["gates_read"], i)
                    for r in range(3):
                        last = nc.tensor.matmul(pG[:, 0:2 * NH1], xT[:, k, min(r, 1), :], wgate[:, r, :], start=r == 0, stop=r == 2)
                    last.then_inc(s["gates_mm"], 1)
                skewed(pe, B, [(-1, turn), (-2, gate)])

            @block.scalar
            def _(act):
                def context(i, k, h):
                    wait(act, s["turned"], i - 1)
                    nc.scalar.activation(cT_in[:, k, :], cx[:, bass.ds(i, 1), :].rearrange("p a d -> p (a d)"), ACT.Copy).then_inc(s_ctx, 1)
                skewed(act, B, [(0, context)])

    with ExitStack() as st:
        def t(name, shape=(P, B * NH1), dt=F32):
            return sb(st, name + "_g", list(shape), dt)
        ig, fg, ab, l1, mn, lf, cs, a, ac, nac, mm_ = [t(n) for n in ("ig", "fg", "ab", "l1", "mn", "lf", "cs", "a", "ac", "nac", "mm")]
        AT = t("AT", (P, 2, P))
        one = t("one", (P, P))
        res = t("res")
        parts = t("parts", (P, B // 4, 3, 4 * NH1), BF16)
        nparts = t("nparts", (P, B // 4, 3, 4 * NH1), BF16)
        pcs, paT, pAc = ps(st, "pcs"), ps(st, "paT"), ps(st, "pAc")
        p3 = [ps(st, f"p3{n}", (P, 1024), BF16) for n in range(2)]
        names = ("step", "abs_ready", "exp_done", "lf_ready", "pe_done", "a_ready", "AT_ready", "m_ready", "parts_ready")
        s = {n: sem(st, n + "_g") for n in names}
        with nc.Block() as block:
            @block.scalar
            def _(act):
                act.wait_ge(s["abs_ready"], 1)
                nc.scalar.activation(l1[:], ab[:], ACT.Exp, scale=-1.0).then_inc(s["exp_done"], 1)
                act.wait_ge(s["exp_done"], 1)
                nc.scalar.activation(l1[:], l1[:], ACT.Ln, bias=1.0).then_inc(s["exp_done"], 1)
                act.wait_ge(s["m_ready"], 1)
                nc.scalar.activation(enm[:].rearrange("p b h -> p (b h)"), mm_[:], ACT.Exp, scale=-1.0).then_inc(s["exp_done"], 1)

            @block.vector
            def _(v):
                ch = Chain(v, s["step"], 0, None)
                tt = v.tensor_tensor
                bh = lambda x: x[:].rearrange("p (b h) -> p b h", b=B)
                bb = lambda n: gbias[:, n, :].unsqueeze(1).broadcast_to([P, B, NH1])
                ch(tt(bh(fg), gall[:, 1], bb(1), ALU.add))
                v.scalar_tensor_tensor(ab[:], fg[:], -1.0, fg[:], ALU.mult, ALU.max).then_inc(s["abs_ready"], 1)
                ch(tt(bh(ig), gall[:, 0], bb(0), ALU.add))
                ch(v.tensor_scalar(mn[:], fg[:], 0.0, None, ALU.min))
                ch(v.memset(one[:], 1.0))
                v.wait_ge(s["exp_done"], 2)
                tt(lf[:], mn[:], l1[:], ALU.subtract).then_inc(s["lf_ready"], 1)
                v.wait_ge(s["pe_done"], 1)
                ch(v.tensor_copy(cs[:], pcs[:, 0:B * NH1]))
                tt(a[:], ig[:], cs[:], ALU.subtract).then_inc(s["a_ready"], 1)
                v.wait_ge(s["pe_done"], 2)
                for n in range(2):
                    v.tensor_tensor_scan(AT[:, n, :], one[:], paT[:, n * P:(n + 1) * P], -3e38, ALU.mult, ALU.max).then_inc(s["AT_ready"], 1)
                v.wait_ge(s["pe_done"], 3)
                ch(v.tensor_copy(ac[:], pAc[:, 0:B * NH1]))
                tt(mm_[:], cs[:], ac[:], ALU.add).then_inc(s["m_ready"], 1)
                ch(v.tensor_scalar(nac[:], ac[:], -1.0, None, ALU.mult))
                for x, to in ((a, parts), (nac, nparts)):
                    g4 = lambda y: y[:].rearrange("p (g c) -> p g c", c=4 * NH1)
                    ch(v.tensor_copy(to[:, :, 0, :], g4(x)))
                    ch(tt(g4(res), g4(x), to[:, :, 0, :], ALU.subtract))
                    ch(v.tensor_copy(to[:, :, 1, :], g4(res)))
                    ch(tt(g4(res), g4(res), to[:, :, 1, :], ALU.subtract))
                    v.tensor_copy(to[:, :, 2, :], g4(res)).then_inc(s["parts_ready"], 1)
                    v.wait_ge(s["parts_ready"], 1 if to is parts else 2)
                for n, to in enumerate((aT3, nT3)):
                    v.wait_ge(s["pe_done"], n + 4)
                    ch(v.tensor_copy(to[:].rearrange("p g s -> p (g s)"), p3[n][0:96, :]))

            @block.tensor
            def _(pe):
                pe.wait_ge(s["lf_ready"], 1)
                nc.tensor.matmul(pcs[:, 0:B * NH1], cf[:, CF_UPI:CF_UPI + P], lf[:], start=True, stop=True).then_inc(s["pe_done"], 1)
                pe.wait_ge(s["a_ready"], 1)
                nc.tensor.transpose(paT[:, 0:P], a[:, 0:P], ident)
                nc.tensor.transpose(paT[:, P:2 * P], a[:, P:2 * P], ident).then_inc(s["pe_done"], 1)
                pe.wait_ge(s["AT_ready"], 2)
                nc.tensor.transpose(pAc[:, 0:P], AT[:, 0, :], ident)
                nc.tensor.transpose(pAc[:, P:2 * P], AT[:, 1, :], ident).then_inc(s["pe_done"], 1)
                pe.wait_ge(s["parts_ready"], 2)
                for n, x in enumerate((parts, nparts)):
                    for g in range(B // 4):
                        last = nc.tensor.transpose(p3[n][0:96, g * P:(g + 1) * P], x[:, g].rearrange("p t c -> p (t c)"), identb)
                    last.then_inc(s["pe_done"], 1)

    QR = 6 * DH1
    with ExitStack() as st:
        qn, qr, kr = sb(st, "qn_c", [P, P]), sb(st, "qr_c", [P, P]), sb(st, "kr_c", [P, P])
        qx = sb(st, "qx_c", [P, 2, NH1, QR], BF16)
        kx = sb(st, "kx_c", [P, 2, NH1, QR], BF16)
        vx = sb(st, "vx_c", [P, 2, NH1, 32])
        qT = sb(st, "qT_c", [QR, 2, NH1, P], BF16)
        kT = sb(st, "kT_c", [QR, 2, NH1, P], BF16)
        D = sb(st, "D_c", [P, 2, 2, 4 * P])
        C = sb(st, "C_c", [P, 2, 2, 4 * P])
        ao = sb(st, "ao_c", [P, 2, 2 * P])
        den = sb(st, "den_c", [P, NH1])
        hh = sb(st, "hh_c", [P, 2, NH1, DH1])
        hn = sb(st, "hn_c", [P, P])
        st6, st6b = sb(st, "st6_c", [P, 6]), sb(st, "st6b_c", [P, 6])
        mv, mvb = sb(st, "mv_c", [P, 2, 2]), sb(st, "mvb_c", [P, 2, 2])
        rs, rsb = sb(st, "rs_c", [P, 2, 1]), sb(st, "rsb_c", [P, 2, 1])
        pd = [ps(st, f"pd{r}") for r in range(2)]
        pq = [ps(st, f"pq{r}") for r in range(2)]
        pqk, po, pv = ps(st, "pqk_c", (P, NH1 * P), BF16), ps(st, "po_c"), ps(st, "pv_c")
        o = router_pe_dve(st, 1)
        names = ("init", "kx_ready", "vx_ready", "qx_ready", "qk_t", "qk_ready", "d_done", "D_ready", "s_done", "C_ready",
                 "h_done", "ao_ready", "out_t", "h_read", "pool_step", "q_step", "h_step", "var1", "rstd1", "var2", "rstd2", "x_step")
        s = {n: sem(st, n + "_c") for n in names}
        with nc.Block() as block:
            @block.sync
            def _(sp):
                skewed(sp, B, [(-4, sp_xn(sp, o, 1))])
                for k in range(2):
                    sp.wait_ge(o["stored"][k], 16 * B // 2)

            @block.gpsimd
            def _(g):
                g.memset(vx[:, :, :, DH1 + 1:], 0.0)
                g.memset(vx[:, :, :, DH1:DH1 + 1], 1.0).then_inc(s["init"], 1)
                g.wait_ge(s["init"], 1)
                c = lambda i: cx[:, bass.ds(i, 1), :].rearrange("p a (h d) -> p (a h) d", d=DH1)

                def keys(i, k, h):
                    wait_apart(g, s["qk_t"], 2 * i - 2, gfence)
                    r = kr[:].rearrange("p (h d) -> p h d", d=DH1)
                    ch = Chain(g, s["pool_step"], i, 4)
                    ch(g.tensor_copy(kx[:, k, :, 0:DH1], c(i)), gfence)
                    ch(g.tensor_tensor(r, c(i), kx[:, k, :, 0:DH1], ALU.subtract), gfence)
                    ch(g.tensor_copy(kx[:, k, :, DH1:2 * DH1], r))
                    ch(g.tensor_tensor(kx[:, k, :, 2 * DH1:3 * DH1], r, kx[:, k, :, DH1:2 * DH1], ALU.subtract), gfence)
                    ch.end()
                    g.tensor_copy(kx[:, k, :, 3 * DH1:5 * DH1], kx[:, k, :, 0:2 * DH1])
                    g.tensor_copy(kx[:, k, :, 5 * DH1:], kx[:, k, :, 0:DH1]).then_inc(s["kx_ready"], 1)

                def values(i, k, h):
                    wait_apart(g, s["h_done"], i - 1, gfence)
                    g.tensor_copy(vx[:, k, :, 0:DH1], c(i)).then_inc(s["vx_ready"], 1)

                def root1(i, k, h):
                    g.wait_ge(s["var1"], i + 1)
                    g.tensor_tensor(rs[:, k, :], mv[:, k, 1:2], half[:], ALU.pow).then_inc(s["rstd1"], 1)

                def root2(i, k, h):
                    g.wait_ge(s["var2"], i + 1)
                    g.tensor_tensor(rsb[:, k, :], mvb[:, k, 1:2], half[:], ALU.pow).then_inc(s["rstd2"], 1)
                skewed(g, B, [(2, keys), (0, values), (-3, root2), (-2, root1)])

            @block.vector
            def _(v):
                v.wait_ge(s["init"], 1)

                def query(i, k, h):
                    wait(v, s["qk_t"], 2 * i - 2)
                    mo = mvx[:, bass.ds(i, 1), :].rearrange("p a n -> p (a n)")
                    q = qn[:].rearrange("p (h d) -> p h d", d=DH1)
                    r = qr[:].rearrange("p (h d) -> p h d", d=DH1)
                    spread = lambda x, n: x.unsqueeze(2).broadcast_to([P, NH1, n, DH1])
                    ch = Chain(v, s["q_step"], i, 4)
                    yield from ch.step(v.tensor_scalar(qn[:], xs[:, bass.ds(i, 1), :].rearrange("p a d -> p (a d)"), mo[:, 0:1], mo[:, 1:2],
                                       ALU.subtract, ALU.mult))
                    yield from ch.step(v.tensor_copy(qx[:, k, :, 0:3 * DH1].rearrange("p h (n d) -> p h n d", n=3), spread(q, 3)))
                    yield from ch.step(v.tensor_tensor(r, q, qx[:, k, :, 0:DH1], ALU.subtract))
                    yield from ch.step(v.tensor_copy(qx[:, k, :, 3 * DH1:5 * DH1].rearrange("p h (n d) -> p h n d", n=2), spread(r, 2)))
                    ch.end()
                    v.tensor_tensor(qx[:, k, :, 5 * DH1:], r, qx[:, k, :, 3 * DH1:4 * DH1], ALU.subtract).then_inc(s["qx_ready"], 1)

                def products(i, k, h):
                    for r in range(2):
                        v.wait_ge(s["s_done"], 2 * i + r + 1)
                        v.wait_ge(s["D_ready"], 2 * i + r + 1)
                        if r == 0:
                            wait(v, s["h_done"], i - 1)
                        v.scalar_tensor_tensor(C[:, k, r, :], pq[r][:], float(DH1) ** -0.5, D[:, k, r, :], ALU.mult, ALU.mult).then_inc(s["C_ready"], 1)
                        yield

                def divide(i, k, h):
                    v.wait_ge(s["out_t"], i + 1)
                    ov = pv[:, 0:2 * P].rearrange("p (n d) -> p n d", d=32)
                    ch = Chain(v, s["h_step"], i, 6)
                    rt = lambda x: x.rearrange("p (t r) -> p r t", r=2)
                    sums = ov[:, :, DH1].rearrange("p (r t) -> p r t", r=2)
                    yield from ch.step(v.scalar_tensor_tensor(rt(den[:]), sums, -1.0, rt(enm[:, bass.ds(i, 1), :].rearrange("p a h -> p (a h)")), ALU.mult, ALU.max))
                    yield from ch.step(v.tensor_tensor(rt(den[:]), sums, rt(den[:]), ALU.max))
                    yield from ch.step(v.tensor_scalar(den[:], den[:], NORM_EPS, None, ALU.add))
                    yield from ch.step(v.reciprocal(den[:], den[:]))
                    v.tensor_tensor(hh[:, k].rearrange("p (t r) d -> p r t d", r=2),
                                    ov[:, :, 0:DH1].rearrange("p (r t) d -> p r t d", r=2),
                                    rt(den[:]).unsqueeze(3).broadcast_to([P, 2, 4, DH1]), ALU.mult).then_inc(s["h_read"], 1)
                    yield
                    wait_apart(v, s["h_read"], i + 1, vfence)
                    yield from ch.step(v.bn_stats(st6[:], hh[:, k].rearrange("p h d -> p (h d)")), vfence)
                    yield from ch.step(v.bn_aggr(mv[:, k, :], st6[:]))
                    ch.end()
                    v.tensor_scalar(mv[:, k, 1:2], mv[:, k, 1:2], LN_EPS, None, ALU.add).then_inc(s["var1"], 1)

                def add(i, k, h):
                    v.wait_ge(s["rstd1"], i + 1)
                    xv = xs[:, bass.ds(i, 1), :].rearrange("p a d -> p (a d)")
                    ch = Chain(v, s["x_step"], i, 5)
                    yield from ch.step(v.tensor_scalar(hn[:], hh[:, k].rearrange("p h d -> p (h d)"), mv[:, k, 0:1], rs[:, k, :], ALU.subtract, ALU.mult))
                    yield from ch.step(v.tensor_tensor(hn[:], hn[:], lnsc[:], ALU.mult))
                    yield from ch.step(v.tensor_tensor(xv, xv, hn[:], ALU.add), vfence)
                    yield from ch.step(v.bn_stats(st6b[:], xv), vfence)
                    yield from ch.step(v.bn_aggr(mvb[:, k, :], st6b[:]))
                    ch.end()
                    v.tensor_scalar(mvb[:, k, 1:2], mvb[:, k, 1:2], LN_EPS, None, ALU.add).then_inc(s["var2"], 1)

                def norm2(i, k, h):
                    v.wait_ge(s["rstd2"], i + 1)
                    wait(v, o["stored"][k], 16 * h)
                    wait(v, o["xn_t"], i - 1)
                    v.tensor_scalar(o["xn"][:, k, :], xs[:, bass.ds(i, 1), :].rearrange("p a d -> p (a d)"), mvb[:, k, 0:1],
                                    rsb[:, k, :], ALU.subtract, ALU.mult).then_inc(o["xn_ready"], 1)
                skewed(v, B, [[(0, products), (-6, dve_top(v, o)), (2, query), (-3, add), (-2, divide)], (-4, norm2)])

            @block.scalar
            def _(act):
                def operand(n, i, k):
                    act.wait_ge(s["qk_t"], 2 * i + n + 1)
                    wait(act, s["s_done"], 2 * i - 2)
                    nc.scalar.activation((qT, kT)[n][:, k].rearrange("p a b -> p (a b)"), pqk[0:QR, :], ACT.Copy).then_inc(s["qk_ready"], 1)

                def decays(i, k, h):
                    for r in range(2):
                        act.wait_ge(s["d_done"], 2 * i + r + 1)
                        if r == 0:
                            wait(act, s["C_ready"], 2 * i - 2)
                        nc.scalar.activation(D[:, k, r, :], pd[r][:], ACT.Exp).then_inc(s["D_ready"], 1)

                def weighted(i, k, h):
                    act.wait_ge(s["h_done"], i + 1)
                    wait(act, s["out_t"], i - 1)
                    nc.scalar.activation(ao[:, k, :], po[:, 0:2 * P], ACT.Copy).then_inc(s["ao_ready"], 1)
                skewed(act, B, [(0, decays), (1, lambda i, k, h: operand(0, i, k)), (-1, weighted), (1, lambda i, k, h: operand(1, i, k)),
                                (-5, act_xnT(act, o))])

            @block.tensor
            def _(pe):
                mm = nc.tensor.matmul
                h4 = lambda x: x.rearrange("p (t k) -> p t k", t=4)

                def exponents(i, k, h):
                    for r in range(2):
                        wait(pe, s["D_ready"], 2 * i + r - 1)
                        c0 = (i % 4) * NH1 + r
                        grp = i // 4
                        mm(h4(pd[r][:]), identb, cb[:, CB_TRI:CB_TRI + P].unsqueeze(1).broadcast_to([P, 4, P]), start=True, stop=True)
                        mm(h4(pd[r][:]), aT3[:, bass.ds(grp, 1), :].rearrange("p g s -> p (g s)"),
                           cb[0:96, bass.ds(CB_SEL + c0, 4, 2)].unsqueeze(2).broadcast_to([96, 4, P]), start=False, stop=True, skip_group_check=True)
                        for t in range(4):
                            last = mm(pd[r][:, t * P:(t + 1) * P], cb[0:96, bass.ds(CB_SEL + c0 + 2 * t, 1)].broadcast_to([96, P]),
                                      nT3[:, bass.ds(grp, 1), :].rearrange("p g s -> p (g s)"), start=False, stop=True, skip_group_check=True)
                        last.then_inc(s["d_done"], 1)

                def turn(n, i, k):
                    pe.wait_ge(s["qx_ready" if n == 0 else "kx_ready"], i + 1)
                    wait(pe, s["qk_ready"], 2 * i + n)
                    x = (qx, kx)[n]
                    for hd in range(NH1):
                        last = nc.tensor.transpose(pqk[0:QR, hd * P:(hd + 1) * P], x[:, k, hd, :], identb)
                    last.then_inc(s["qk_t"], 1)

                def scores(i, k, h):
                    pe.wait_ge(s["qk_ready"], 2 * i + 2)
                    for r in range(2):
                        wait(pe, s["C_ready"], 2 * i + r - 1)
                        for t in range(4):
                            last = mm(pq[r][:, t * P:(t + 1) * P], kT[:, k, 2 * t + r, :], qT[:, k, 2 * t + r, :], start=True, stop=True)
                        last.then_inc(s["s_done"], 1)

                def weigh(i, k, h):
                    pe.wait_ge(s["C_ready"], 2 * i + 2)
                    pe.wait_ge(s["vx_ready"], i + 1)
                    wait(pe, s["ao_ready"], i)
                    for r in range(2):
                        for t in range(4):
                            last = mm(po[32 * t:32 * t + 32, r * P:(r + 1) * P], vx[:, k, 2 * t + r, :], C[:, k, r, t * P:(t + 1) * P],
                                      start=True, stop=True)
                    last.then_inc(s["h_done"], 1)

                def turn_out(i, k, h):
                    pe.wait_ge(s["ao_ready"], i + 1)
                    wait(pe, s["h_read"], i)
                    for r in range(2):
                        last = nc.tensor.transpose(pv[:, r * P:(r + 1) * P], ao[:, k, r * P:(r + 1) * P], ident)
                    last.then_inc(s["out_t"], 1)
                skewed(pe, B, [(-6, pe_score(pe, o, 1)), (0, exponents), (-2, turn_out), (0, scores), (1, lambda i, k, h: turn(0, i, k)),
                               (-5, pe_xnT(pe, o)), (-1, weigh), (1, lambda i, k, h: turn(1, i, k))], unroll=4)
    stB.close()

    route(1)
    experts(1, [(w11, 1), (w12, FC)], w13, ACT.Gelu, [b - BO[2] for b in BO[2:]])

    with ExitStack() as st:
        ix = [sb(st, f"ix{n}_e", [P, 2], I32) for n in range(TOPK)]
        yg = [sb(st, f"yg{n}_e", [P, 2, P]) for n in range(TOPK)]
        tmp = sb(st, "tmp_e", [P, P])
        xo = sb(st, "xo_e", [P, 2, P])
        s_ix, s_x, s_st = sem(st, "ix_ready_e"), sem(st, "x_added_e"), sem(st, "step_e")
        s_g = [sem(st, f"y_in{k}_e") for k in range(2)]
        s_o = [sem(st, f"out_stored{k}") for k in range(2)]
        with nc.Block() as block:
            @block.gpsimd
            def _(g):
                skewed(g, B, [(2, gather_pair(g, 1, ix, yg, s_ix, s_g, s_x, lambda i: i - 1))])

            @block.vector
            def _(v):
                def combine(i, k, h):
                    v.wait_ge(s_g[k], 32 * (h + 1))
                    xv = xs[:, bass.ds(i, 1), :].rearrange("p a d -> p (a d)")
                    wv = wt[:, bass.ds(i, 1), :].rearrange("p a n -> p (a n)")
                    wait(v, s_x, i)
                    ch = Chain(v, s_st, i, 1)
                    ch(v.scalar_tensor_tensor(tmp[:], yg[0][:, k, :], wv[:, 0:1], xv, ALU.mult, ALU.add))
                    ch.end()
                    wait(v, s_o[k], 16 * h)
                    v.scalar_tensor_tensor(xo[:, k, :], yg[1][:, k, :], wv[:, 1:2], tmp[:], ALU.mult, ALU.add).then_inc(s_x, 1)
                skewed(v, B, [(0, combine)])

            @block.sync
            def _(sp):
                def store(i, k, h):
                    sp.wait_ge(s_x, i + 1)
                    sp.dma_start(out_d[bass.ds(i, 1), :, :].rearrange("a s d -> (a s) d"), xo[:, k, :]).then_inc(s_o[k], 16)
                skewed(sp, B, [(0, store)])
                for k in range(2):
                    sp.wait_ge(s_o[k], 16 * B // 2)
    return keep


INS = ['x', 'ctx_1024', 'mask_Bx1xSxS2_ik1', 'g_xattn', 'g_ffn', 'L0_ffn_Wg', 'L0_ffn_W1', 'L0_ffn_b1', 'L0_ffn_W2', 'L0_ffn_b2',
       'L1_xattn_igate_w', 'L1_xattn_igate_b', 'L1_xattn_fgate_w', 'L1_xattn_fgate_b', 'L1_xattn_ln_scale',
       'L1_ffn_expert_tokens', 'L1_ffn_W1', 'L1_ffn_b1', 'L1_ffn_W2', 'L1_ffn_b2', 'L1_ffn_W3', 'L1_ffn_b3']


def kernel(**inputs):
    import numpy as np
    import concourse.bacc as bacc
    from concourse.bass_utils import run_bass_kernel_spmd

    nc = bacc.Bacc("TRN2", target_bir_lowering=False, num_devices=1)
    arrays, args = {}, []
    cf, cb = constants()
    for name, a in [("const_f32", cf), ("const_small", cb)] + [(n, np.ascontiguousarray(inputs[n])) for n in INS]:
        arrays[f"in_{name}"] = a
        args.append(nc.dram_tensor(f"in_{name}", a.shape, mybir.dt.from_np(a.dtype), kind="ExternalInput").ap())
    args.append(nc.dram_tensor("out_0", (B, P, P), F32, kind="ExternalOutput").ap())
    build(nc, *args)
    r = run_bass_kernel_spmd(nc, [arrays], core_ids=[0])
    return r.results[0]["out_0"]
```

```python
import concourse.bass as bass
from concourse import mybir
from contextlib import ExitStack

F32 = mybir.dt.float32
F32R = mybir.dt.float32r
BF16 = mybir.dt.bfloat16
I32 = mybir.dt.int32
U32 = mybir.dt.uint32
ALU = mybir.AluOpType
ACT = mybir.ActivationFunctionType
AX = mybir.AxisListType

P = 128
B = 32
E = 8
F = 512
FC = F // P
NH0, DH0 = 16, 8
NH1, DH1 = 8, 16
TOPK = 2
NT = TOPK * B + E
LN_EPS = 1e-5
NORM_EPS = 1e-6
BIG = 1e9

CF_ID, CF_UPI, CF_IOTA, CF_P, CF_E, CF_THR, CF_J, CF_U, CF_W = 0, 128, 256, 384, 385, 641, 897, 969, 1041
CB_ID, CB_UPS, CB_ONE, CB_TRI, CB_SEL, CB_T, CB_SELM, CB_W = 0, 128, 256, 384, 512, 544, 608, 616
def constants():
    import numpy as np
    p = np.arange(P)
    cf = np.zeros((P, CF_W), np.float32)
    cf[:, CF_ID:CF_ID + P] = np.eye(P)
    cf[:, CF_UPI:CF_UPI + P] = p[:, None] <= p[None, :]
    cf[:, CF_IOTA:CF_IOTA + P] = p
    cf[:, CF_P] = p
    cf[:, CF_E:CF_E + E * B] = np.repeat(np.arange(E), B)
    cf[:, CF_THR:CF_THR + E * B] = np.tile(np.arange(B) * P, E)
    cf[:, CF_J:CF_J + NT] = np.arange(NT)
    cf[:, CF_U:CF_U + NT] = (np.arange(NT) - (NT - 1)) * P + p[:, None]
    cb = np.zeros((P, CB_W), np.float32)
    cb[:, CB_ID:CB_ID + P] = np.eye(P)
    cb[:, CB_UPS:CB_UPS + P] = p[:, None] < p[None, :]
    cb[:, CB_ONE:CB_ONE + P] = 1
    cb[:, CB_TRI:CB_TRI + P] = np.where(p[:, None] <= p[None, :], 0, -1e30)
    cb[:, CB_SEL:CB_SEL + 32] = (p[:, None] % 32 == np.arange(32)) & (p[:, None] < 96)
    cb[:, CB_T:CB_T + TOPK * B] = np.arange(TOPK * B) + 1
    cb[:, CB_SELM:CB_SELM + 8] = -((p[:, None] % 8 == np.arange(8)) & (p[:, None] % 64 < 24)).astype(np.float32)
    return cf, cb


def wait(eng, sem, value):
    if not isinstance(value, int) or value > 0:
        eng.wait_ge(sem, value)


def wait_apart(eng, sem, value, fence):
    if not isinstance(value, int) or value > 0:
        eng.wait_ge(sem, value)
        fence(eng)


class Chain:

    def __init__(self, eng, sem, i, per):
        self.eng, self.sem, self.base, self.per, self.n = eng, sem, i * (per or 0), per, 0

    def __call__(self, ins, fence=None):
        self.n += 1
        ins.then_inc(self.sem, 1)
        if fence is None:
            self.eng.wait_ge(self.sem, self.base + self.n)
        else:
            wait_apart(self.eng, self.sem, self.base + self.n, fence)

    def step(self, ins, fence=None):
        self.n += 1
        ins.then_inc(self.sem, 1)
        yield
        if fence is None:
            self.eng.wait_ge(self.sem, self.base + self.n)
        else:
            wait_apart(self.eng, self.sem, self.base + self.n, fence)

    def end(self):
        assert self.per in (None, self.n), (self.n, self.per)


def woven(stages):
    while stages:
        stages = [st for st in stages if next(st, stages) is not stages]


def skewed(eng, n, stages, unroll=2, slots=2):
    groups = [st if isinstance(st, list) else [st] for st in stages]
    leads = [lead for group in groups for lead, _ in group]

    def issue(group, tile):
        issued = [stage(*tile(lead)) for lead, stage in group if tile(lead)]
        woven([st for st in issued if st is not None])

    def step(j):
        for group in groups:
            issue(group, lambda lead: (j + lead, (j + lead) % slots, (j + lead) // 2) if 0 <= j + lead < n else None)

    first = 2 + max(0, -min(leads))
    first += -first % unroll
    last = n - max(0, max(leads))
    last -= (last - first) % unroll
    for j in range(-max(leads), first):
        step(j)
    with eng.Fori(first // unroll, last // unroll) as jj:
        for k in range(unroll):
            for group in groups:
                issue(group, lambda lead: (unroll * jj + k + lead, (k + lead) % slots, (unroll // 2) * jj + (k + lead) // 2))
    for j in range(last, n - min(leads)):
        step(j)


def build(nc, cf_d, cb_d, x_d, ctx_d, mask_d, gx_d, gf_d, wg0_d, w01_d, b01_d, w02_d, b02_d, igw_d,
          igb_d, fgw_d, fgb_d, lns_d, tok_d, w11_d, b11_d, w12_d, b12_d, w13_d, b13_d, out_d):
    def dram(name, shape, dt=F32):
        return nc.dram_tensor(name, shape, dt).ap()

    xn_d = [dram("normed0", (B * P, P)), dram("normed1", (B * P, P))]
    y_d = [dram(f"results{l}", ((NT + TOPK * B) * P, P)) for l in range(2)]

    keep = ExitStack()

    def sb(stack, name, shape, dt=F32):
        return stack.enter_context(nc.sbuf_tensor(name, shape, dt))

    def ps(stack, name, shape=(P, 512), dt=F32):
        return stack.enter_context(nc.psum_tensor(name, list(shape), dt))

    def sem(stack, name):
        return stack.enter_context(nc.semaphore(name))

    cf = sb(keep, "cf", [P, CF_W])
    cb = sb(keep, "cb", [P, CB_W], BF16)
    xs = sb(keep, "xs", [P, B, P])
    cx = sb(keep, "cx", [P, B, P])
    wts = sb(keep, "wts", [P, 2 * E * F + E * FC * F])
    bT = sb(keep, "bT", [P, 3 * E * FC])
    bout = [sb(keep, "bout0", [P, E * P]), sb(keep, "bout1", [P, E * P])]
    gts = sb(keep, "gts", [P, 4])
    half = sb(keep, "half", [P, 1])
    none = sb(keep, "none", [P, 1], I32)
    wr = [sb(keep, "wr0", [P, E]), sb(keep, "wr1", [P, E])]
    wgate = sb(keep, "wgate", [P, 3, 2 * NH1])
    gbias = sb(keep, "gbias", [P, 2, NH1])
    lnsc = sb(keep, "lnsc", [P, P])
    topv = sb(keep, "topv", [P, B, 2])
    topi = sb(keep, "topi", [P, B, 2])
    wt = sb(keep, "wt", [P, B, 2])
    dst = sb(keep, "dst", [P, NT], I32)
    src = sb(keep, "src", [P, NT], I32)
    texp = sb(keep, "texp", [P, NT], I32)

    junk = [sb(keep, "junk_v", [P, 32]), sb(keep, "junk_g", [P, 32])]
    fences = [0, 0]

    def vfence(v):
        fences[0] = (fences[0] + 1) % 32
        v.memset(junk[0][:, fences[0]:fences[0] + 1], 0.0)

    def gfence(g):
        fences[1] = (fences[1] + 1) % 32
        g.tensor_tensor(junk[1][:, fences[1]:fences[1] + 1], half[:], half[:], ALU.mult)

    ident = cf[:, CF_ID:CF_ID + P]
    identb = cb[:, CB_ID:CB_ID + P]
    identb4 = identb.unsqueeze(1).broadcast_to([P, 4, P])
    w01 = wts[:, 0:E * F].rearrange("p (e f) -> p e f", e=E)
    w02 = wts[:, E * F:2 * E * F].rearrange("p (e c d) -> p e c d", e=E, c=FC)
    w12 = wts[:, 2 * E * F:].rearrange("p (e c f) -> p e c f", e=E, c=FC)

    s_w, s_small = sem(keep, "weights_in"), sem(keep, "small_in")
    with ExitStack() as st:
        cbf = sb(st, "cbf", [P, CB_W])
        braw = sb(st, "braw", [3 * E * FC, P])
        pb = ps(st, "pb")
        s_c, s_gt, s_b = [sem(st, n) for n in ("const_in", "gates_in", "bias_in")]
        s_bt, s_t = sem(st, "bias_turned"), sem(st, "tanh_done")
        with nc.Block() as block:
            @block.sync
            def _(sp):
                sp.dma_start(cf[:], cf_d).then_inc(s_c, 16)
                sp.dma_start(cbf[:], cb_d).then_inc(s_c, 16)
                for n, bd in enumerate((b01_d, b11_d, b12_d)):
                    sp.dma_start(braw[n * E * FC:(n + 1) * E * FC, :], bd.rearrange("e (c p) -> (e c) p", p=P)).then_inc(s_b, 16)
                for to, row, arrived in ((gts[:, 0:2], gx_d, s_gt), (gts[:, 2:4], gf_d, s_gt), (lnsc[:], lns_d, s_gt),
                                         (gbias[:, 0, :], igb_d, s_small), (gbias[:, 1, :], fgb_d, s_small)):
                    sp.dma_start(to, row.rearrange("(a n) -> a n", a=1).broadcast_to([P, row.shape[0]])).then_inc(arrived, 16)
                sp.dma_start(wr[0][:], wg0_d).then_inc(s_gt, 16)
                for to, bd in zip(bout, (b02_d, b13_d)):
                    sp.dma_start(to[:], bd.rearrange("e d -> (e d)").rearrange("(a n) -> a n", a=1).broadcast_to([P, E * P])).then_inc(s_w, 16)

            @block.scalar
            def _(act):
                with nc.allow_non_contiguous_dma(reason="small weights, transposed on the way in"):
                    act.dma_start(wr[1][:], tok_d.rearrange("e d -> d e")).then_inc(s_small, 16)
                    for r in range(3):
                        act.dma_start(wgate[:, r, 0:NH1], igw_d[:, r * P:(r + 1) * P].rearrange("h d -> d h")).then_inc(s_small, 16)
                        act.dma_start(wgate[:, r, NH1:], fgw_d[:, r * P:(r + 1) * P].rearrange("h d -> d h")).then_inc(s_small, 16)
                act.wait_ge(s_gt, 4 * 16)
                nc.scalar.activation(gts[:], gts[:], ACT.Tanh).then_inc(s_t, 1)

            @block.gpsimd
            def _(g):
                g.memset(half[:], -0.5)
                g.memset(none[:], 0)

            @block.tensor
            def _(pe):
                pe.wait_ge(s_c, 32)
                pe.wait_ge(s_b, 3 * 16)
                nc.tensor.transpose(pb[:, 0:3 * E * FC], braw[:], ident[0:3 * E * FC, 0:3 * E * FC]).then_inc(s_bt, 1)

            @block.vector
            def _(v):
                v.wait_ge(s_c, 32)
                v.tensor_copy(cb[:], cbf[:])
                v.wait_ge(s_bt, 1)
                v.tensor_copy(bT[:], pb[:, 0:3 * E * FC])
                v.wait_ge(s_t, 1)
                v.tensor_scalar(lnsc[:], lnsc[:], gts[:, 1:2], None, ALU.mult)

    def router_buffers(st, l):
        o = {}
        o["xn"] = sb(st, f"xn{l}", [P, 2, P])
        o["xnT"] = sb(st, f"xnT{l}", [P, 2, P])
        o["sc"] = sb(st, f"sc{l}", [P, E])
        o["mx8"] = sb(st, f"mx8{l}", [P, 8])
        o["ix8"] = sb(st, f"ix8{l}", [P, 8], U32)
        o["ps"] = ps(st, f"psR{l}")
        for n in ("xn_ready", "xn_t", "xnT_ready", "score_mm", "score_read", "rt_step"):
            o[n] = sem(st, n + str(l))
        o["stored"] = [sem(st, f"xn_stored{l}{k}") for k in range(2)]
        return o

    def pe_xnT(pe, o):
        def stage(i, k, h):
            pe.wait_ge(o["xn_ready"], i + 1)
            wait(pe, o["score_read"], i)
            nc.tensor.transpose(o["ps"][:, 0:P], o["xn"][:, k % 2, :], ident).then_inc(o["xn_t"], 1)
        return stage

    def pe_score(pe, o, l):
        def stage(i, k, h):
            pe.wait_ge(o["xnT_ready"], i + 1)
            nc.tensor.matmul(o["ps"][:, P:P + E], o["xnT"][:, k % 2, :], wr[l][:], start=True, stop=True).then_inc(o["score_mm"], 1)
        return stage

    def act_xnT(act, o):
        def stage(i, k, h):
            act.wait_ge(o["xn_t"], i + 1)
            nc.scalar.activation(o["xnT"][:, k % 2, :], o["ps"][:, 0:P], ACT.Copy).then_inc(o["xnT_ready"], 1)
        return stage

    def dve_top(v, o):
        def stage(i, k, h):
            v.wait_ge(o["score_mm"], i + 1)
            v.tensor_copy(o["sc"][:], o["ps"][:, P:P + E]).then_inc(o["score_read"], 1)
            yield
            wait_apart(v, o["score_read"], i + 1, vfence)
            ch = Chain(v, o["rt_step"], i, 4)
            yield from ch.step(v.max(o["mx8"][:], o["sc"][:]), vfence)
            yield from ch.step(v.max_index(o["ix8"][:], o["mx8"][:], o["sc"][:]))
            yield from ch.step(v.tensor_copy(topv[:, bass.ds(i, 1), :].rearrange("p a c -> p (a c)"), o["mx8"][:, 0:2]))
            yield from ch.step(v.tensor_copy(topi[:, bass.ds(i, 1), :].rearrange("p a c -> p (a c)"), o["ix8"][:, 0:2]))
            ch.end()
        return stage

    def sp_xn(sp, o, l):
        def stage(i, k, h):
            sp.wait_ge(o["xn_ready"], i + 1)
            sp.dma_start(xn_d[l][bass.ts(i, P), :], o["xn"][:, k, :]).then_inc(o["stored"][k], 16)
        return stage

    HR = 64

    def head_of(g, t):
        return 2 * (4 * (g // 2) + t) + g % 2

    with ExitStack() as st:
        free_at = [2 * E * F]

        def scratch(words):
            free_at[0] += words
            return wts[:, free_at[0] - words:free_at[0]]
        mk = sb(st, "mk", [P, 2, P], I32)
        nz = sb(st, "nz", [P, 2, P])
        anyk = sb(st, "anyk", [P, 2, 2])
        mb = scratch(B * P // 2).bitcast(BF16).rearrange("p (b k) -> p b k", b=B)
        st6 = sb(st, "st6", [P, 6])
        mv = sb(st, "mv", [P, 2, 2])
        rs = sb(st, "rs", [P, 2, 1])
        qn = sb(st, "qn", [P, P])
        qr = sb(st, "qr", [P, P])
        kr = sb(st, "kr", [P, P])
        qx = sb(st, "qx", [P, 2, NH0, HR], BF16)
        kx = sb(st, "kx", [P, 2, NH0, HR], BF16)
        vx = scratch(2 * NH0 * 32).rearrange("p (k h d) -> p k h d", k=2, h=NH0)
        qT = sb(st, "qT", [P, 4, 8, P], BF16)
        kT = sb(st, "kT", [P, 4, 8, P], BF16)
        pr = scratch(2 * 4 * 4 * P).rearrange("p (k g n) -> p k g n", k=2, g=4)
        mx = sb(st, "mx", [P, 2, 8])
        mr = sb(st, "mr", [P, 2, 8])
        m3 = sb(st, "m3", [P, 2, HR], BF16)
        mT = sb(st, "mT", [P, 2, P], BF16)
        ao = scratch(2 * 4 * P).rearrange("p (k n) -> p k n", k=2)
        rd = sb(st, "rd", [P, NH0])
        at = sb(st, "at", [P, NH0, DH0])
        st6b = sb(st, "st6b", [P, 6])
        mvb = sb(st, "mvb", [P, 2, 2])
        rsb = sb(st, "rsb", [P, 2, 1])
        p1 = [ps(st, f"p1{k}") for k in range(2)]
        p2 = [ps(st, f"p2{k}") for k in range(2)]
        pqk, po, pv = ps(st, "pqk", (P, 8 * P), BF16), ps(st, "po"), ps(st, "pv")
        o = router_buffers(st, 0)
        names = ("mask_bits", "mask_ready", "row_any", "bias_step", "kx_ready", "vx_ready", "var1", "rstd1", "q_step", "qx_ready",
                 "qk_t", "qk_ready", "s1_done", "max_done", "m_step", "m_ready", "m_t", "mT_ready", "s2_done", "exp_done",
                 "av_done", "ao_ready", "out_t", "o_read", "o_step", "var2", "rstd2", "pool_step", "init_done", "x_step")
        s = {n: sem(st, n + "A") for n in names}
        s_in = [sem(st, f"tile_in{k}") for k in range(2)]

        with nc.Block() as block:
            @block.sync
            def _(sp):
                def load(i, k, h):
                    wait(sp, s["mask_bits"], i - 1)
                    sp.dma_start(xs[:, bass.ds(i, 1), :], x_d[bass.ds(i, 1), :, :].rearrange("a s d -> s a d")).then_inc(s_in[k], 16)
                    sp.dma_start(cx[:, bass.ds(i, 1), :], ctx_d[bass.ds(i, 1), :, :].rearrange("a s d -> s a d")).then_inc(s_in[k], 16)
                    sp.dma_start(mk[:, k, :], mask_d[bass.ds(i, 1), :, :, :].rearrange("a b q k -> (a b q) k")).then_inc(s_in[k], 16)
                    if isinstance(i, int) and i == 4:
                        sp.dma_start(w01, w01_d.rearrange("e d f -> d e f")).then_inc(s_w, 16)
                        for e in range(E):
                            sp.dma_start(w02[:, e], w02_d[e].rearrange("(c p) d -> p c d", p=P)).then_inc(s_w, 16)
                skewed(sp, B, [(5, load), (-4, sp_xn(sp, o, 0))])
                for k in range(2):
                    sp.wait_ge(o["stored"][k], 16 * B // 2)
                sp.wait_ge(s_w, 16 * (3 + E))
                sp.wait_ge(s_small, 16 * 9)

            @block.gpsimd
            def _(g):
                g.memset(kx[:, :, :, 6 * DH0:], 0.0)
                g.memset(qx[:, :, :, 6 * DH0:], 0.0)
                g.memset(m3[:], 0.0)
                g.memset(vx[:, :, :, DH0 + 1:], 0.0)
                g.memset(vx[:, :, :, DH0:DH0 + 1], 1.0).then_inc(s["init_done"], 1)
                g.wait_ge(s["init_done"], 1)

                def keys(i, k, h):
                    wait(g, s["qk_t"], 2 * i - 2)
                    wait_apart(g, s_in[k], 48 * (h + 1), gfence)
                    c = cx[:, bass.ds(i, 1), :].rearrange("p a (h d) -> p (a h) d", d=DH0)
                    r = kr[:].rearrange("p (h d) -> p h d", d=DH0)
                    ch = Chain(g, s["pool_step"], i, 4)
                    ch(g.tensor_copy(kx[:, k, :, 0:8], c), gfence)
                    ch(g.tensor_tensor(r, c, kx[:, k, :, 0:8], ALU.subtract), gfence)
                    ch(g.tensor_copy(kx[:, k, :, 8:16], r))
                    ch(g.tensor_tensor(kx[:, k, :, 16:24], r, kx[:, k, :, 8:16], ALU.subtract), gfence)
                    ch.end()
                    g.tensor_copy(kx[:, k, :, 24:40], kx[:, k, :, 0:16])
                    g.tensor_copy(kx[:, k, :, 40:48], kx[:, k, :, 0:8]).then_inc(s["kx_ready"], 1)

                def values(i, k, h):
                    wait_apart(g, s["av_done"], i - 1, gfence)
                    g.tensor_copy(vx[:, k, :, 0:DH0],
                                  cx[:, bass.ds(i, 1), :].rearrange("p a (h d) -> p (a h) d", d=DH0)).then_inc(s["vx_ready"], 1)

                def root1(i, k, h):
                    g.wait_ge(s["var1"], i + 1)
                    g.tensor_tensor(rs[:, k, :], mv[:, k, 1:2], half[:], ALU.pow).then_inc(s["rstd1"], 1)

                def root2(i, k, h):
                    g.wait_ge(s["var2"], i + 1)
                    g.tensor_tensor(rsb[:, k, :], mvb[:, k, 1:2], half[:], ALU.pow).then_inc(s["rstd2"], 1)
                skewed(g, B, [(2, keys), (-1, values), (-4, root2), (3, root1)])

            @block.vector
            def _(v):
                v.wait_ge(s["init_done"], 1)

                def norm1(i, k, h):
                    wait(v, s["rstd1"], i - 1)
                    wait_apart(v, s_in[k], 48 * (h + 1), vfence)
                    ch = Chain(v, s["x_step"], i, 2)
                    yield from ch.step(v.bn_stats(st6[:], xs[:, bass.ds(i, 1), :].rearrange("p a d -> p (a d)")), vfence)
                    yield from ch.step(v.bn_aggr(mv[:, k, :], st6[:]))
                    ch.end()
                    v.tensor_scalar(mv[:, k, 1:2], mv[:, k, 1:2], LN_EPS, None, ALU.add).then_inc(s["var1"], 1)
                    wait(v, s["mask_ready"], i - 1)
                    v.tensor_scalar(nz[:, k, :], mk[:, k, :], 0.0, None, ALU.not_equal).then_inc(s["mask_bits"], 1)
                    yield
                    v.wait_ge(s["mask_bits"], i + 1)
                    v.reduce_max(anyk[:, k, 0:1], nz[:, k, :], AX.X).then_inc(s["row_any"], 1)
                    yield
                    v.wait_ge(s["row_any"], i + 1)
                    ch = Chain(v, s["bias_step"], i, 1)
                    yield from ch.step(v.tensor_scalar(anyk[:, k, 1:2], anyk[:, k, 0:1], BIG, None, ALU.mult))
                    ch.end()

                def query(i, k, h):
                    v.wait_ge(s["rstd1"], i + 1)
                    wait(v, s["qk_t"], 2 * i - 2)
                    v.tensor_scalar(mb[:, bass.ds(i, 1), :].rearrange("p a k -> p (a k)"), nz[:, k, :], 1.0, anyk[:, k, 1:2],
                                    ALU.subtract, ALU.mult).then_inc(s["mask_ready"], 1)
                    ch = Chain(v, s["q_step"], i, 5)
                    yield from ch.step(v.tensor_tensor(rs[:, k, :], rs[:, k, :], anyk[:, k, 0:1], ALU.mult))
                    yield from ch.step(v.tensor_scalar(qn[:], xs[:, bass.ds(i, 1), :].rearrange("p a d -> p (a d)"), mv[:, k, 0:1], rs[:, k, :],
                                       ALU.subtract, ALU.mult))
                    q = qn[:].rearrange("p (h d) -> p h d", d=DH0)
                    r = qr[:].rearrange("p (h d) -> p h d", d=DH0)
                    yield from ch.step(v.tensor_copy(qx[:, k, :, 0:24].rearrange("p h (n d) -> p h n d", n=3), q.unsqueeze(2).broadcast_to([P, NH0, 3, DH0])))
                    yield from ch.step(v.tensor_tensor(r, q, qx[:, k, :, 0:8], ALU.subtract))
                    yield from ch.step(v.tensor_copy(qx[:, k, :, 24:40].rearrange("p h (n d) -> p h n d", n=2), r.unsqueeze(2).broadcast_to([P, NH0, 2, DH0])))
                    ch.end()
                    v.tensor_tensor(qx[:, k, :, 40:48], r, qx[:, k, :, 24:32], ALU.subtract).then_inc(s["qx_ready"], 1)

                def maxima(i, k, h):
                    for g in range(4):
                        v.wait_ge(s["s1_done"], 4 * i + g + 1)
                        if g == 0:
                            wait(v, s["m_ready"], i)
                        v.reduce_max(mx[:, g % 2, 4 * (g // 2):4 * (g // 2) + 4], p1[g % 2][:].rearrange("p (t k) -> p t k", t=4), AX.X).then_inc(s["max_done"], 1)
                    yield
                    v.wait_ge(s["max_done"], 4 * i + 4)
                    wait(v, s["m_t"], i)
                    ch = Chain(v, s["m_step"], i, 3)
                    yield from ch.step(v.tensor_copy(m3[:, :, 0:8], mx[:]))
                    yield from ch.step(v.tensor_tensor(mr[:], mx[:], m3[:, :, 0:8], ALU.subtract))
                    yield from ch.step(v.tensor_copy(m3[:, :, 8:16], mr[:]))
                    ch.end()
                    v.tensor_tensor(m3[:, :, 16:24], mr[:], m3[:, :, 8:16], ALU.subtract).then_inc(s["m_ready"], 1)

                def attended(i, k, h):
                    for _ in range(3):
                        yield
                    v.wait_ge(s["out_t"], i + 1)
                    ov = pv[:].rearrange("p (n d) -> p n d", d=32)
                    ch = Chain(v, s["o_step"], i, 4)
                    yield from ch.step(v.reciprocal(rd[:], ov[:, :, DH0]))
                    for a in range(2):
                        last = v.tensor_tensor(at[:].rearrange("p (a t b) d -> p a b t d", a=2, b=2)[:, a],
                                               ov[:, 8 * a:8 * a + 8, 0:DH0].rearrange("p (b t) d -> p b t d", b=2),
                                               rd[:, 8 * a:8 * a + 8].rearrange("p (b t) -> p b t", b=2).unsqueeze(3).broadcast_to([P, 2, 4, DH0]), ALU.mult)
                    last.then_inc(s["o_read"], 1)
                    yield
                    wait(v, s["rstd2"], i - 1)
                    v.wait_ge(s["o_read"], i + 1)
                    xv = xs[:, bass.ds(i, 1), :].rearrange("p a d -> p (a d)")
                    yield from ch.step(v.scalar_tensor_tensor(xv, at[:].rearrange("p h d -> p (h d)"), gts[:, 0:1], xv, ALU.mult, ALU.add), vfence)
                    yield from ch.step(v.bn_stats(st6b[:], xv), vfence)
                    yield from ch.step(v.bn_aggr(mvb[:, k, :], st6b[:]))
                    ch.end()
                    v.tensor_scalar(mvb[:, k, 1:2], mvb[:, k, 1:2], LN_EPS, None, ALU.add).then_inc(s["var2"], 1)

                def norm2(i, k, h):
                    v.wait_ge(s["rstd2"], i + 1)
                    wait(v, o["stored"][k], 16 * h)
                    wait(v, o["xn_t"], i - 1)
                    v.tensor_scalar(o["xn"][:, k, :], xs[:, bass.ds(i, 1), :].rearrange("p a d -> p (a d)"), mvb[:, k, 0:1],
                                    rsb[:, k, :], ALU.subtract, ALU.mult).then_inc(o["xn_ready"], 1)
                skewed(v, B, [[(0, maxima), (2, query), (-6, dve_top(v, o)), (3, norm1), (-3, attended)], (-4, norm2)])

            @block.scalar
            def _(act):
                def operand(n, i, k):
                    act.wait_ge(s["qk_t"], 2 * i + n + 1)
                    wait(act, s["s2_done"], 4 * i - 12)
                    nc.scalar.activation((qT, kT)[n][:, k].rearrange("p a b -> p (a b)"), pqk[:], ACT.Copy).then_inc(s["qk_ready"], 1)

                def max_rows(i, k, h):
                    act.wait_ge(s["m_t"], i + 1)
                    wait(act, s["s2_done"], 4 * i - 4)
                    nc.scalar.activation(mT[:, k % 2, :], pqk[:, 0:P], ACT.Copy).then_inc(s["mT_ready"], 1)

                def exps(i, k, h):
                    for g in range(4):
                        act.wait_ge(s["s2_done"], 4 * i + g + 1)
                        if g == 0:
                            wait(act, s["av_done"], i - 1)
                        nc.scalar.activation(pr[:, k % 2, g, :], p2[g % 2][:], ACT.Exp, scale=float(DH0) ** -0.5).then_inc(s["exp_done"], 1)

                def weighted(i, k, h):
                    act.wait_ge(s["av_done"], i + 1)
                    wait(act, s["out_t"], i - 1)
                    nc.scalar.activation(ao[:, k % 2, :], po[:], ACT.Copy).then_inc(s["ao_ready"], 1)
                skewed(act, B, [(1, lambda i, k, h: operand(0, i, k)), (-1, exps), (1, lambda i, k, h: operand(1, i, k)),
                                (-5, act_xnT(act, o)), (-2, weighted), (0, max_rows)], unroll=4, slots=4)

            @block.tensor
            def _(pe):
                mm = nc.tensor.matmul

                def first(i, k, h):
                    pe.wait_ge(s["qk_ready"], 2 * i + 2)
                    pe.wait_ge(s["mask_ready"], i + 1)
                    for g in range(4):
                        wait(pe, s["max_done"], 4 * i + g - 1)
                        mm(p1[g % 2][:].rearrange("p (t k) -> p t k", t=4), identb,
                           mb[:, bass.ds(i, 1), :].broadcast_to([P, 4, P]), start=True, stop=True)
                        rows = slice(HR * (g % 2), HR * (g % 2) + HR)
                        for t in range(4):
                            last = mm(p1[g % 2][:, t * P:(t + 1) * P], qT[rows, k, 4 * (g // 2) + t, :],
                                      kT[rows, k, 4 * (g // 2) + t, :], start=False, stop=True, skip_group_check=True)
                        last.then_inc(s["s1_done"], 1)

                def turn(n, i, k):
                    pe.wait_ge(s["qx_ready" if n == 0 else "kx_ready"], i + 1)
                    wait(pe, s["qk_ready"], 2 * i + n)
                    if n == 0:
                        wait(pe, s["mT_ready"], i - 1)
                    x = (qx, kx)[n]
                    for t in range(8):
                        last = nc.tensor.transpose(pqk[:, t * P:(t + 1) * P], x[:, k % 2, 2 * t:2 * t + 2, :].rearrange("p h d -> p (h d)"), identb)
                    last.then_inc(s["qk_t"], 1)

                def turn_m(i, k, h):
                    pe.wait_ge(s["m_ready"], i + 1)
                    pe.wait_ge(s["qk_ready"], min(2 * i + 4, 2 * B) if isinstance(i, int) else 2 * i + 4)
                    nc.tensor.transpose(pqk[:, 0:P], m3[:].rearrange("p g t -> p (g t)"), identb).then_inc(s["m_t"], 1)

                def second(i, k, h):
                    pe.wait_ge(s["mT_ready"], i + 1)
                    for g in range(4):
                        wait(pe, s["exp_done"], 4 * i + g - 1)
                        mm(p2[g % 2][:].rearrange("p (t k) -> p t k", t=4), mb[:, bass.ds(i, 1), :].rearrange("p a k -> p (a k)"),
                           identb4, start=True, stop=True)
                        rows = slice(HR * (g % 2), HR * (g % 2) + HR)
                        for t in range(4):
                            to = p2[g % 2][:, t * P:(t + 1) * P]
                            j = 4 * (g // 2) + t
                            mm(to, kT[rows, k, j, :], qT[rows, k, j, :], start=False, stop=False, skip_group_check=True)
                            last = mm(to, cb[rows, CB_SELM + j:CB_SELM + j + 1].broadcast_to([HR, P]), mT[rows, k % 2, :],
                                      start=False, stop=True, skip_group_check=True)
                        last.then_inc(s["s2_done"], 1)

                def weigh(i, k, h):
                    pe.wait_ge(s["exp_done"], 4 * i + 4)
                    pe.wait_ge(s["vx_ready"], i + 1)
                    wait(pe, s["ao_ready"], i)
                    for g in range(4):
                        for t in range(4):
                            last = mm(po[32 * t:32 * t + 32, g * P:(g + 1) * P], vx[:, k % 2, head_of(g, t), :],
                                      pr[:, k % 2, g, t * P:(t + 1) * P], start=True, stop=True)
                    last.then_inc(s["av_done"], 1)

                def turn_out(i, k, h):
                    pe.wait_ge(s["ao_ready"], i + 1)
                    wait(pe, s["o_read"], i)
                    for g in range(4):
                        last = nc.tensor.transpose(pv[:, g * P:(g + 1) * P], ao[:, k % 2, g * P:(g + 1) * P], ident)
                    last.then_inc(s["out_t"], 1)
                skewed(pe, B, [(-6, pe_score(pe, o, 0)), (-3, turn_out), (1, lambda i, k, h: turn(0, i, k)), (0, first),
                               (-1, second), (1, lambda i, k, h: turn(1, i, k)), (-5, pe_xnT(pe, o)), (-2, weigh),
                               (0, turn_m)], unroll=4, slots=4)


    def route(l):
        with ExitStack() as st:
            def t(name, shape, dt=F32):
                return sb(st, f"{name}_r{l}", shape, dt)
            one = t("one", [P, E * B])
            oh = [t("oh0", [P, E, B]), t("oh1", [P, E, B])]
            sel = t("sel", [P, E, B], BF16)
            pre = t("pre", [P, E, B])
            tot = t("tot", [P, E, B])
            run = t("run", [P, E, B])
            exc = t("exc", [P, E, B])
            cmp = t("cmp", [P, E, B])
            cnt, nte, end, off = [t(n, [P, E]) for n in ("cnt", "nte", "end", "off")]
            slf = t("slf", [P, B, 2])
            slot = t("slot", [P, B, 2], I32)
            dsti = t("dsti", [P, NT], I32)
            unused = t("unused", [P, NT])
            hi = t("hi", [P, B, 2], I32)
            lo = t("lo", [P, B, 2], I32)
            hif, lof = t("hif", [P, B, 2]), t("lof", [P, B, 2])
            cmpj = t("cmpj", [P, NT, E])
            tef = t("tef", [P, NT])
            H = B // 2
            ohlo2 = t("ohlo", [P, 2, H, P], BF16)
            ohhi2 = t("ohhi", [P, 2, H, NT], BF16)
            rhs2 = t("rhs", [P, 2, H, 2, NT], BF16)
            srcf = t("srcf", [P, NT])
            wx = t("wx", [P, B])
            pp, pt, pi = [ps(st, f"{n}_r{l}") for n in ("pp", "pt", "pi")]
            s_st, s_sel, s_pre, s_lo, s_hi, s_rhs, s_tok, s_inv = [sem(st, f"{n}_r{l}") for n in
                ("route_step", "sel_ready", "prefix_done", "ohlo_ready", "ohhi_ready", "tile_lists_ready", "token_lists_ready", "inverse_done")]
            if l == 0:
                s_wx, s_we = sem(st, "gap_ready"), sem(st, "gap_exp")
            with nc.Block() as block:
                @block.tensor
                def _(pe):
                    pe.wait_ge(s_sel, 1)
                    se = sel[:].rearrange("p e t -> p (e t)")
                    nc.tensor.matmul(pp[:, 0:E * B], cb[:, CB_UPS:CB_UPS + P], se, start=True, stop=True)
                    nc.tensor.matmul(pt[:, 0:E * B], cb[:, CB_ONE:CB_ONE + P], se, start=True, stop=True).then_inc(s_pre, 1)
                    for part in range(TOPK * B // H):
                        pe.wait_ge(s_lo, part + 1)
                        pe.wait_ge(s_rhs, part + 1)
                        pe.wait_ge(s_tok, part + 1)
                        for m in range(H):
                            last = nc.tensor.matmul(pi[:, 0:2 * NT], ohlo2[:, part % 2, m, :], rhs2[:, part % 2, m].rearrange("p a j -> p (a j)"),
                                                    start=(part == 0 and m == 0), stop=(part == TOPK * B // H - 1 and m == H - 1))
                        last.then_inc(s_inv, 1)

                @block.gpsimd
                def _(g):
                    for part in range(TOPK * B // H):
                        g.wait_ge(s_hi, part + 1)
                        g.tensor_tensor(rhs2[:, part % 2, :, 0, :], ohhi2[:, part % 2],
                                        cb[:, CB_T + part * H:CB_T + (part + 1) * H].unsqueeze(2).broadcast_to([P, H, NT]),
                                        ALU.mult).then_inc(s_rhs, 1)

                @block.scalar
                def _(act):
                    if l == 0:
                        act.wait_ge(s_wx, 1)
                        nc.scalar.activation(wx[:], wx[:], ACT.Exp).then_inc(s_we, 1)
                    for part in range(TOPK * B // H):
                        act.wait_ge(s_hi, part + 1)
                        nc.scalar.activation(rhs2[:, part % 2, :, 1, :], ohhi2[:, part % 2], ACT.Copy, scale=cf[:, CF_P:CF_P + 1]).then_inc(s_tok, 1)

                @block.vector
                def _(v):
                    ch = Chain(v, s_st, 0, None)
                    tt, ts = v.tensor_tensor, v.tensor_scalar
                    eb = cf[:, CF_E:CF_E + E * B].rearrange("p (e t) -> p e t", e=E)
                    for k in range(2):
                        ch(tt(oh[k][:], topi[:, :, k].unsqueeze(1).broadcast_to([P, E, B]), eb, ALU.is_equal))
                    tt(sel[:], oh[0][:], oh[1][:], ALU.add).then_inc(s_sel, 1)
                    if l == 0:
                        tt(wx[:], topv[:, :, 1], topv[:, :, 0], ALU.subtract).then_inc(s_wx, 1)
                        v.wait_ge(s_we, 1)
                        ch(ts(wt[:, :, 1], wx[:], 1.0, None, ALU.add))
                        ch(v.reciprocal(wt[:, :, 0], wt[:, :, 1]))
                        ch(tt(wt[:, :, 1], wx[:], wt[:, :, 0], ALU.mult))
                        ch(ts(wt[:].rearrange("p t k -> p (t k)"), wt[:].rearrange("p t k -> p (t k)"), gts[:, 2:3], None, ALU.mult))
                    else:
                        ch(v.memset(wt[:], 1.0 / TOPK))
                        ch(ts(wt[:].rearrange("p t k -> p (t k)"), wt[:].rearrange("p t k -> p (t k)"), gts[:, 3:4], None, ALU.mult))
                    ch(v.memset(one[:], 1.0))
                    v.wait_ge(s_pre, 1)
                    ch(v.tensor_copy(pre[:].rearrange("p e t -> p (e t)"), pp[:, 0:E * B]))
                    ch(v.tensor_copy(tot[:].rearrange("p e t -> p (e t)"), pt[:, 0:E * B]))
                    ch(v.tensor_tensor_scan(run[:].rearrange("p e t -> p (e t)"), one[:], tot[:].rearrange("p e t -> p (e t)"),
                                            0.0, ALU.mult, ALU.add))
                    ch(tt(exc[:], run[:], tot[:], ALU.subtract))
                    ch(tt(cnt[:], run[:, :, B - 1], exc[:, :, 0], ALU.subtract))
                    ch(tt(cmp[:], cnt[:].unsqueeze(2).broadcast_to([P, E, B]),
                          cf[:, CF_THR:CF_THR + E * B].rearrange("p (e t) -> p e t", e=E), ALU.is_gt))
                    ch(v.tensor_reduce(nte[:], cmp[:], AX.X, ALU.add))
                    ch(v.tensor_tensor_scan(end[:], one[:, 0:E], nte[:], 0.0, ALU.mult, ALU.add))
                    ch(tt(off[:], end[:], nte[:], ALU.subtract))
                    ch(v.scalar_tensor_tensor(off[:], off[:], float(P), exc[:, :, 0], ALU.mult, ALU.subtract))
                    ch(tt(pre[:], pre[:], exc[:], ALU.add))
                    ch(tt(pre[:], pre[:], off[:].unsqueeze(2).broadcast_to([P, E, B]), ALU.add))
                    for k in range(2):
                        ch(tt(oh[k][:], oh[k][:], pre[:], ALU.mult))
                        ch(v.tensor_reduce(slf[:, :, k], oh[k][:].rearrange("p e t -> p t e"), AX.X, ALU.add))
                    ch(v.tensor_copy(slot[:], slf[:]))
                    ch(ts(hi[:], slot[:], 7, None, ALU.arith_shift_right))
                    ch(ts(lo[:], slot[:], P - 1, None, ALU.bitwise_and))
                    ch(v.tensor_copy(hif[:], hi[:]))
                    ch(v.tensor_copy(lof[:], lo[:]))
                    lf = lof[:].rearrange("p t k -> p (t k)")
                    hf = hif[:].rearrange("p t k -> p (t k)")
                    jb = cf[:, CF_J:CF_J + NT]
                    for part in range(TOPK * B // H):
                        ms = slice(part * H, (part + 1) * H)
                        wait(v, s_inv, part - 1)
                        ohlo, ohhi = ohlo2[:, part % 2], ohhi2[:, part % 2]
                        tt(ohhi, hf[:, ms].unsqueeze(2).broadcast_to([P, H, NT]), jb.unsqueeze(1).broadcast_to([P, H, NT]),
                           ALU.is_equal).then_inc(s_hi, 1)
                        tt(ohlo, lf[:, ms].unsqueeze(2).broadcast_to([P, H, P]),
                           cf[:, CF_IOTA:CF_IOTA + P].unsqueeze(1).broadcast_to([P, H, P]), ALU.is_equal).then_inc(s_lo, 1)
                    ch(tt(cmpj[:], end[:].unsqueeze(1).broadcast_to([P, NT, E]), jb.unsqueeze(2).broadcast_to([P, NT, E]), ALU.is_le))
                    ch(v.tensor_reduce(tef[:], cmpj[:], AX.X, ALU.add))
                    ch(ts(tef[:], tef[:], float(E - 1), None, ALU.min))
                    ch(v.tensor_copy(texp[:], tef[:]))
                    v.wait_ge(s_inv, TOPK * B // H)
                    ch(ts(srcf[:], pi[:, 0:NT], float(P), None, ALU.mult))
                    ch(tt(srcf[:], srcf[:], pi[:, NT:2 * NT], ALU.add))
                    ch(ts(unused[:], srcf[:], 0.0, None, ALU.is_equal))
                    ch(tt(unused[:], unused[:], cf[:, CF_U:CF_U + NT], ALU.mult))
                    ch(tt(unused[:], unused[:], srcf[:], ALU.add))
                    ch(ts(unused[:], unused[:], float((NT - 1) * P), None, ALU.add))
                    ch(v.tensor_copy(dst[:], unused[:]))
                    ch(ts(srcf[:], srcf[:], float(-P), 0.0, ALU.add, ALU.max))
                    ch(v.tensor_copy(dsti[:], srcf[:]))
                    ch(ts(src[:], dsti[:], 8, 7, ALU.arith_shift_right, ALU.logical_shift_left))
                    ch(ts(dsti[:], dsti[:], P - 1, None, ALU.bitwise_and))
                    ch(tt(src[:], src[:], dsti[:], ALU.bitwise_or))
                    ch.end()

    route(0)

    def experts(l, hidden, w_out, fn, layer0, loads=()):
        L = len(hidden)
        with ExitStack() as st:
            ix, iy = sb(st, f"ix_f{l}", [P, 2], I32), sb(st, f"iy_f{l}", [P, 2], I32)
            xg = sb(st, f"xg_f{l}", [P, 2, P])
            act_in = [sb(st, f"in{n}_f{l}", [P, 2, (F if n else P)]) for n in range(L + 1)]
            mats = hidden + [(w_out, FC)]
            cols = [F] * L + [P]
            wb = [sb(st, f"w{n}_f{l}", [P, 2, c * cols[n]]) for n, (_, c) in enumerate(mats)]
            bb = [sb(st, f"b{n}_f{l}", [P, 2, FC]) for n in range(L)] + [sb(st, f"b{L}_f{l}", [P, 2, P])]
            y = sb(st, f"y_f{l}", [P, 2, P])
            ptr = ps(st, f"pt_f{l}")
            pmm = [ps(st, f"pm{n}_f{l}") for n in range(L + 1)]
            s_g = [sem(st, f"gathered{k}_f{l}") for k in range(2)]
            s_o = [sem(st, f"stored{k}_f{l}") for k in range(2)]
            s_ix, s_t = sem(st, f"index_ready_f{l}"), sem(st, f"turned_f{l}")
            s_ld = sem(st, f"loaded_f{l}") if loads else None
            s_in = [sem(st, f"input_ready{n}_f{l}") for n in range(L + 1)]
            s_w = [sem(st, f"weights_ready{n}_f{l}") for n in range(L + 1)]
            s_m = [sem(st, f"product{n}_f{l}") for n in range(L + 1)]
            s_y = sem(st, f"result_ready_f{l}")
            with nc.Block() as block:
                @block.gpsimd
                def _(g):
                    def gather(i, k, h):
                        wait(g, s_t, i - 1)
                        g.tensor_tensor(ix[:, k:k + 1], src[:, bass.ds(i, 1)], none[:], ALU.add).then_inc(s_ix, 1)
                        wait_apart(g, s_ix, i + 1, gfence)
                        g.indirect_dma_start(xg[:, k, :], None, xn_d[l], bass.IndirectOffsetOnAxis(ix[:, k:k + 1], axis=0)).then_inc(s_g[k], 16)

                    def scatter(i, k, h):
                        wait_apart(g, s_y, 2 * i + 2, gfence)
                        g.indirect_dma_start(y_d[l], bass.IndirectOffsetOnAxis(iy[:, k:k + 1], axis=0), y[:, k, :], None).then_inc(s_o[k], 16)
                    skewed(g, NT, [(L + 2, gather), (-1, scatter)])
                    for k in range(2):
                        g.wait_ge(s_o[k], 16 * NT // 2)

                @block.tensor
                def _(pe):
                    mm = nc.tensor.matmul

                    def turn(i, k, h):
                        pe.wait_ge(s_g[k], 16 * (h + 1))
                        wait(pe, s_in[0], i)
                        nc.tensor.transpose(ptr[:, 0:P], xg[:, k, :], ident).then_inc(s_t, 1)

                    def layer(n):
                        chunks = hidden[n][1]

                        def stage(i, k, h):
                            pe.wait_ge(s_in[n], i + 1)
                            pe.wait_ge(s_w[n], i + 1)
                            wait(pe, s_in[n + 1], i)
                            for f in range(FC):
                                to = pmm[n][:, f * P:(f + 1) * P]
                                for c in range(chunks):
                                    last = mm(to, wb[n][:, k, c * F + f * P:c * F + (f + 1) * P], act_in[n][:, k, c * P:(c + 1) * P],
                                              start=c == 0, stop=c == chunks - 1)
                            last.then_inc(s_m[n], 1)
                        return stage

                    def output(i, k, h):
                        pe.wait_ge(s_in[L], i + 1)
                        pe.wait_ge(s_w[L], i + 1)
                        wait(pe, s_y, 2 * i)
                        for c in range(FC):
                            last = mm(pmm[L][:, 0:P], act_in[L][:, k, c * P:(c + 1) * P],
                                      wb[L][:, k, c * P:(c + 1) * P], start=c == 0, stop=c == FC - 1)
                        last.then_inc(s_m[L], 1)
                    skewed(pe, NT, [(L + 1, turn)] + [(L - n, layer(n)) for n in range(L)] + [(0, output)], unroll=4)

                @block.scalar
                def _(act):
                    def activate(n):
                        def stage(i, k, h):
                            act.wait_ge(s_m[n], i + 1)
                            wait(act, s_m[n + 1], i - 1)
                            for f in range(FC):
                                last = nc.scalar.activation(act_in[n + 1][:, k, f * P:(f + 1) * P], pmm[n][:, f * P:(f + 1) * P], fn,
                                                            bias=bb[n][:, k, f:f + 1])
                            last.then_inc(s_in[n + 1], 1)
                        return stage
                    skewed(act, NT, [(L - n, activate(n)) for n in range(L)])

                @block.vector
                def _(v):
                    def inputs(i, k, h):
                        v.wait_ge(s_t, i + 1)
                        wait(v, s_m[0], i - 1)
                        nc.vector.tensor_copy(act_in[0][:, k, :], ptr[:, 0:P]).then_inc(s_in[0], 1)

                    def weights(n):
                        w, chunks = mats[n]

                        def stage(i, k, h):
                            e = v.value_load(texp[0:1, bass.ds(i, 1)], min_val=0, max_val=E - 1)
                            wait(v, s_m[n], i - 1)
                            if n == L:
                                wait(v, s_y, 2 * (i - 1))
                            else:
                                wait(v, s_in[n + 1], i - 1)
                            frm = w[:, bass.ds(e, 1)].rearrange("p a c f -> p (a c f)" if chunks > 1 else "p a f -> p (a f)")
                            v.tensor_copy(wb[n][:, k, :], frm)
                            bias = bT[:, bass.ds(e * FC + (layer0 + n) * E * FC, FC)] if n < L else bout[l][:, bass.ds(e * P, P)]
                            v.tensor_copy(bb[n][:, k, :], bias).then_inc(s_w[n], 1)
                        return stage

                    def result(i, k, h):
                        v.wait_ge(s_m[L], i + 1)
                        wait(v, s_o[k], 16 * h)
                        v.tensor_tensor(y[:, k, :], pmm[L][:, 0:P], bb[L][:, k, :], ALU.add).then_inc(s_y, 1)
                        nc.vector.tensor_copy(iy[:, k:k + 1], dst[:, bass.ds(i, 1)]).then_inc(s_y, 1)
                    skewed(v, NT, [(L + 1, inputs)] + [(L - n + 1, weights(n)) for n in range(L + 1)] + [(0, result)], unroll=4)

                @block.sync
                def _(sp):
                    for to, frm in loads:
                        sp.dma_start(to, frm).then_inc(s_ld, 16)
                    if loads:
                        sp.wait_ge(s_ld, 16 * len(loads))

    experts(0, [(w01, 1)], w02, ACT.Relu, 0, [(w12[:, e], w12_d[e].rearrange("(c p) f -> p c f", p=P)) for e in range(E)])

    w11 = wts[:, 0:E * F].rearrange("p (e f) -> p e f", e=E)
    w13 = wts[:, E * F:2 * E * F].rearrange("p (e c d) -> p e c d", e=E, c=FC)

    stB = ExitStack()
    gall = sb(stB, "gall", [P, 2, B, NH1])
    mvx = sb(stB, "mvx", [P, B, 2])
    enm = sb(stB, "enm", [P, B, NH1])
    aT3 = sb(stB, "aT3", [96, B // 4, P], BF16)
    nT3 = sb(stB, "nT3", [96, B // 4, P], BF16)
    with ExitStack() as st:
        yg = sb(st, "yg_b", [P, 2, TOPK, P])
        tmp = sb(st, "tmp_b", [P, P])
        st6 = sb(st, "st6_b", [P, 6])
        mv = sb(st, "mv_b", [P, 2, 2])
        xn = sb(st, "xn_b", [P, 2, P])
        xT = sb(st, "xT_b", [P, 2, 2, P])
        cT_in = sb(st, "cT_in", [P, 2, P])
        s_ctx = sem(st, "ctx_copied_b")
        pT, pG = ps(st, "pT_b"), ps(st, "pG_b")
        names = ("x_added", "norm_step", "var_ready", "rstd_ready", "xn_ready", "turned", "xT_ready", "gates_mm", "gates_read", "w_in")
        s = {n: sem(st, n + "_b") for n in names}
        s_g = [sem(st, f"y_in{k}_b") for k in range(2)]
        with nc.Block() as block:
            @block.sync
            def _(sp):
                sp.dma_start(w11, w11_d.rearrange("e d f -> d e f")).then_inc(s["w_in"], 16)
                for e in range(E):
                    sp.dma_start(w13[:, e], w13_d[e].rearrange("(c p) d -> p c d", p=P)).then_inc(s["w_in"], 16)

                def load(i, k, h):
                    wait(sp, s["x_added"], i - 1)
                    sp.dma_start(yg[:, k], y_d[0][bass.ds(NT * P + i * (TOPK * P), TOPK * P), :].rearrange("(n p) d -> p n d", n=TOPK)).then_inc(s_g[k], 16)
                skewed(sp, B, [(2, load)])
                sp.wait_ge(s["w_in"], 16 * (E + 1))

            @block.gpsimd
            def _(g):
                def root(i, k, h):
                    g.wait_ge(s["var_ready"], i + 1)
                    mo = mvx[:, bass.ds(i, 1), :].rearrange("p a n -> p (a n)")
                    g.tensor_tensor(mo[:, 1:2], mv[:, k, 1:2], half[:], ALU.pow)
                    g.tensor_copy(mo[:, 0:1], mv[:, k, 0:1]).then_inc(s["rstd_ready"], 1)
                skewed(g, B, [(1, root)])

            @block.vector
            def _(v):
                def combine(i, k, h):
                    v.wait_ge(s_g[k], 16 * (h + 1))
                    xv = xs[:, bass.ds(i, 1), :].rearrange("p a d -> p (a d)")
                    wv = wt[:, bass.ds(i, 1), :].rearrange("p a n -> p (a n)")
                    ch = Chain(v, s["norm_step"], i, 3)
                    yield from ch.step(v.scalar_tensor_tensor(tmp[:], yg[:, k, 0, :], wv[:, 0:1], xv, ALU.mult, ALU.add))
                    v.scalar_tensor_tensor(xv, yg[:, k, 1, :], wv[:, 1:2], tmp[:], ALU.mult, ALU.add).then_inc(s["x_added"], 1)
                    yield
                    wait_apart(v, s["x_added"], i + 1, vfence)
                    yield from ch.step(v.bn_stats(st6[:], xv), vfence)
                    wait_apart(v, s["rstd_ready"], i - 1, vfence)
                    yield from ch.step(v.bn_aggr(mv[:, k, :], st6[:]))
                    ch.end()
                    v.tensor_scalar(mv[:, k, 1:2], mv[:, k, 1:2], LN_EPS, None, ALU.add).then_inc(s["var_ready"], 1)

                def normed(i, k, h):
                    v.wait_ge(s["rstd_ready"], i + 1)
                    wait(v, s["turned"], i - 1)
                    mo = mvx[:, bass.ds(i, 1), :].rearrange("p a n -> p (a n)")
                    v.tensor_scalar(xn[:, k, :], xs[:, bass.ds(i, 1), :].rearrange("p a d -> p (a d)"), mo[:, 0:1], mo[:, 1:2],
                                    ALU.subtract, ALU.mult).then_inc(s["xn_ready"], 1)

                def turned(i, k, h):
                    yield
                    v.wait_ge(s["turned"], i + 1)
                    wait(v, s["gates_mm"], i - 1)
                    v.tensor_copy(xT[:, k].rearrange("p a s -> p (a s)"), pT[:, 0:2 * P]).then_inc(s["xT_ready"], 1)

                def gates(i, k, h):
                    yield
                    yield
                    v.wait_ge(s["gates_mm"], i + 1)
                    v.tensor_copy(gall[:, :, bass.ds(i, 1), :].rearrange("p n a h -> p n (a h)"),
                                  pG[:, 0:2 * NH1].rearrange("p (n h) -> p n h", n=2)).then_inc(s["gates_read"], 1)
                skewed(v, B, [[(1, combine), (-1, normed), (-2, turned), (-3, gates)]])

            @block.tensor
            def _(pe):
                def turn(i, k, h):
                    pe.wait_ge(s["xn_ready"], i + 1)
                    pe.wait_ge(s_ctx, i + 1)
                    wait(pe, s["xT_ready"], i)
                    nc.tensor.transpose(pT[:, 0:P], xn[:, k, :], ident)
                    nc.tensor.transpose(pT[:, P:2 * P], cT_in[:, k, :], ident).then_inc(s["turned"], 1)

                def gate(i, k, h):
                    pe.wait_ge(s["xT_ready"], i + 1)
                    wait(pe, s["gates_read"], i)
                    for r in range(3):
                        last = nc.tensor.matmul(pG[:, 0:2 * NH1], xT[:, k, min(r, 1), :], wgate[:, r, :], start=r == 0, stop=r == 2)
                    last.then_inc(s["gates_mm"], 1)
                skewed(pe, B, [(-1, turn), (-2, gate)])

            @block.scalar
            def _(act):
                def context(i, k, h):
                    wait(act, s["turned"], i - 1)
                    nc.scalar.activation(cT_in[:, k, :], cx[:, bass.ds(i, 1), :].rearrange("p a d -> p (a d)"), ACT.Copy).then_inc(s_ctx, 1)
                skewed(act, B, [(0, context)])

    with ExitStack() as st:
        def t(name, shape=(P, B * NH1), dt=F32):
            return sb(st, name + "_g", list(shape), dt)
        ig, fg, ab, l1, mn, lf, cs, a, ac, nac, m_all = [t(n) for n in ("ig", "fg", "ab", "l1", "mn", "lf", "cs", "a", "ac", "nac", "m_all")]
        AT = t("AT", (P, 2, P))
        one = t("one", (P, P))
        res = t("res")
        parts = t("parts", (P, B // 4, 3, 4 * NH1), BF16)
        nparts = t("nparts", (P, B // 4, 3, 4 * NH1), BF16)
        pcs, paT, pAc = ps(st, "pcs"), ps(st, "paT"), ps(st, "pAc")
        p3 = [ps(st, f"p3{n}", (P, 1024), BF16) for n in range(2)]
        names = ("step", "abs_ready", "exp_done", "lf_ready", "pe_done", "a_ready", "AT_ready", "m_ready", "parts_ready")
        s = {n: sem(st, n + "_g") for n in names}
        with nc.Block() as block:
            @block.scalar
            def _(act):
                act.wait_ge(s["abs_ready"], 1)
                nc.scalar.activation(l1[:], ab[:], ACT.Exp, scale=-1.0).then_inc(s["exp_done"], 1)
                act.wait_ge(s["exp_done"], 1)
                nc.scalar.activation(l1[:], l1[:], ACT.Ln, bias=1.0).then_inc(s["exp_done"], 1)
                act.wait_ge(s["m_ready"], 1)
                nc.scalar.activation(enm[:].rearrange("p b h -> p (b h)"), m_all[:], ACT.Exp, scale=-1.0).then_inc(s["exp_done"], 1)

            @block.vector
            def _(v):
                ch = Chain(v, s["step"], 0, None)
                tt = v.tensor_tensor
                bh = lambda x: x[:].rearrange("p (b h) -> p b h", b=B)
                bb = lambda n: gbias[:, n, :].unsqueeze(1).broadcast_to([P, B, NH1])
                ch(tt(bh(fg), gall[:, 1], bb(1), ALU.add))
                v.scalar_tensor_tensor(ab[:], fg[:], -1.0, fg[:], ALU.mult, ALU.max).then_inc(s["abs_ready"], 1)
                ch(tt(bh(ig), gall[:, 0], bb(0), ALU.add))
                ch(v.tensor_scalar(mn[:], fg[:], 0.0, None, ALU.min))
                ch(v.memset(one[:], 1.0))
                v.wait_ge(s["exp_done"], 2)
                tt(lf[:], mn[:], l1[:], ALU.subtract).then_inc(s["lf_ready"], 1)
                v.wait_ge(s["pe_done"], 1)
                ch(v.tensor_copy(cs[:], pcs[:, 0:B * NH1]))
                tt(a[:], ig[:], cs[:], ALU.subtract).then_inc(s["a_ready"], 1)

                def three_parts(x, to):
                    g4 = lambda y: y[:].rearrange("p (g c) -> p g c", c=4 * NH1)
                    ch(v.tensor_copy(to[:, :, 0, :], g4(x)))
                    ch(tt(g4(res), g4(x), to[:, :, 0, :], ALU.subtract))
                    ch(v.tensor_copy(to[:, :, 1, :], g4(res)))
                    ch(tt(g4(res), g4(res), to[:, :, 1, :], ALU.subtract))
                    v.tensor_copy(to[:, :, 2, :], g4(res)).then_inc(s["parts_ready"], 1)
                    v.wait_ge(s["parts_ready"], 1 if to is parts else 2)
                v.wait_ge(s["a_ready"], 1)
                three_parts(a, parts)
                v.wait_ge(s["pe_done"], 2)
                for n in range(2):
                    v.tensor_tensor_scan(AT[:, n, :], one[:], paT[:, n * P:(n + 1) * P], -3e38, ALU.mult, ALU.max).then_inc(s["AT_ready"], 1)
                v.wait_ge(s["pe_done"], 3)
                ch(v.tensor_copy(aT3[:].rearrange("p g s -> p (g s)"), p3[0][0:96, :]))
                v.wait_ge(s["pe_done"], 4)
                ch(v.tensor_copy(ac[:], pAc[:, 0:B * NH1]))
                ch(v.tensor_scalar(nac[:], ac[:], -1.0, None, ALU.mult))
                three_parts(nac, nparts)
                tt(m_all[:], cs[:], ac[:], ALU.add).then_inc(s["m_ready"], 1)
                v.wait_ge(s["pe_done"], 5)
                v.tensor_copy(nT3[:].rearrange("p g s -> p (g s)"), p3[1][0:96, :])

            @block.tensor
            def _(pe):
                pe.wait_ge(s["lf_ready"], 1)
                nc.tensor.matmul(pcs[:, 0:B * NH1], cf[:, CF_UPI:CF_UPI + P], lf[:], start=True, stop=True).then_inc(s["pe_done"], 1)
                pe.wait_ge(s["a_ready"], 1)
                nc.tensor.transpose(paT[:, 0:P], a[:, 0:P], ident)
                nc.tensor.transpose(paT[:, P:2 * P], a[:, P:2 * P], ident).then_inc(s["pe_done"], 1)

                def turn_parts(n):
                    pe.wait_ge(s["parts_ready"], n + 1)
                    for g in range(B // 4):
                        last = nc.tensor.transpose(p3[n][0:96, g * P:(g + 1) * P], (parts, nparts)[n][:, g].rearrange("p t c -> p (t c)"), identb)
                    last.then_inc(s["pe_done"], 1)
                turn_parts(0)
                pe.wait_ge(s["AT_ready"], 2)
                nc.tensor.transpose(pAc[:, 0:P], AT[:, 0, :], ident)
                nc.tensor.transpose(pAc[:, P:2 * P], AT[:, 1, :], ident).then_inc(s["pe_done"], 1)
                turn_parts(1)

    QR = 6 * DH1
    with ExitStack() as st:
        qn, qr, kr = sb(st, "qn_c", [P, P]), sb(st, "qr_c", [P, P]), sb(st, "kr_c", [P, P])
        qx = sb(st, "qx_c", [P, 2, NH1, QR], BF16)
        kx = sb(st, "kx_c", [P, 2, NH1, QR], BF16)
        vx = sb(st, "vx_c", [P, 2, NH1, 32])
        qT = sb(st, "qT_c", [QR, 4, NH1, P], BF16)
        kT = sb(st, "kT_c", [QR, 4, NH1, P], BF16)
        D = sb(st, "D_c", [P, 2, 2, 4 * P])
        C = sb(st, "C_c", [P, 2, 2, 4 * P])
        ao = sb(st, "ao_c", [P, 2, 2 * P])
        den = sb(st, "den_c", [P, NH1])
        hh = sb(st, "hh_c", [P, 2, NH1, DH1])
        hn = sb(st, "hn_c", [P, P])
        st6, st6b = sb(st, "st6_c", [P, 6]), sb(st, "st6b_c", [P, 6])
        mv, mvb = sb(st, "mv_c", [P, 2, 2]), sb(st, "mvb_c", [P, 2, 2])
        rs, rsb = sb(st, "rs_c", [P, 2, 1]), sb(st, "rsb_c", [P, 2, 1])
        pd = [ps(st, f"pd{r}") for r in range(2)]
        pq = [ps(st, f"pq{r}") for r in range(2)]
        pqk, po, pv = ps(st, "pqk_c", (P, NH1 * P), BF16), ps(st, "po_c"), ps(st, "pv_c")
        o = router_buffers(st, 1)
        names = ("init", "k_parts", "kx_ready", "vx_ready", "qx_ready", "qk_t", "qk_ready", "d_done", "D_ready", "s_done", "C_ready",
                 "h_done", "ao_ready", "out_t", "h_read", "pool_step", "q_step", "h_step", "var1", "rstd1", "var2", "rstd2", "x_step")
        s = {n: sem(st, n + "_c") for n in names}
        with nc.Block() as block:
            @block.sync
            def _(sp):
                skewed(sp, B, [(-4, sp_xn(sp, o, 1))])
                for k in range(2):
                    sp.wait_ge(o["stored"][k], 16 * B // 2)

            @block.gpsimd
            def _(g):
                g.memset(vx[:, :, :, DH1 + 1:], 0.0)
                g.memset(vx[:, :, :, DH1:DH1 + 1], 1.0).then_inc(s["init"], 1)
                g.wait_ge(s["init"], 1)
                c = lambda i: cx[:, bass.ds(i, 1), :].rearrange("p a (h d) -> p (a h) d", d=DH1)

                def keys(i, k, h):
                    wait_apart(g, s["qk_t"], 2 * i - 2, gfence)
                    r = kr[:].rearrange("p (h d) -> p h d", d=DH1)
                    ch = Chain(g, s["pool_step"], i, 3)
                    ch(g.tensor_copy(kx[:, k, :, 0:DH1], c(i)), gfence)
                    ch(g.tensor_tensor(r, c(i), kx[:, k, :, 0:DH1], ALU.subtract), gfence)
                    ch(g.tensor_copy(kx[:, k, :, DH1:2 * DH1], r))
                    ch.end()
                    g.tensor_tensor(kx[:, k, :, 2 * DH1:3 * DH1], r, kx[:, k, :, DH1:2 * DH1], ALU.subtract).then_inc(s["k_parts"], 1)

                def values(i, k, h):
                    wait_apart(g, s["h_done"], i - 1, gfence)
                    g.tensor_copy(vx[:, k, :, 0:DH1], c(i)).then_inc(s["vx_ready"], 1)

                def root1(i, k, h):
                    g.wait_ge(s["var1"], i + 1)
                    g.tensor_tensor(rs[:, k, :], mv[:, k, 1:2], half[:], ALU.pow).then_inc(s["rstd1"], 1)

                def root2(i, k, h):
                    g.wait_ge(s["var2"], i + 1)
                    g.tensor_tensor(rsb[:, k, :], mvb[:, k, 1:2], half[:], ALU.pow).then_inc(s["rstd2"], 1)
                skewed(g, B, [(2, keys), (0, values), (-3, root2), (-2, root1)])

            @block.vector
            def _(v):
                v.wait_ge(s["init"], 1)

                def query(i, k, h):
                    wait(v, s["qk_t"], 2 * i - 2)
                    mo = mvx[:, bass.ds(i, 1), :].rearrange("p a n -> p (a n)")
                    q = qn[:].rearrange("p (h d) -> p h d", d=DH1)
                    r = qr[:].rearrange("p (h d) -> p h d", d=DH1)
                    spread = lambda x, n: x.unsqueeze(2).broadcast_to([P, NH1, n, DH1])
                    ch = Chain(v, s["q_step"], i, 4)
                    yield from ch.step(v.tensor_scalar(qn[:], xs[:, bass.ds(i, 1), :].rearrange("p a d -> p (a d)"), mo[:, 0:1], mo[:, 1:2],
                                       ALU.subtract, ALU.mult))
                    yield from ch.step(v.tensor_copy(qx[:, k, :, 0:3 * DH1].rearrange("p h (n d) -> p h n d", n=3), spread(q, 3)))
                    yield from ch.step(v.tensor_tensor(r, q, qx[:, k, :, 0:DH1], ALU.subtract))
                    yield from ch.step(v.tensor_copy(qx[:, k, :, 3 * DH1:5 * DH1].rearrange("p h (n d) -> p h n d", n=2), spread(r, 2)))
                    ch.end()
                    v.tensor_tensor(qx[:, k, :, 5 * DH1:], r, qx[:, k, :, 3 * DH1:4 * DH1], ALU.subtract).then_inc(s["qx_ready"], 1)

                def products(i, k, h):
                    for r in range(2):
                        v.wait_ge(s["s_done"], 2 * i + r + 1)
                        v.wait_ge(s["D_ready"], 2 * i + r + 1)
                        if r == 0:
                            wait(v, s["h_done"], i - 1)
                        v.scalar_tensor_tensor(C[:, k, r, :], pq[r][:], float(DH1) ** -0.5, D[:, k, r, :], ALU.mult, ALU.mult).then_inc(s["C_ready"], 1)
                        yield

                def divide(i, k, h):
                    v.wait_ge(s["out_t"], i + 1)
                    ov = pv[:, 0:2 * P].rearrange("p (n d) -> p n d", d=32)
                    ch = Chain(v, s["h_step"], i, 6)
                    rt = lambda x: x.rearrange("p (t r) -> p r t", r=2)
                    sums = ov[:, :, DH1].rearrange("p (r t) -> p r t", r=2)
                    yield from ch.step(v.scalar_tensor_tensor(rt(den[:]), sums, -1.0, rt(enm[:, bass.ds(i, 1), :].rearrange("p a h -> p (a h)")), ALU.mult, ALU.max))
                    yield from ch.step(v.tensor_tensor(rt(den[:]), sums, rt(den[:]), ALU.max))
                    yield from ch.step(v.tensor_scalar(den[:], den[:], NORM_EPS, None, ALU.add))
                    yield from ch.step(v.reciprocal(den[:], den[:]))
                    v.tensor_tensor(hh[:, k].rearrange("p (t r) d -> p r t d", r=2),
                                    ov[:, :, 0:DH1].rearrange("p (r t) d -> p r t d", r=2),
                                    rt(den[:]).unsqueeze(3).broadcast_to([P, 2, 4, DH1]), ALU.mult).then_inc(s["h_read"], 1)
                    yield
                    wait_apart(v, s["h_read"], i + 1, vfence)
                    yield from ch.step(v.bn_stats(st6[:], hh[:, k].rearrange("p h d -> p (h d)")), vfence)
                    yield from ch.step(v.bn_aggr(mv[:, k, :], st6[:]))
                    ch.end()
                    v.tensor_scalar(mv[:, k, 1:2], mv[:, k, 1:2], LN_EPS, None, ALU.add).then_inc(s["var1"], 1)

                def add(i, k, h):
                    v.wait_ge(s["rstd1"], i + 1)
                    xv = xs[:, bass.ds(i, 1), :].rearrange("p a d -> p (a d)")
                    ch = Chain(v, s["x_step"], i, 5)
                    yield from ch.step(v.tensor_scalar(hn[:], hh[:, k].rearrange("p h d -> p (h d)"), mv[:, k, 0:1], rs[:, k, :], ALU.subtract, ALU.mult))
                    yield from ch.step(v.tensor_tensor(hn[:], hn[:], lnsc[:], ALU.mult))
                    yield from ch.step(v.tensor_tensor(xv, xv, hn[:], ALU.add), vfence)
                    yield from ch.step(v.bn_stats(st6b[:], xv), vfence)
                    yield from ch.step(v.bn_aggr(mvb[:, k, :], st6b[:]))
                    ch.end()
                    v.tensor_scalar(mvb[:, k, 1:2], mvb[:, k, 1:2], LN_EPS, None, ALU.add).then_inc(s["var2"], 1)

                def norm2(i, k, h):
                    v.wait_ge(s["rstd2"], i + 1)
                    wait(v, o["stored"][k], 16 * h)
                    wait(v, o["xn_t"], i - 1)
                    v.tensor_scalar(o["xn"][:, k, :], xs[:, bass.ds(i, 1), :].rearrange("p a d -> p (a d)"), mvb[:, k, 0:1],
                                    rsb[:, k, :], ALU.subtract, ALU.mult).then_inc(o["xn_ready"], 1)
                skewed(v, B, [[(0, products), (-2, divide), (-6, dve_top(v, o)), (-3, add), (2, query)], (-4, norm2)])

            @block.scalar
            def _(act):
                def operand(n, i, k):
                    act.wait_ge(s["qk_t"], 2 * i + n + 1)
                    wait(act, s["s_done"], 2 * i - 6)
                    nc.scalar.activation((qT, kT)[n][:, k].rearrange("p a b -> p (a b)"), pqk[0:QR, :], ACT.Copy).then_inc(s["qk_ready"], 1)

                def decays(i, k, h):
                    for r in range(2):
                        act.wait_ge(s["d_done"], 2 * i + r + 1)
                        if r == 0:
                            wait(act, s["C_ready"], 2 * i - 2)
                        nc.scalar.activation(D[:, k % 2, r, :], pd[r][:], ACT.Exp).then_inc(s["D_ready"], 1)

                def weighted(i, k, h):
                    act.wait_ge(s["h_done"], i + 1)
                    wait(act, s["out_t"], i - 1)
                    nc.scalar.activation(ao[:, k % 2, :], po[:, 0:2 * P], ACT.Copy).then_inc(s["ao_ready"], 1)
                def repeats(i, k, h):
                    act.wait_ge(s["k_parts"], i + 1)
                    nc.scalar.activation(kx[:, k % 2, :, 3 * DH1:5 * DH1], kx[:, k % 2, :, 0:2 * DH1], ACT.Copy)
                    nc.scalar.activation(kx[:, k % 2, :, 5 * DH1:], kx[:, k % 2, :, 0:DH1], ACT.Copy).then_inc(s["kx_ready"], 1)
                skewed(act, B, [(0, decays), (1, lambda i, k, h: operand(0, i, k)), (-1, weighted), (-5, act_xnT(act, o)),
                                (1, lambda i, k, h: operand(1, i, k)), (2, repeats)], unroll=4, slots=4)

            @block.tensor
            def _(pe):
                mm = nc.tensor.matmul
                h4 = lambda x: x.rearrange("p (t k) -> p t k", t=4)

                def exponents(i, k, h):
                    for r in range(2):
                        wait(pe, s["D_ready"], 2 * i + r - 1)
                        c0 = (i % 4) * NH1 + r
                        grp = i // 4
                        mm(h4(pd[r][:]), identb, cb[:, CB_TRI:CB_TRI + P].unsqueeze(1).broadcast_to([P, 4, P]), start=True, stop=True)
                        mm(h4(pd[r][:]), aT3[:, bass.ds(grp, 1), :].rearrange("p g s -> p (g s)"),
                           cb[0:96, bass.ds(CB_SEL + c0, 4, 2)].unsqueeze(2).broadcast_to([96, 4, P]), start=False, stop=True, skip_group_check=True)
                        for t in range(4):
                            last = mm(pd[r][:, t * P:(t + 1) * P], cb[0:96, bass.ds(CB_SEL + c0 + 2 * t, 1)].broadcast_to([96, P]),
                                      nT3[:, bass.ds(grp, 1), :].rearrange("p g s -> p (g s)"), start=False, stop=True, skip_group_check=True)
                        last.then_inc(s["d_done"], 1)

                def turn(n, i, k):
                    pe.wait_ge(s["qx_ready" if n == 0 else "kx_ready"], i + 1)
                    wait(pe, s["qk_ready"], 2 * i + n)
                    x = (qx, kx)[n]
                    for hd in range(NH1):
                        last = nc.tensor.transpose(pqk[0:QR, hd * P:(hd + 1) * P], x[:, k % 2, hd, :], identb)
                    last.then_inc(s["qk_t"], 1)

                def scores(i, k, h):
                    pe.wait_ge(s["qk_ready"], 2 * i + 2)
                    for r in range(2):
                        wait(pe, s["C_ready"], 2 * i + r - 1)
                        for t in range(4):
                            last = mm(pq[r][:, t * P:(t + 1) * P], kT[:, k, 2 * t + r, :], qT[:, k, 2 * t + r, :], start=True, stop=True)
                        last.then_inc(s["s_done"], 1)

                def weigh(i, k, h):
                    pe.wait_ge(s["C_ready"], 2 * i + 2)
                    pe.wait_ge(s["vx_ready"], i + 1)
                    wait(pe, s["ao_ready"], i)
                    for r in range(2):
                        for t in range(4):
                            last = mm(po[32 * t:32 * t + 32, r * P:(r + 1) * P], vx[:, k % 2, 2 * t + r, :], C[:, k % 2, r, t * P:(t + 1) * P],
                                      start=True, stop=True)
                    last.then_inc(s["h_done"], 1)

                def turn_out(i, k, h):
                    pe.wait_ge(s["ao_ready"], i + 1)
                    wait(pe, s["h_read"], i)
                    for r in range(2):
                        last = nc.tensor.transpose(pv[:, r * P:(r + 1) * P], ao[:, k % 2, r * P:(r + 1) * P], ident)
                    last.then_inc(s["out_t"], 1)
                skewed(pe, B, [(0, exponents), (-2, turn_out), (0, scores), (-6, pe_score(pe, o, 1)),
                               (1, lambda i, k, h: turn(0, i, k)), (-1, weigh), (1, lambda i, k, h: turn(1, i, k)),
                               (-5, pe_xnT(pe, o))], unroll=4, slots=4)
    stB.close()

    route(1)
    experts(1, [(w11, 1), (w12, FC)], w13, ACT.Gelu, 1)

    with ExitStack() as st:
        PARTS = 4
        per = B // PARTS
        yg = wts[:, 0:B * TOPK * P].rearrange("p (b n d) -> p b n d", b=B, n=TOPK)
        tmp = sb(st, "tmp_e", [P, 2, P])
        xo = wts[:, B * TOPK * P:B * TOPK * P + B * P].rearrange("p (b d) -> p b d", b=B)
        s_x, s_st = sem(st, "x_added_e"), sem(st, "step_e")
        s_g = [sem(st, f"part_in{c}") for c in range(PARTS)]
        s_o = sem(st, "out_stored")
        with nc.Block() as block:
            @block.sync
            def _(sp):
                for c in range(PARTS):
                    for b in range(c * per, (c + 1) * per, per // 2):
                        at = (NT + b * TOPK) * P
                        sp.dma_start(yg[:, b:b + per // 2].rearrange("p b n d -> p (b n) d"),
                                     y_d[1][at:at + per // 2 * TOPK * P, :].rearrange("(m p) d -> p m d", p=P)).then_inc(s_g[c], 16)
                for c in range(PARTS):
                    sp.wait_ge(s_x, (c + 1) * per)
                    sp.dma_start(out_d[c * per:(c + 1) * per].rearrange("b s d -> s b d"), xo[:, c * per:(c + 1) * per, :]).then_inc(s_o, 16)
                sp.wait_ge(s_o, 16 * PARTS)

            @block.vector
            def _(v):
                for c in range(PARTS):
                    v.wait_ge(s_g[c], 32)

                    def first(i, k, h):
                        i = i + c * per
                        wait(v, s_x, i - 1)
                        xv = xs[:, bass.ds(i, 1), :].rearrange("p a d -> p (a d)")
                        v.scalar_tensor_tensor(tmp[:, k, :], yg[:, bass.ds(i, 1), 0, :].rearrange("p a d -> p (a d)"),
                                               wt[:, bass.ds(i, 1), 0], xv, ALU.mult, ALU.add).then_inc(s_st, 1)

                    def second(i, k, h):
                        i = i + c * per
                        v.wait_ge(s_st, i + 1)
                        v.scalar_tensor_tensor(xo[:, bass.ds(i, 1), :].rearrange("p a d -> p (a d)"),
                                               yg[:, bass.ds(i, 1), 1, :].rearrange("p a d -> p (a d)"),
                                               wt[:, bass.ds(i, 1), 1], tmp[:, k, :], ALU.mult, ALU.add).then_inc(s_x, 1)
                    skewed(v, per, [(1, first), (0, second)])
    return keep


INS = ['x', 'ctx_1024', 'mask_Bx1xSxS2_ik1', 'g_xattn', 'g_ffn', 'L0_ffn_Wg', 'L0_ffn_W1', 'L0_ffn_b1', 'L0_ffn_W2', 'L0_ffn_b2',
       'L1_xattn_igate_w', 'L1_xattn_igate_b', 'L1_xattn_fgate_w', 'L1_xattn_fgate_b', 'L1_xattn_ln_scale',
       'L1_ffn_expert_tokens', 'L1_ffn_W1', 'L1_ffn_b1', 'L1_ffn_W2', 'L1_ffn_b2', 'L1_ffn_W3', 'L1_ffn_b3']


def kernel(**inputs):
    import numpy as np
    import concourse.bacc as bacc
    from concourse.bass_utils import run_bass_kernel_spmd

    nc = bacc.Bacc("TRN2", target_bir_lowering=False, num_devices=1)
    arrays, args = {}, []
    cf, cb = constants()
    for name, a in [("const_f32", cf), ("const_small", cb)] + [(n, np.ascontiguousarray(inputs[n])) for n in INS]:
        arrays[f"in_{name}"] = a
        args.append(nc.dram_tensor(f"in_{name}", a.shape, mybir.dt.from_np(a.dtype), kind="ExternalInput").ap())
    args.append(nc.dram_tensor("out_0", (B, P, P), F32, kind="ExternalOutput").ap())
    build(nc, *args)
    r = run_bass_kernel_spmd(nc, [arrays], core_ids=[0])
    return r.results[0]["out_0"]
```
